# Optimizing a Trainium2 kernel written in Bass

```python
import numpy as np
import jax
import jax.numpy as jnp

def _softmax(x, axis=-1):
    return jax.nn.softmax(x, axis=axis)

def _gelu(x):
    return jax.nn.gelu(x, approximate=True)

def _silu(x):
    return jax.nn.silu(x)

def _sigmoid(x):
    return jax.nn.sigmoid(x)

def _layernorm(x, axis=-1, eps=1e-05):
    m = jnp.mean(x, axis=axis, keepdims=True)
    v = jnp.var(x, axis=axis, keepdims=True)
    return (x - m) / jnp.sqrt(v + eps)

def _scatter_add(tgt, idx, src, axis=0):
    return tgt.at[idx].add(src)

def _segment_sum(src, seg, n):
    return jax.ops.segment_sum(src, seg, n)
kernel_name = 'mk_seq_preln_d2_jaxref_r4_8cdb87'

def setup_inputs(seed: int=0):
    np.random.seed(seed)
    _w = jnp.asarray

    def _L0_attn_setup():
        import jax, jax.numpy as jnp
        import numpy as np
        B, L, D = (4, 1024, 512)
        EPS = 1e-05
        W_SCALE = 0.02

        def _hgrn_forward(x, Wi, Wf, Wg, g_norm_weight, Wo):
            i = jnp.einsum('bld,ed->ble', x, Wi)
            f = jnp.einsum('bld,ed->ble', x, Wf)
            gate = jax.nn.sigmoid(f)
            i_in = jax.nn.silu(i) * (1.0 - gate)

            def combine(c1, c2):
                a1, b1 = c1
                a2, b2 = c2
                return (a1 * a2, a2 * b1 + b2)
            _, o = jax.lax.associative_scan(combine, (gate, i_in), axis=1)
            g = jnp.einsum('bld,ed->ble', x, Wg)
            rms = jax.lax.rsqrt(jnp.mean(jnp.square(g), axis=-1, keepdims=True) + EPS)
            out = g * rms * g_norm_weight * (o * jax.nn.sigmoid(o))
            return jnp.einsum('ble,de->bld', out, Wo)
        key = jax.random.key(seed)
        kx, ki, kf, kg, ko = jax.random.split(key, 5)
        return {'hidden_states': jax.random.normal(kx, (B, L, D), dtype=jnp.float32), 'Wi': jax.random.normal(ki, (D, D), dtype=jnp.float32) * W_SCALE, 'Wf': jax.random.normal(kf, (D, D), dtype=jnp.float32) * W_SCALE, 'Wg': jax.random.normal(kg, (D, D), dtype=jnp.float32) * W_SCALE, 'g_norm_weight': jnp.ones((D,), dtype=jnp.float32), 'Wo': jax.random.normal(ko, (D, D), dtype=jnp.float32) * W_SCALE}
    _L0_attn_in = _L0_attn_setup()

    def _L0_ffn_setup():
        import jax, jax.numpy as jnp
        import numpy as np
        DIM_IN = 512
        DIM_HIDDEN = 2048
        key = jax.random.key(seed)
        k_x, k_g, k_u, k_d = jax.random.split(key, 4)
        s_in = 1.0 / np.sqrt(DIM_IN)
        s_hid = 1.0 / np.sqrt(DIM_HIDDEN)
        x = jax.random.normal(k_x, (4, 512, DIM_IN), dtype=jnp.float32)
        w_gate = jax.random.uniform(k_g, (DIM_HIDDEN, DIM_IN), jnp.float32, -s_in, s_in)
        w_up = jax.random.uniform(k_u, (DIM_HIDDEN, DIM_IN), jnp.float32, -s_in, s_in)
        w_down = jax.random.uniform(k_d, (DIM_IN, DIM_HIDDEN), jnp.float32, -s_hid, s_hid)
        return {'x': x, 'w_gate': w_gate, 'w_up': w_up, 'w_down': w_down}
    _L0_ffn_in = _L0_ffn_setup()

    def _L1_attn_setup():
        import jax, jax.numpy as jnp
        import numpy as np
        HIDDEN = 512
        N_HEADS = 16
        N_KV_HEADS = 4
        HEAD_DIM = 128
        THETA = 10000.0
        MASK_NEG = -2.3819763e+38

        def apply_rotary_emb(x, theta=THETA):
            B, S, H, D = x.shape
            half = D // 2
            freqs = 1.0 / theta ** (jnp.arange(0, D, 2, dtype=jnp.float32) / D)
            ang = jnp.arange(S, dtype=jnp.float32)[:, None] * freqs[None, :]
            cos = jnp.cos(ang)[None, :, None, :]
            sin = jnp.sin(ang)[None, :, None, :]
            xf = x.astype(jnp.float32)
            x1, x2 = (xf[..., :half], xf[..., half:])
            real = x1 * cos - x2 * sin
            imag = x1 * sin + x2 * cos
            return jnp.concatenate([real, imag], axis=-1).astype(x.dtype)
        key = jax.random.key(seed)
        k1, k2, k3 = jax.random.split(key, 3)
        B, S = (2, 512)
        lim_qkv = 1.0 / np.sqrt(HIDDEN)
        lim_o = 1.0 / np.sqrt(N_HEADS * HEAD_DIM)
        x = jax.random.normal(k1, (B, S, HIDDEN), dtype=jnp.float32)
        Wqkv = jax.random.uniform(k2, (HIDDEN, (N_HEADS + 2 * N_KV_HEADS) * HEAD_DIM), minval=-lim_qkv, maxval=lim_qkv, dtype=jnp.float32)
        Wo = jax.random.uniform(k3, (N_HEADS * HEAD_DIM, HIDDEN), minval=-lim_o, maxval=lim_o, dtype=jnp.float32)
        return {'x': x, 'Wqkv': Wqkv, 'Wo': Wo}
    _L1_attn_in = _L1_attn_setup()

    def _L1_ffn_setup():
        import jax, jax.numpy as jnp
        import numpy as np
        K = 2
        SCALING = 16.0 / 16.0
        key = jax.random.key(seed)
        ks = jax.random.split(key, 7)
        B, T, D, O, E, R = (2, 1024, 512, 512, 8, 16)
        return {'x': jax.random.normal(ks[0], (B, T, D), dtype=jnp.float32), 'W': jax.random.normal(ks[1], (O, D), dtype=jnp.float32) * (1.0 / np.sqrt(D)), 'b': jax.random.normal(ks[2], (O,), dtype=jnp.float32) * 0.02, 'lora_A': jax.random.normal(ks[3], (E, R, D), dtype=jnp.float32) * (1.0 / np.sqrt(D)), 'lora_B': jax.random.normal(ks[4], (E, O, R), dtype=jnp.float32) * 0.02, 'gate_w': jax.random.normal(ks[5], (E, D), dtype=jnp.float32) * 0.02, 'gate_b': jax.random.normal(ks[6], (E,), dtype=jnp.float32) * 0.02}
    _L1_ffn_in = _L1_ffn_setup()
    _d = {'L0_attn_hidden_states': _L0_attn_in['hidden_states'], 'L0_attn_Wi': _L0_attn_in['Wi'], 'L0_attn_Wf': _L0_attn_in['Wf'], 'L0_attn_Wg': _L0_attn_in['Wg'], 'L0_attn_g_norm_weight': _L0_attn_in['g_norm_weight'], 'L0_attn_Wo': _L0_attn_in['Wo'], 'L0_ffn_w_gate': _L0_ffn_in['w_gate'], 'L0_ffn_w_up': _L0_ffn_in['w_up'], 'L0_ffn_w_down': _L0_ffn_in['w_down'], 'L1_attn_Wqkv': _L1_attn_in['Wqkv'], 'L1_attn_Wo': _L1_attn_in['Wo'], 'L1_ffn_W': _L1_ffn_in['W'], 'L1_ffn_b': _L1_ffn_in['b'], 'L1_ffn_lora_A': _L1_ffn_in['lora_A'], 'L1_ffn_lora_B': _L1_ffn_in['lora_B'], 'L1_ffn_gate_w': _L1_ffn_in['gate_w'], 'L1_ffn_gate_b': _L1_ffn_in['gate_b']}
    _x0 = _d['L0_attn_hidden_states']
    _d['L0_attn_hidden_states'] = jax.random.normal(jax.random.fold_in(jax.random.key(seed), 1), (4, 512, 512), dtype=_x0.dtype)
    del _x0
    return _d

def reference(L0_attn_hidden_states, L0_attn_Wi, L0_attn_Wf, L0_attn_Wg, L0_attn_g_norm_weight, L0_attn_Wo, L0_ffn_w_gate, L0_ffn_w_up, L0_ffn_w_down, L1_attn_Wqkv, L1_attn_Wo, L1_ffn_W, L1_ffn_b, L1_ffn_lora_A, L1_ffn_lora_B, L1_ffn_gate_w, L1_ffn_gate_b):

    def _L0_attn_ref(hidden_states, Wi, Wf, Wg, g_norm_weight, Wo):
        import jax, jax.numpy as jnp
        import numpy as np
        B, L, D = (4, 1024, 512)
        EPS = 1e-05
        W_SCALE = 0.02

        def _hgrn_forward(x, Wi, Wf, Wg, g_norm_weight, Wo):
            i = jnp.einsum('bld,ed->ble', x, Wi)
            f = jnp.einsum('bld,ed->ble', x, Wf)
            gate = jax.nn.sigmoid(f)
            i_in = jax.nn.silu(i) * (1.0 - gate)

            def combine(c1, c2):
                a1, b1 = c1
                a2, b2 = c2
                return (a1 * a2, a2 * b1 + b2)
            _, o = jax.lax.associative_scan(combine, (gate, i_in), axis=1)
            g = jnp.einsum('bld,ed->ble', x, Wg)
            rms = jax.lax.rsqrt(jnp.mean(jnp.square(g), axis=-1, keepdims=True) + EPS)
            out = g * rms * g_norm_weight * (o * jax.nn.sigmoid(o))
            return jnp.einsum('ble,de->bld', out, Wo)
        return _hgrn_forward(hidden_states, Wi, Wf, Wg, g_norm_weight, Wo)

    def _L0_ffn_ref(x, w_gate, w_up, w_down):
        import jax, jax.numpy as jnp
        import numpy as np
        DIM_IN = 512
        DIM_HIDDEN = 2048
        gate = jnp.einsum('bsd,hd->bsh', x, w_gate)
        up = jnp.einsum('bsd,hd->bsh', x, w_up)
        gated = jax.nn.silu(gate) * up
        return jnp.einsum('bsh,dh->bsd', gated, w_down)

    def _L1_attn_ref(x, Wqkv, Wo):
        import jax, jax.numpy as jnp
        import numpy as np
        HIDDEN = 512
        N_HEADS = 16
        N_KV_HEADS = 4
        HEAD_DIM = 128
        THETA = 10000.0
        MASK_NEG = -2.3819763e+38

        def apply_rotary_emb(x, theta=THETA):
            B, S, H, D = x.shape
            half = D // 2
            freqs = 1.0 / theta ** (jnp.arange(0, D, 2, dtype=jnp.float32) / D)
            ang = jnp.arange(S, dtype=jnp.float32)[:, None] * freqs[None, :]
            cos = jnp.cos(ang)[None, :, None, :]
            sin = jnp.sin(ang)[None, :, None, :]
            xf = x.astype(jnp.float32)
            x1, x2 = (xf[..., :half], xf[..., half:])
            real = x1 * cos - x2 * sin
            imag = x1 * sin + x2 * cos
            return jnp.concatenate([real, imag], axis=-1).astype(x.dtype)
        B, S, _ = x.shape
        q_size = N_HEADS * HEAD_DIM
        kv_size = N_KV_HEADS * HEAD_DIM
        g = N_HEADS // N_KV_HEADS
        xqkv = x @ Wqkv
        xq = xqkv[..., :q_size].reshape(B, S, N_HEADS, HEAD_DIM)
        xk = xqkv[..., q_size:q_size + kv_size].reshape(B, S, N_KV_HEADS, HEAD_DIM)
        xv = xqkv[..., q_size + kv_size:].reshape(B, S, N_KV_HEADS, HEAD_DIM)
        xq = apply_rotary_emb(xq)
        xk = apply_rotary_emb(xk)
        xk = jnp.repeat(xk, g, axis=2)
        xv = jnp.repeat(xv, g, axis=2)
        scale = HEAD_DIM ** (-0.5)
        scores = jnp.einsum('bqhd,bkhd->bhqk', xq, xk) * scale
        causal_add = jnp.triu(jnp.full((S, S), MASK_NEG, dtype=jnp.float32), k=1)
        scores = scores + causal_add[None, None]
        probs = jax.nn.softmax(scores, axis=-1)
        attn = jnp.einsum('bhqk,bkhd->bqhd', probs, xv).reshape(B, S, q_size)
        return attn @ Wo

    def _L1_ffn_ref(x, W, b, lora_A, lora_B, gate_w, gate_b):
        import jax, jax.numpy as jnp
        import numpy as np
        K = 2
        SCALING = 16.0 / 16.0
        orig_shape = x.shape
        D = orig_shape[-1]
        O = W.shape[0]
        x_flat = x.reshape(-1, D)
        base = x_flat @ W.T + b
        logits = x_flat @ gate_w.T + gate_b
        topk_logits, topk_idx = jax.lax.top_k(logits, K)
        gates = jax.nn.softmax(topk_logits, axis=-1)
        xA = jnp.einsum('nd,erd->ner', x_flat, lora_A)
        delta_all = jnp.einsum('ner,eor->neo', xA, lora_B)
        delta_topk = jnp.take_along_axis(delta_all, topk_idx[:, :, None], axis=1)
        lora_update = jnp.sum(delta_topk * gates[:, :, None], axis=1)
        out = base + SCALING * lora_update
        return out.reshape(*orig_shape[:-1], O)
    x = L0_attn_hidden_states
    x = x + _L0_attn_ref(_layernorm(x, axis=-1), L0_attn_Wi, L0_attn_Wf, L0_attn_Wg, L0_attn_g_norm_weight, L0_attn_Wo)
    x = x + _L0_ffn_ref(_layernorm(x, axis=-1), L0_ffn_w_gate, L0_ffn_w_up, L0_ffn_w_down)
    x = x + _L1_attn_ref(_layernorm(x, axis=-1), L1_attn_Wqkv, L1_attn_Wo)
    x = x + _L1_ffn_ref(_layernorm(x, axis=-1), L1_ffn_W, L1_ffn_b, L1_ffn_lora_A, L1_ffn_lora_B, L1_ffn_gate_w, L1_ffn_gate_b)
    return x

_drawn_inputs = setup_inputs


def setup_inputs(seed=0):
    import zlib

    import numpy as np

    out = dict(_drawn_inputs(seed))
    spreads = {'L0_attn_g_norm_weight': (1.0, 0.6)}
    factors = {'L0_attn_Wf': 3.379, 'L1_ffn_b': 4.284, 'L1_ffn_gate_b': 22.78}
    for name, (base, spread) in spreads.items():
        noise = np.random.default_rng([zlib.crc32(name.encode()), seed]).standard_normal(out[name].shape)
        drawn = base * np.exp(spread * noise) if base else spread * noise
        out[name] = jnp.asarray(drawn.astype(out[name].dtype))
    for name, factor in factors.items():
        out[name] = (out[name] * factor).astype(out[name].dtype)
    return out
```

```python
import numpy as np
import concourse.bass as bass
from concourse import mybir
from contextlib import ExitStack

B, L, D = 4, 512, 512
P = 128
NT, NC = L // P, D // P
HID = 2048
NQ = HID // D
NH, NKV, HD = 16, 4, 128
GH = NH // NKV
E, R = 8, 16
EPS = 1e-5
MASK_NEG = -2.3819763e38
THETA = 10000.0

S_Y = 2.0 ** 8
S_W = 2.0 ** 8
S_U = 2.0 ** 8
S_G = 2.0 ** 6
S_Q = 2.0 ** 6
S_P = 2.0 ** 8
S_A = 2.0 ** 6
S_X = 2.0 ** 8
PROJ = 1.0 / (S_Y * S_W)

CH_BIG, CH_ATT = 1536, 1280
U_HGRN = 4 * NC * D
U_FFN = 3 * NC * D
U_ATT = NC * D + NC * 2 * HD + GH * D
HGRN_CHUNKS = -(-U_HGRN // CH_BIG)
SLOT1 = HGRN_CHUNKS * CH_BIG
W_COLS = SLOT1 + U_FFN
N_CHUNKS = HGRN_CHUNKS + 4 * (NQ + NKV + 1)
FIRST_ATT_CHUNK = HGRN_CHUNKS + 4 * NQ
W_I, W_F, W_G, W_O = 0, NC * D, 2 * NC * D, 3 * NC * D
W_GATE, W_UP, W_DOWN = 0, NC * D, 2 * NC * D
W_Q, W_KV, W_AO = 0, NC * D, NC * D + NC * 2 * HD
W_BASE, W_LA, W_LB, W_RT = 0, NC * D, NC * D + NC * P, NC * D + NC * P + D

ALU = mybir.AluOpType
ACT = mybir.ActivationFunctionType
AX = mybir.AxisListType
f32, f16, bf16 = mybir.dt.float32, mybir.dt.float16, mybir.dt.bfloat16


def slot(unit):
    return (unit % 2) * SLOT1


def cols(t, start, n):
    return t[:, start:start + n] if isinstance(start, int) else t[:, bass.ds(start, n)]


def need(eng, sem, count):
    if not (isinstance(count, int) and count <= 0):
        eng.wait_ge(sem, count)


def build(nc, x_in, w_in, gnw_in, bias_in, gate_b_in, rope_in, tri_in, ident_in, mask_in, out):
    ctx = ExitStack()
    with ctx:
        def sb(name, n, dt=f32, parts=P):
            return ctx.enter_context(nc.sbuf_tensor(name, [parts, n], dt))

        def sem(name):
            return ctx.enter_context(nc.semaphore(name))

        x = sb("x", B * NT * D)
        yT_h, yT_l = sb("yT_h", B * NC * L, f16), sb("yT_l", B * NC * L, f16)
        w_h, w_l = sb("w_h", W_COLS, f16), sb("w_l", W_COLS, f16)
        stage = sb("stage", 2 * CH_BIG)
        y_h, y_l = sb("y_h", NT * D, f16), sb("y_l", NT * D, f16)
        y_full = sb("y_full", 2 * D)
        stats, moments = sb("stats", NT * 6), sb("moments", NT * 2)
        var, rstd, shift = sb("var", NT), sb("rstd", NT), sb("shift", NT)
        minus_half = sb("minus_half", NT)
        ones, pause = sb("ones", 1), sb("pause", 2)
        gnw, gnw_s = sb("gnw", NC), sb("gnw_s", NC)
        gate_b = sb("gate_b", E)
        ident, causal = sb("ident", P, f16), sb("causal", P, bf16)
        rope_c, rope_s = sb("rope_c", L), sb("rope_s", L)

        stage_ctx = ExitStack()

        def tmp(name, n, dt=f32):
            return stage_ctx.enter_context(nc.sbuf_tensor(name, [P, n], dt))

        with stage_ctx:
            sig_i, sig_nf = tmp("sig_i", 2 * L), tmp("sig_nf", 2 * L)
            fgate = tmp("fgate", NC * L)
            inject, state = tmp("inject", 2 * L), tmp("state", 2 * L)
            sig_o, u = tmp("sig_o", 2 * L), tmp("u", 2 * L)
            g_sq = tmp("g_sq", NC * L)
            u_h, u_l = tmp("u_h", NC * L, f16), tmp("u_l", NC * L, f16)
            ms, rms = tmp("ms", NT), tmp("rms", NT)
        stage_ctx = ExitStack()
        with stage_ctx:
            silu_g, gated = tmp("silu_g", 2 * L), tmp("gated", NC * L)
            gated_h, gated_l = tmp("gated_h", NC * L, f16), tmp("gated_l", NC * L, f16)
        stage_ctx = ExitStack()
        with stage_ctx:
            r_cos, r_sin = tmp("r_cos", 2 * L), tmp("r_sin", 2 * L)
            k_h, k_l = tmp("k_h", L, f16), tmp("k_l", L, f16)
            v_h, v_l = tmp("v_h", L, f16), tmp("v_l", L, f16)
            q_h, q_l = tmp("q_h", GH * L, f16), tmp("q_l", GH * L, f16)
            NP = NT * (NT + 1) // 2 * P
            p_e = tmp("p_e", 2 * NP)
            p_h, p_l = tmp("p_h", 2 * NP, f16), tmp("p_l", 2 * NP, f16)
            pT = tmp("pT", 2 * NP, f16)
            ao_h, ao_l = tmp("ao_h", GH * L, f16), tmp("ao_l", GH * L, f16)
            smax, sneg, ssum, sinv = tmp("smax", 8), tmp("sneg", 8), tmp("ssum", 8), tmp("sinv", 8)
        stage_ctx = ExitStack()
        with stage_ctx:
            logit, top, lshift, lexp = tmp("logit", NT * E), tmp("top", NT), tmp("lshift", NT * E), tmp("lexp", NT * E)
            above, equal, rank = tmp("above", NT * E * E), tmp("equal", NT * E * E), tmp("rank", NT * E)
            picked, psum_, gates = tmp("picked", NT * E), tmp("picked_sum", NT), tmp("gates", NT * E)
            g_h, g_l = tmp("g_h", NT * E * R, f16), tmp("g_l", NT * E * R, f16)
            gT, xa = tmp("gT", L), tmp("xa", L)
            xa_h, xa_l = tmp("xa_h", L, f16), tmp("xa_l", L, f16)
            tri = tmp("tri", E * E)
            bias = tmp("bias", D)

        bank = [ctx.enter_context(nc.psum_tensor(f"bank{i}", [P, L], f32)) for i in range(8)]
        bank16 = [bk[:, :].bitcast(f16) for bk in bank]

        const_in = sem("const_in")
        late_in = sem("late_in")
        x_loaded = [sem(f"x_loaded{b}") for b in range(B)]
        w_first = [sem(f"w_first{k}") for k in range(HGRN_CHUNKS)]
        w_loaded, w_hi, w_lo = sem("w_loaded"), sem("w_hi"), sem("w_lo")
        memset_done, gnw_ready = sem("memset_done"), sem("gnw_ready")
        ln_stat, ln_var, ln_rstd, ln_shift = sem("ln_stat"), sem("ln_var"), sem("ln_rstd"), sem("ln_shift")
        ln_hi, ln_full, ln_lo = sem("ln_hi"), sem("ln_full"), sem("ln_lo")
        ln_T, ln_outh, ln_outl = sem("ln_T"), sem("ln_outh"), sem("ln_outl")
        out_ready, x_new = sem("out_ready"), sem("x_new")
        i_ready, f_ready, g_ready = sem("i_ready"), sem("f_ready"), sem("g_ready")
        sig_if, fgate_done, inj_mix, injected = sem("sig_if"), sem("fgate_done"), sem("inj_mix"), sem("injected")
        scanned, sigo_done, silu_o, u_done = sem("scanned"), sem("sigo_done"), sem("silu_o"), sem("u_done")
        u_hi, u_lo, gsq_done, gsum = sem("u_hi"), sem("u_lo"), sem("gsq_done"), sem("gsum")
        ms_ready, ms_out, rms_done = sem("ms_ready"), sem("ms_out"), sem("rms_done")
        gate_ready, up_ready, silu_done = sem("gate_ready"), sem("up_ready"), sem("silu_done")
        gated_done, gated_hi, gated_lo = sem("gated_done"), sem("gated_hi"), sem("gated_lo")
        rp_ready, rp_read, rp_sum, rp_hi, rp_lo = (sem(n) for n in ("rp_ready", "rp_read", "rp_sum", "rp_hi", "rp_lo"))
        v_ready, v_hi, v_lo = sem("v_ready"), sem("v_hi"), sem("v_lo")
        s_ready, s_max, s_neg, s_exp, s_scaled, s_inv = (sem(n) for n in ("s_ready", "s_max", "s_neg", "s_exp", "s_scaled", "s_inv"))
        p_hi, p_lo, pT_ready, pT_vec, pT_act = (sem(n) for n in ("p_hi", "p_lo", "pT_ready", "pT_vec", "pT_act"))
        pv_ready, ao_hi, ao_lo = sem("pv_ready"), sem("ao_hi"), sem("ao_lo")
        lg_ready, xa_ready, gT_ready = sem("lg_ready"), sem("xa_ready"), sem("gT_ready")
        gate_step, lexp_done, gT_out, xa_done, xa_hi, xa_lo = (sem(n) for n in ("gate_step", "lexp_done", "gT_out", "xa_done", "xa_hi", "xa_lo"))
        gate_rcp, gate_val = sem("gate_rcp"), sem("gate_val")
        biased, stored = sem("biased"), sem("stored")

        block = ctx.enter_context(nc.Block())

        X_FFN, X_ATT, X_MIX = 4 * B, 4 * B + 4 * NQ * B, 4 * B + 4 * NQ * B + 4 * NKV * B
        N_FFN, N_ATT, N_MIX = B, 2 * B, 3 * B
        HGRN_BANKS, FFN_BANKS, ATT_BANKS, MIX_BANKS = (0, 1, 2, 3), (4, 5, 0, 1), (1, 5, 1, 5), (0, 1, 5, 3)
        Q_OFF = [sum(range(t + 1)) * P for t in range(NT)]
        S_TILES = ((2, ((3, 0),)), (3, ((2, 0), (0, 3 * P))), (4, ((1, 0),)))
        PT_TILES = ((6, (0,)), (7, (1,)), (6, (2, 3)))
        PT_OFF, at = {}, 0
        for _, kbs in PT_TILES:
            for kb in kbs:
                PT_OFF[kb] = at
                at += 2 * (NT - kb) * P

        @block.sync
        def _(eng):
            def first_chunk(k):
                n = min(CH_BIG, U_HGRN - k * CH_BIG)
                if k >= 2:
                    eng.wait_ge(w_lo, k - 1)
                eng.dma_start(stage[:, (k % 2) * CH_BIG:(k % 2) * CH_BIG + n], w_in[k, :, 0:n]).then_inc(w_first[k], 16)

            def load_x(b):
                eng.dma_start(x[:, b * NT * D:(b + 1) * NT * D].rearrange("p (t d) -> p t d", t=NT),
                              x_in[b].rearrange("(t p) d -> p t d", p=P)).then_inc(x_loaded[b], 16)

            load_x(0)
            eng.dma_start(ident[:, :], ident_in).then_inc(const_in, 16)
            eng.dma_start(gnw[:, :], gnw_in).then_inc(const_in, 16)
            first_chunk(0)
            first_chunk(1)
            for b in range(1, B):
                load_x(b)
            eng.dma_start(rope_c[:, :], rope_in[0]).then_inc(const_in, 16)
            eng.dma_start(rope_s[:, :], rope_in[1]).then_inc(const_in, 16)
            eng.dma_start(causal[:, :], mask_in).then_inc(const_in, 16)
            eng.dma_start(gate_b[:, :], gate_b_in).then_inc(const_in, 16)
            for k in range(2, HGRN_CHUNKS):
                first_chunk(k)

            def later_chunk(k, n):
                eng.wait_ge(w_lo, k)
                eng.dma_start(cols(stage, (k % 2) * CH_BIG, n), w_in[k, :, 0:n] if isinstance(k, int)
                              else w_in[bass.ds(k, 1), :, 0:n].rearrange("a p n -> (a p) n")).then_inc(w_loaded, 16)
            later_chunk(HGRN_CHUNKS, CH_BIG)
            with eng.Fori(HGRN_CHUNKS + 1, FIRST_ATT_CHUNK) as k:
                later_chunk(k, CH_BIG)
            with eng.Fori(FIRST_ATT_CHUNK, N_CHUNKS) as k:
                later_chunk(k, CH_ATT)
            eng.wait_ge(x_new, X_MIX)
            eng.dma_start(tri[:, :], tri_in).then_inc(late_in, 16)
            eng.dma_start(bias[:, :], bias_in).then_inc(late_in, 16)
            with eng.Fori(0, B) as b:
                eng.wait_ge(x_new, X_MIX + NT * b + NT)
                eng.dma_start(out[bass.ds(b, 1)].rearrange("a (t p) d -> p (a t) d", p=P),
                              cols(x, b * NT * D, NT * D).rearrange("p (t d) -> p t d", t=NT)).then_inc(stored, 16)
            eng.wait_ge(stored, 16 * B)

        @block.tensor
        def _(pe):
            def mm3(dst, ah, al, bh, bl, first, last):
                nc.tensor.matmul(dst, ah, bh, start=first, stop=False)
                nc.tensor.matmul(dst, ah, bl, start=False, stop=False)
                return nc.tensor.matmul(dst, al, bh, start=False, stop=last)

            def project(bk, w_off, stride, b):
                for k in range(NC):
                    wo, yo = w_off + k * stride, b * (NC * L) + k * L
                    i = mm3(bank[bk][:, :], cols(w_h, wo, P), cols(w_l, wo, P), cols(yT_h, yo, L), cols(yT_l, yo, L),
                            k == 0, k == NC - 1)
                return i

            def back(bk, t, ah, al, w_off, chunks, first, last):
                for c in chunks:
                    i = mm3(bank[bk][:, :], ah[:, c * L + t * P:c * L + (t + 1) * P], al[:, c * L + t * P:c * L + (t + 1) * P],
                            cols(w_h, w_off + c * D, D), cols(w_l, w_off + c * D, D),
                            first and c == chunks[0], last and c == chunks[-1])
                return i

            def transpose_ln(n):
                for r in range(2):
                    need(pe, ln_hi, NT * n + 2 * r + 2)
                    need(pe, ln_lo, NT * n + 2 * r + 2)
                    for bk, src, emptied in ((6, y_h, ln_outh), (7, y_l, ln_outl)):
                        need(pe, emptied, 2 * n + r)
                        for t in range(2):
                            for c in range(NC):
                                i = nc.tensor.transpose(bank16[bk][:, (2 * c + t) * P:(2 * c + t + 1) * P],
                                                        src[:, (2 * r + t) * D + c * P:(2 * r + t) * D + (c + 1) * P], ident[:, :])
                        i.then_inc(ln_T, 1)

            def yT_there(n):
                need(pe, ln_outh, 2 * n + 2)
                need(pe, ln_outl, 2 * n + 2)

            def hgrn_step(b, ln):
                J = NC * b
                yT_there(b)
                for c in range(NC):
                    need(pe, x_new, NT * (b - 1) + 3 + c if c < 2 else 0)
                    need(pe, injected, J + c - 1)
                    if isinstance(b, int) and b == 0:
                        need(pe, w_lo, -(-(W_I + NC * D) // CH_BIG))
                    project(2 + c % 2, W_I + c * P, D, b).then_inc(i_ready, 1)
                    need(pe, fgate_done, J + c - 1)
                    if isinstance(b, int) and b == 0:
                        need(pe, w_lo, -(-(W_F + NC * D) // CH_BIG))
                    project(c % 2, W_F + c * P, D, b).then_inc(f_ready, 1)
                    need(pe, u_done, J + c - 1)
                    if c == 0:
                        need(pe, ms_out, b)
                    if isinstance(b, int) and b == 0:
                        need(pe, w_lo, -(-(W_G + NC * D) // CH_BIG))
                    project(4 + c % 2, W_G + c * P, D, b).then_inc(g_ready, 1)
                need(pe, w_lo, HGRN_CHUNKS)
                pe.wait_ge(u_lo, J + 3)
                for t in range(NT):
                    if t == 0:
                        pe.wait_ge(fgate_done, J + 4)
                    if t == 2:
                        pe.wait_ge(injected, J + 4)
                    back(HGRN_BANKS[t], t, u_h, u_l, W_O, (0, 1, 2), True, False)
                pe.wait_ge(gsum, 3 * b + 3)
                pe.wait_ge(u_done, J + 3)
                for t in range(NT):
                    i = nc.tensor.matmul(bank[4][:, t:t + 1], g_sq[:, t * P:(t + 1) * P], ones[:, :], start=True, stop=True)
                i.then_inc(ms_ready, 1)
                if ln is not None:
                    transpose_ln(ln)
                pe.wait_ge(u_lo, J + 4)
                for t in range(NT):
                    back(HGRN_BANKS[t], t, u_h, u_l, W_O, (3,), False, True).then_inc(out_ready, 1)

            def ffn_step(it, ln):
                b, J = it % B, NC * it
                W = slot(it // B + 1)
                if isinstance(it, int) and it == 0:
                    pe.wait_ge(x_new, X_FFN)
                yT_there(N_FFN + b)
                pe.wait_ge(w_lo, HGRN_CHUNKS + 4 * (it // B) + 4)
                for j in range(NC):
                    if j < 2:
                        need(pe, x_new, X_FFN + NT * (it - 1) + 3 + j)
                    else:
                        need(pe, silu_done, J + j - 1)
                    project(j % 2, W + W_GATE + j * P, D, b).then_inc(gate_ready, 1)
                    need(pe, gated_done, J + j - 1)
                    project(2 + j % 2, W + W_UP + j * P, D, b).then_inc(up_ready, 1)
                pe.wait_ge(gated_lo, J + 3)
                for t in range(NT):
                    if t == 2:
                        pe.wait_ge(silu_done, J + 4)
                    back(FFN_BANKS[t], t, gated_h, gated_l, W + W_DOWN, (0, 1, 2), True, False)
                if ln is not None:
                    transpose_ln(ln)
                pe.wait_ge(gated_lo, J + 4)
                for t in range(NT):
                    back(FFN_BANKS[t], t, gated_h, gated_l, W + W_DOWN, (3,), False, True).then_inc(out_ready, 1)

            def rope_tile(it, r, bk, w_off, stride):
                need(pe, rp_read, 5 * it + (0, 0, 1, 3, 4)[r])
                project(bk, w_off, stride, it % B).then_inc(rp_ready, 1)

            def scores(it, h):
                G = GH * it + h
                pe.wait_ge(rp_lo, 5 * it + h + 2)
                for i, (bk, parts) in enumerate(S_TILES):
                    need(pe, s_exp, 4 * G - (3, 1, 0)[i])
                    for qb, at in parts:
                        n = (qb + 1) * P
                        qs = slice(h * L + qb * P, h * L + (qb + 1) * P)
                        mm3(bank[bk][:, at:at + n], q_h[:, qs], q_l[:, qs], k_h[:, 0:n], k_l[:, 0:n], True, False)
                        i_ = nc.tensor.matmul(bank[bk][:, at + qb * P:at + n], ident[:, :], causal[:, :], start=False, stop=True)
                    i_.then_inc(s_ready, 1)

            def transpose_p(G, h):
                pe.wait_ge(p_lo, 4 * G + 4)
                pb = (h % 2) * NP
                for i, (bk, kbs) in enumerate(PT_TILES):
                    need(pe, pT_act if bk == 7 else pT_vec, G if bk == 7 else 2 * G + (i > 0))
                    base = PT_OFF[kbs[0]]
                    for kb in kbs:
                        for part, src in enumerate((p_h, p_l)):
                            for qb in range(kb, NT):
                                dst = PT_OFF[kb] - base + (part * (NT - kb) + qb - kb) * P
                                s = pb + Q_OFF[qb] + kb * P
                                t = nc.tensor.transpose(bank16[bk][:, dst:dst + P], src[:, s:s + P], ident[:, :])
                    t.then_inc(pT_ready, 1)

            def weigh_v(G):
                pe.wait_ge(pT_vec, 2 * G + 2)
                pe.wait_ge(pT_act, G + 1)
                need(pe, ao_lo, G)
                for kb in range(NT):
                    n = (NT - kb) * P
                    o = PT_OFF[kb]
                    i = mm3(bank[5][:, kb * P:L], v_h[:, kb * P:(kb + 1) * P], v_l[:, kb * P:(kb + 1) * P],
                            pT[:, o:o + n], pT[:, o + n:o + 2 * n], kb == 0, kb == NT - 1)
                i.then_inc(pv_ready, 1)

            def att_back(it):
                pe.wait_ge(ao_lo, GH * (it + 1))
                W = slot(it // B + NQ + 1) + W_AO
                for t in range(NT):
                    if t >= 2:
                        pe.wait_ge(x_new, X_ATT + NT * it + t - 1)
                    back(ATT_BANKS[t], t, ao_h, ao_l, W, (0, 1, 2, 3), True, True).then_inc(out_ready, 1)

            def att_step(it, ln):
                b, first = it % B, isinstance(it, int) and it == 0
                W = slot(it // B + NQ + 1)
                G = GH * it
                if first:
                    pe.wait_ge(x_new, X_ATT)
                yT_there(N_ATT + b)
                pe.wait_ge(w_lo, HGRN_CHUNKS + 4 * NQ + 4 * (it // B) + 4)
                rope_tile(it, 0, 0, W + W_KV, 2 * HD)
                if not first:
                    weigh_v(G - 2)
                    need(pe, x_new, X_ATT + NT * (it - 2) + 3)
                rope_tile(it, 1, 1, W + W_Q, D)
                if not first:
                    transpose_p(G - 1, 3)
                rope_tile(it, 2, 0, W + W_Q + HD, D)
                if ln is not None:
                    need(pe, pT_vec, 2 * G)
                    need(pe, pT_act, G)
                    transpose_ln(ln)
                if not first:
                    weigh_v(G - 1)
                pe.wait_ge(rp_read, 5 * it + 2)
                for t in range(NT):
                    for k in range(NC):
                        yo, wo = b * (NC * L) + k * L + t * P, W + W_KV + k * 2 * HD + HD
                        i = mm3(bank[1][:, t * P:(t + 1) * P], cols(yT_h, yo, P), cols(yT_l, yo, P),
                                cols(w_h, wo, HD), cols(w_l, wo, HD), k == 0, k == NC - 1)
                i.then_inc(v_ready, 1)
                scores(it, 0)
                rope_tile(it, 3, 0, W + W_Q + 2 * HD, D)
                pe.wait_ge(v_lo, it + 1)
                if not first:
                    att_back(it - 1)
                scores(it, 1)
                transpose_p(G, 0)
                rope_tile(it, 4, 0, W + W_Q + 3 * HD, D)
                if not first:
                    pe.wait_ge(x_new, X_ATT + NT * it)
                weigh_v(G)
                scores(it, 2)
                transpose_p(G + 1, 1)
                scores(it, 3)
                weigh_v(G + 1)
                transpose_p(G + 2, 2)

            def att_end(ln):
                G = GH * NKV * B
                weigh_v(G - 2)
                transpose_p(G - 1, 3)
                pe.wait_ge(pT_vec, 2 * G)
                pe.wait_ge(pT_act, G)
                transpose_ln(ln)
                weigh_v(G - 1)
                pe.wait_ge(x_new, X_MIX - 2 * NT + NT)
                att_back(NKV * B - 1)

            def mix_step(b, ln):
                W = slot(NQ + NKV + 1)
                if isinstance(b, int) and b == 0:
                    pe.wait_ge(w_lo, N_CHUNKS)
                    pe.wait_ge(x_new, X_MIX)
                yT_there(N_MIX + b)
                need(pe, gate_step, 12 * b)
                for t in range(NT):
                    for k in range(NC):
                        yo, wo = b * (NC * L) + k * L + t * P, W + W_RT + k * E
                        i = mm3(bank[2][:, t * E:(t + 1) * E], cols(yT_h, yo, P), cols(yT_l, yo, P),
                                w_h[:, wo:wo + E], w_l[:, wo:wo + E], k == 0, k == NC - 1)
                i.then_inc(lg_ready, 1)
                need(pe, xa_done, b)
                project(4, W + W_LA, E * R, b).then_inc(xa_ready, 1)
                if ln is not None:
                    transpose_ln(ln)
                for t in range(NT):
                    need(pe, x_new, X_MIX + NT * (b - 1) + t + 1)
                    for k in range(NC):
                        yo, wo = b * (NC * L) + k * L + t * P, W + W_BASE + k * D
                        mm3(bank[MIX_BANKS[t]][:, :], cols(yT_h, yo, P), cols(yT_l, yo, P),
                            w_h[:, wo:wo + D], w_l[:, wo:wo + D], k == 0, False)
                pe.wait_ge(gate_step, 12 * b + 12)
                need(pe, gT_out, b)
                for t in range(NT):
                    nc.tensor.matmul(bank[6][:, t * P:(t + 1) * P], g_h[:, t * P:(t + 1) * P], ident[:, :], start=True, stop=False)
                    i = nc.tensor.matmul(bank[6][:, t * P:(t + 1) * P], g_l[:, t * P:(t + 1) * P], ident[:, :], start=False, stop=True)
                i.then_inc(gT_ready, 1)
                pe.wait_ge(xa_lo, b + 1)
                for t in range(NT):
                    ts = slice(t * P, (t + 1) * P)
                    mm3(bank[MIX_BANKS[t]][:, :], xa_h[:, ts], xa_l[:, ts],
                        w_h[:, W + W_LB:W + W_LB + D], w_l[:, W + W_LB:W + W_LB + D], False, True).then_inc(out_ready, 1)

            pe.wait_ge(const_in, 16 * 6)
            pe.wait_ge(memset_done, 2)
            transpose_ln(0)
            with pe.Fori(1, B) as n:
                transpose_ln(n)
            hgrn_step(0, None)
            with pe.Fori(1, B) as b:
                hgrn_step(b, N_FFN - 1 + b)
            ffn_step(0, N_FFN + B - 1)
            with pe.Fori(1, NQ * B - 3) as it:
                ffn_step(it, None)
            with pe.Fori(NQ * B - 3, NQ * B) as it:
                ffn_step(it, it - (NQ * B - 3) + N_ATT)
            att_step(0, N_ATT + B - 1)
            with pe.Fori(1, NKV * B - 2) as it:
                att_step(it, None)
            with pe.Fori(NKV * B - 2, NKV * B) as it:
                att_step(it, it - (NKV * B - 2) + N_MIX)
            att_end(N_MIX + 2)
            mix_step(0, N_MIX + 3)
            with pe.Fori(1, B) as b:
                mix_step(b, None)

        @block.scalar
        def _(act):
            def split_hi(k, dst, n):
                if isinstance(k, int) and k < HGRN_CHUNKS:
                    act.wait_ge(w_first[k], 16)
                else:
                    act.wait_ge(w_loaded, 16 * (k - HGRN_CHUNKS + 1))
                nc.scalar.activation(cols(w_h, dst, n), cols(stage, (k % 2) * CH_BIG, n), ACT.Copy, scale=S_W).then_inc(w_hi, 1)

            def ln_hi_part(n, b):
                act.wait_ge(ln_shift, n + 1)
                for t in range(NT):
                    nc.scalar.activation(y_h[:, t * D:(t + 1) * D], cols(x, (b * NT + t) * D, D), ACT.Identity,
                                         scale=rstd[:, t:t + 1], bias=shift[:, t:t + 1]).then_inc(ln_hi, 1)

            def ln_out(n, b):
                for r in range(2):
                    act.wait_ge(ln_T, 4 * n + 2 * r + 2)
                    nc.scalar.activation(cols(yT_l, b * (NC * L), NC * L).rearrange("p (c n) -> p c n", c=NC)[:, :, 2 * r * P:2 * (r + 1) * P],
                                         bank16[7].rearrange("p (c n) -> p c n", c=NC), ACT.Copy).then_inc(ln_outl, 1)

            def hgrn_step(b, ln):
                J = NC * b

                def gates(c):
                    s = slice((c % 2) * L, (c % 2 + 1) * L)
                    act.wait_ge(i_ready, J + c + 1)
                    nc.scalar.activation(sig_i[:, s], bank[2 + c % 2][:, :], ACT.Sigmoid, scale=PROJ)
                    act.wait_ge(f_ready, J + c + 1)
                    nc.scalar.activation(sig_nf[:, s], bank[c % 2][:, :], ACT.Sigmoid, scale=-PROJ).then_inc(sig_if, 1)
                    nc.scalar.activation(fgate[:, c * L:(c + 1) * L], bank[c % 2][:, :], ACT.Sigmoid, scale=PROJ).then_inc(fgate_done, 1)

                def sig_state(c):
                    s = slice((c % 2) * L, (c % 2 + 1) * L)
                    act.wait_ge(scanned, J + c + 1)
                    nc.scalar.activation(sig_o[:, s], state[:, s], ACT.Sigmoid).then_inc(sigo_done, 1)

                def square_g(c):
                    act.wait_ge(g_ready, J + c + 1)
                    nc.scalar.activation(g_sq[:, c * L:(c + 1) * L], bank[4 + c % 2][:, :], ACT.Square, scale=PROJ).then_inc(gsq_done, 1)

                def hi_u(c):
                    s = slice((c % 2) * L, (c % 2 + 1) * L)
                    act.wait_ge(u_done, J + c + 1)
                    nc.scalar.activation(u_h[:, c * L:(c + 1) * L], u[:, s], ACT.Copy).then_inc(u_hi, 1)

                for c in range(NC):
                    gates(c)
                    if c == 0:
                        split_hi(b + HGRN_CHUNKS, SLOT1 + b * CH_BIG, CH_BIG)
                    if c:
                        sig_state(c - 1)
                    square_g(c)
                    if c:
                        hi_u(c - 1)
                sig_state(3)
                hi_u(3)
                if ln is not None:
                    ln_out(ln, b - 1)
                ln_hi_part(N_FFN + b, b)

            def ffn_step(it, ln, norm):
                b, J = it % B, NC * it

                def silu(j):
                    act.wait_ge(gate_ready, J + j + 1)
                    nc.scalar.activation(silu_g[:, (j % 2) * L:(j % 2 + 1) * L], bank[j % 2][:, :], ACT.Silu, scale=PROJ).then_inc(silu_done, 1)

                def hi(j):
                    act.wait_ge(gated_done, J + j + 1)
                    nc.scalar.activation(gated_h[:, j * L:(j + 1) * L], gated[:, j * L:(j + 1) * L], ACT.Copy).then_inc(gated_hi, 1)

                silu(0)
                n = CH_ATT if norm else CH_BIG
                split_hi(it + HGRN_CHUNKS + 4, slot(it // B) + b * n, n)
                for j in range(1, NC):
                    silu(j)
                    hi(j - 1)
                hi(3)
                if ln is not None:
                    ln_out(ln, (b + 3) % B)
                if norm:
                    ln_hi_part(it - (NQ - 1) * B + N_ATT, b)

            def rope_hi(it, r):
                act.wait_ge(rp_sum, 5 * it + r + 1)
                dst = k_h[:, :] if r == 0 else q_h[:, (r - 1) * L:r * L]
                nc.scalar.activation(dst, r_cos[:, (r % 2) * L:(r % 2 + 1) * L], ACT.Copy).then_inc(rp_hi, 1)

            def exps(G, h):
                act.wait_ge(s_neg, G + 1)
                e = (h % 2) * NP
                o = (h % 2) * NT
                for bk, parts in S_TILES:
                    for qb, at in parts:
                        n = (qb + 1) * P
                        nc.scalar.activation(p_e[:, e + Q_OFF[qb]:e + Q_OFF[qb] + n], bank[bk][:, at:at + n], ACT.Exp,
                                             scale=SCORE, bias=sneg[:, o + qb:o + qb + 1],
                                             accum_out=ssum[:, o + qb:o + qb + 1]).then_inc(s_exp, 1)

            def probs_hi(G, h):
                act.wait_ge(s_inv, G + 1)
                e = (h % 2) * NP
                for qb in range(NT):
                    s = slice(e + Q_OFF[qb], e + Q_OFF[qb] + (qb + 1) * P)
                    nc.scalar.activation(p_h[:, s], p_e[:, s], ACT.Copy, scale=sinv[:, (h % 2) * NT + qb:(h % 2) * NT + qb + 1]).then_inc(p_hi, 1)

            def pT_copy(G):
                act.wait_ge(pT_ready, 3 * G + 2)
                o, n = PT_OFF[1], 2 * (NT - 1) * P
                nc.scalar.activation(pT[:, o:o + n], bank16[7][:, 0:n], ACT.Copy).then_inc(pT_act, 1)

            def ao_part(G, h):
                act.wait_ge(pv_ready, G + 1)
                nc.scalar.activation(ao_h[:, h * L:(h + 1) * L], bank[5][:, :], ACT.Copy, scale=S_A / (S_P * S_Q)).then_inc(ao_hi, 1)

            def att_step(it, ln, norm):
                first, b, G = isinstance(it, int) and it == 0, it % B, GH * it
                rope_hi(it, 0)
                split_hi(it + FIRST_ATT_CHUNK + 4, slot(it // B) + b * CH_ATT, CH_ATT)
                if not first:
                    ao_part(G - 2, 2)
                    probs_hi(G - 1, 3)
                rope_hi(it, 1)
                if not first:
                    pT_copy(G - 1)
                rope_hi(it, 2)
                if ln is not None:
                    ln_out(ln, (b + 3) % B if norm is None else (b + 2) % B)
                if not first:
                    ao_part(G - 1, 3)
                act.wait_ge(v_ready, it + 1)
                nc.scalar.activation(v_h[:, :], bank[1][:, :], ACT.Copy, scale=S_Q * PROJ).then_inc(v_hi, 1)
                exps(G, 0)
                rope_hi(it, 3)
                probs_hi(G, 0)
                exps(G + 1, 1)
                if norm is not None:
                    ln_hi_part(norm, (b + 3) % B)
                pT_copy(G)
                rope_hi(it, 4)
                ao_part(G, 0)
                probs_hi(G + 1, 1)
                exps(G + 2, 2)
                pT_copy(G + 1)
                probs_hi(G + 2, 2)
                exps(G + 3, 3)
                ao_part(G + 1, 1)
                pT_copy(G + 2)

            def att_end(ln, norm):
                G = GH * NKV * B
                ao_part(G - 2, 2)
                probs_hi(G - 1, 3)
                pT_copy(G - 1)
                ln_out(ln, 2)
                ao_part(G - 1, 3)
                ln_hi_part(norm, 3)

            def mix_step(b, ln):
                if ln is not None:
                    ln_out(ln, 3)
                act.wait_ge(gate_step, 12 * b + 3)
                nc.scalar.activation(lexp[:, :], lshift[:, :], ACT.Exp).then_inc(lexp_done, 1)
                act.wait_ge(gT_ready, b + 1)
                nc.scalar.activation(gT[:, :], bank[6][:, :], ACT.Copy).then_inc(gT_out, 1)
                act.wait_ge(xa_done, b + 1)
                nc.scalar.activation(xa_h[:, :], xa[:, :], ACT.Copy).then_inc(xa_hi, 1)

            def ln_whole(n):
                ln_hi_part(n, n)
                ln_out(n, n)

            ln_whole(0)
            split_hi(0, 0, CH_BIG)
            split_hi(1, CH_BIG, CH_BIG)
            ln_whole(1)
            split_hi(2, 2 * CH_BIG, CH_BIG)
            ln_whole(2)
            split_hi(3, 3 * CH_BIG, CH_BIG)
            ln_whole(3)
            for k in range(4, HGRN_CHUNKS):
                split_hi(k, k * CH_BIG, min(CH_BIG, U_HGRN - k * CH_BIG))
            hgrn_step(0, None)
            with act.Fori(1, B) as b:
                hgrn_step(b, N_FFN - 1 + b)
            ffn_step(0, N_FFN + B - 1, False)
            with act.Fori(1, (NQ - 1) * B) as it:
                ffn_step(it, None, False)
            ffn_step((NQ - 1) * B, None, True)
            with act.Fori(NQ * B - 3, NQ * B) as it:
                ffn_step(it, it - (NQ * B - 3) + N_ATT, True)
            att_step(0, N_ATT + B - 1, None)
            with act.Fori(1, NKV * B - 3) as it:
                att_step(it, None, None)
            att_step(NKV * B - 3, None, N_MIX)
            with act.Fori(NKV * B - 2, NKV * B) as it:
                att_step(it, it - (NKV * B - 2) + N_MIX, it - (NKV * B - 2) + N_MIX + 1)
            att_end(N_MIX + 2, N_MIX + 3)
            mix_step(0, N_MIX + 3)
            with act.Fori(1, B) as b:
                mix_step(b, None)

        @block.vector
        def _(dve):
            def split_lo(k, dst, n):
                dve.wait_ge(w_hi, k + 1)
                nc.vector.scalar_tensor_tensor(out=cols(w_l, dst, n), in0=cols(stage, (k % 2) * CH_BIG, n), scalar=S_W,
                                               in1=cols(w_h, dst, n), op0=ALU.mult, op1=ALU.subtract).then_inc(w_lo, 1)

            def wait_alone(sem, count, column):
                dve.wait_ge(sem, count)
                nc.vector.memset(pause[:, column:column + 1], 0.0)

            def ln_stat_block(n, b, t):
                nc.vector.bn_stats(stats[:, 6 * t:6 * t + 6], cols(x, (b * NT + t) * D, D)).then_inc(ln_stat, 1)

            def ln_moments(n):
                wait_alone(ln_stat, 8 * n + NT, 1)
                for t in range(NT):
                    nc.vector.bn_aggr(moments[:, 2 * t:2 * t + 2], stats[:, 6 * t:6 * t + 6]).then_inc(ln_stat, 1)
                dve.wait_ge(ln_stat, 8 * n + 2 * NT)
                nc.vector.tensor_scalar(var[:, :], moments[:, :].rearrange("p (t s) -> p t s", s=2)[:, :, 1], EPS, S_Y ** -2,
                                        ALU.add, ALU.mult).then_inc(ln_var, 1)

            def ln_lo_part(n, b):
                dve.wait_ge(ln_rstd, n + 1)
                nc.vector.scalar_tensor_tensor(out=shift[:, :], in0=moments[:, :].rearrange("p (t s) -> p t s", s=2)[:, :, 0],
                                               scalar=-1.0, in1=rstd[:, :], op0=ALU.mult, op1=ALU.mult).then_inc(ln_shift, 1)

                def full(t):
                    nc.vector.tensor_scalar(y_full[:, (t % 2) * D:(t % 2 + 1) * D], cols(x, (b * NT + t) * D, D),
                                            moments[:, 2 * t:2 * t + 1], rstd[:, t:t + 1], ALU.subtract, ALU.mult).then_inc(ln_full, 1)

                def lo(t):
                    dve.wait_ge(ln_full, NT * n + t + 1)
                    dve.wait_ge(ln_hi, NT * n + t + 1)
                    nc.vector.tensor_tensor(y_l[:, t * D:(t + 1) * D], y_full[:, (t % 2) * D:(t % 2 + 1) * D],
                                            y_h[:, t * D:(t + 1) * D], ALU.subtract).then_inc(ln_lo, 1)

                full(0)
                full(1)
                for t in range(NT):
                    lo(t)
                    if t + 2 < NT:
                        dve.wait_ge(ln_lo, NT * n + t + 1)
                        full(t + 2)

            def ln_out(n, b):
                for r in range(2):
                    dve.wait_ge(ln_T, 4 * n + 2 * r + 1)
                    nc.vector.tensor_copy(cols(yT_h, b * (NC * L), NC * L).rearrange("p (c n) -> p c n", c=NC)[:, :, 2 * r * P:2 * (r + 1) * P],
                                          bank16[6].rearrange("p (c n) -> p c n", c=NC)).then_inc(ln_outh, 1)

            def update_x(X, b, banks, scale, n=None):
                for t in range(NT):
                    dve.wait_ge(out_ready, X + t + 1)
                    if n is not None and t:
                        dve.wait_ge(x_new, X + t)
                    xb = cols(x, (b * NT + t) * D, D)
                    nc.vector.scalar_tensor_tensor(out=xb, in0=bank[banks[t]][:, :], scalar=scale(t), in1=xb,
                                                   op0=ALU.mult, op1=ALU.add).then_inc(x_new, 1)
                    if n is not None and t:
                        ln_stat_block(n, b, t - 1)
                if n is not None:
                    wait_alone(x_new, X + NT, 0)
                    ln_stat_block(n, b, NT - 1)
                    ln_moments(n)

            def hgrn_step(b, ln):
                J = NC * b

                def scan(c):
                    s = slice((c % 2) * L, (c % 2 + 1) * L)
                    dve.wait_ge(inj_mix, J + c + 1)
                    nc.vector.scalar_tensor_tensor(out=inject[:, s], in0=bank[2 + c % 2][:, :], scalar=PROJ, in1=sig_i[:, s],
                                                   op0=ALU.mult, op1=ALU.mult).then_inc(injected, 1)
                    dve.wait_ge(injected, J + c + 1)
                    dve.wait_ge(fgate_done, J + c + 1)
                    nc.vector.tensor_tensor_scan(state[:, s], fgate[:, c * L:(c + 1) * L], inject[:, s], 0.0,
                                                 ALU.mult, ALU.add).then_inc(scanned, 1)

                def make_u(c):
                    s = slice((c % 2) * L, (c % 2 + 1) * L)
                    dve.wait_ge(sigo_done, J + c + 1)
                    nc.vector.tensor_tensor(sig_o[:, s], sig_o[:, s], state[:, s], ALU.mult).then_inc(silu_o, 1)
                    dve.wait_ge(silu_o, J + c + 1)
                    dve.wait_ge(gsq_done, J + c + 1)
                    nc.vector.scalar_tensor_tensor(out=u[:, s], in0=bank[4 + c % 2][:, :], scalar=gnw_s[:, c:c + 1], in1=sig_o[:, s],
                                                   op0=ALU.mult, op1=ALU.mult).then_inc(u_done, 1)

                def lo_u(c):
                    s = slice((c % 2) * L, (c % 2 + 1) * L)
                    dve.wait_ge(u_hi, J + c + 1)
                    nc.vector.tensor_tensor(u_l[:, c * L:(c + 1) * L], u[:, s], u_h[:, c * L:(c + 1) * L], ALU.subtract).then_inc(u_lo, 1)

                for c in range(NC):
                    scan(c)
                    if c == 0:
                        split_lo(b + HGRN_CHUNKS, SLOT1 + b * CH_BIG, CH_BIG)
                    if c > 1:
                        lo_u(c - 2)
                    if c:
                        make_u(c - 1)
                lo_u(2)
                make_u(3)
                lo_u(3)
                dve.wait_ge(ms_ready, b + 1)
                back_scale = (S_U * S_W) ** 2
                nc.vector.tensor_scalar(ms[:, :], bank[4][:, 0:NT], back_scale / D, EPS * back_scale, ALU.mult, ALU.add).then_inc(ms_out, 1)
                if ln is not None:
                    ln_out(ln, b - 1)
                dve.wait_ge(rms_done, b + 1)
                update_x(NT * b, b, HGRN_BANKS, lambda t: rms[:, t:t + 1], N_FFN + b)
                ln_lo_part(N_FFN + b, b)

            def ffn_step(it, ln, norm):
                b, J = it % B, NC * it

                def gate(j):
                    s = slice((j % 2) * L, (j % 2 + 1) * L)
                    dve.wait_ge(silu_done, J + j + 1)
                    dve.wait_ge(up_ready, J + j + 1)
                    nc.vector.scalar_tensor_tensor(out=gated[:, j * L:(j + 1) * L], in0=bank[2 + j % 2][:, :], scalar=PROJ * S_G, in1=silu_g[:, s],
                                                   op0=ALU.mult, op1=ALU.mult).then_inc(gated_done, 1)

                def lo(j):
                    dve.wait_ge(gated_hi, J + j + 1)
                    nc.vector.tensor_tensor(gated_l[:, j * L:(j + 1) * L], gated[:, j * L:(j + 1) * L],
                                            gated_h[:, j * L:(j + 1) * L], ALU.subtract).then_inc(gated_lo, 1)

                gate(0)
                n = CH_ATT if norm else CH_BIG
                split_lo(it + HGRN_CHUNKS + 4, slot(it // B) + b * n, n)
                for j in range(1, NC):
                    gate(j)
                    lo(j - 1)
                lo(3)
                if ln is not None:
                    ln_out(ln, (b + 3) % B)
                n = it - (NQ - 1) * B + N_ATT if norm else None
                update_x(X_FFN + NT * it, b, FFN_BANKS, lambda t: 1.0 / (S_G * S_W), n)
                if norm:
                    ln_lo_part(n, b)

            def rotate(it, r):
                bk = 1 if r == 1 else 0
                s = slice((r % 2) * L, (r % 2 + 1) * L)
                h = HD // 2
                dve.wait_ge(rp_ready, 5 * it + r + 1)
                need(dve, rp_lo, 5 * it + r - (1 if r else 0))
                nc.vector.tensor_tensor(r_cos[:, s], bank[bk][:, :], rope_c[:, :], ALU.mult)
                nc.vector.tensor_tensor(r_sin[0:h, s], bank[bk][h:HD, :], rope_s[0:h, :], ALU.mult)
                nc.vector.tensor_tensor(r_sin[h:HD, s], bank[bk][0:h, :], rope_s[h:HD, :], ALU.mult).then_inc(rp_read, 1)

            def maxima(G, h):
                o = (h % 2) * NT
                for i, (bk, parts) in enumerate(S_TILES):
                    dve.wait_ge(s_ready, 3 * G + i + 1)
                    for qb, at in parts:
                        m = nc.vector.reduce_max(smax[:, o + qb:o + qb + 1], bank[bk][:, at:at + (qb + 1) * P], AX.X)
                m.then_inc(s_max, 1)
                dve.wait_ge(s_max, G + 1)
                nc.vector.tensor_scalar(sneg[:, o:o + NT], smax[:, o:o + NT], -SCORE, None, ALU.mult).then_inc(s_neg, 1)

            def recip(G, h):
                o = (h % 2) * NT
                dve.wait_ge(s_exp, 4 * G + 4)
                nc.vector.tensor_scalar(ssum[:, o:o + NT], ssum[:, o:o + NT], 1.0 / S_P, None, ALU.mult).then_inc(s_scaled, 1)
                dve.wait_ge(s_scaled, G + 1)
                nc.vector.reciprocal(sinv[:, o:o + NT], ssum[:, o:o + NT]).then_inc(s_inv, 1)

            def probs_lo(G, h):
                e = (h % 2) * NP
                dve.wait_ge(s_inv, G + 1)
                for qb in range(NT):
                    s = slice(e + Q_OFF[qb], e + Q_OFF[qb] + (qb + 1) * P)
                    dve.wait_ge(p_hi, 4 * G + qb + 1)
                    nc.vector.scalar_tensor_tensor(out=p_l[:, s], in0=p_e[:, s], scalar=sinv[:, (h % 2) * NT + qb:(h % 2) * NT + qb + 1],
                                                   in1=p_h[:, s], op0=ALU.mult, op1=ALU.subtract).then_inc(p_lo, 1)

            def pT_copy(G):
                for i in (0, 2):
                    o = PT_OFF[PT_TILES[i][1][0]]
                    n = sum(2 * (NT - kb) * P for kb in PT_TILES[i][1])
                    dve.wait_ge(pT_ready, 3 * G + i + 1)
                    nc.vector.tensor_copy(pT[:, o:o + n], bank16[6][:, 0:n]).then_inc(pT_vec, 1)

            def ao_part(G, h):
                s = slice(h * L, (h + 1) * L)
                dve.wait_ge(ao_hi, G + 1)
                nc.vector.scalar_tensor_tensor(out=ao_l[:, s], in0=bank[5][:, :], scalar=S_A / (S_P * S_Q), in1=ao_h[:, s],
                                               op0=ALU.mult, op1=ALU.subtract).then_inc(ao_lo, 1)

            ATT_BACK = 1.0 / (S_A * S_W)

            def att_step(it, ln, norm):
                first, b, G = isinstance(it, int) and it == 0, it % B, GH * it
                rotate(it, 0)
                split_lo(it + FIRST_ATT_CHUNK + 4, slot(it // B) + b * CH_ATT, CH_ATT)
                if not first:
                    recip(G - 1, 3)
                    ao_part(G - 2, 2)
                    probs_lo(G - 1, 3)
                rotate(it, 1)
                if not first:
                    pT_copy(G - 1)
                rotate(it, 2)
                if ln is not None:
                    ln_out(ln, (b + 3) % B if norm is None else (b + 2) % B)
                if not first:
                    ao_part(G - 1, 3)
                dve.wait_ge(v_hi, it + 1)
                nc.vector.scalar_tensor_tensor(out=v_l[:, :], in0=bank[1][:, :], scalar=S_Q * PROJ, in1=v_h[:, :],
                                               op0=ALU.mult, op1=ALU.subtract).then_inc(v_lo, 1)
                maxima(G, 0)
                rotate(it, 3)
                recip(G, 0)
                probs_lo(G, 0)
                if not first:
                    update_x(X_ATT + NT * (it - 1), (b + 3) % B, ATT_BANKS, lambda t: ATT_BACK, norm)
                maxima(G + 1, 1)
                if norm is not None:
                    ln_lo_part(norm, (b + 3) % B)
                pT_copy(G)
                rotate(it, 4)
                recip(G + 1, 1)
                ao_part(G, 0)
                probs_lo(G + 1, 1)
                maxima(G + 2, 2)
                pT_copy(G + 1)
                recip(G + 2, 2)
                maxima(G + 3, 3)
                probs_lo(G + 2, 2)
                ao_part(G + 1, 1)
                pT_copy(G + 2)

            def att_end(ln, norm):
                G = GH * NKV * B
                recip(G - 1, 3)
                ao_part(G - 2, 2)
                probs_lo(G - 1, 3)
                pT_copy(G - 1)
                ln_out(ln, 2)
                ao_part(G - 1, 3)
                update_x(X_MIX - NT, 3, ATT_BANKS, lambda t: ATT_BACK, norm)
                ln_lo_part(norm, 3)

            def mix_step(b, ln):
                if ln is not None:
                    ln_out(ln, 3)
                g0 = 12 * b
                count = [0]

                def step(ins):
                    ins.then_inc(gate_step, 1)
                    count[0] += 1
                    dve.wait_ge(gate_step, g0 + count[0])

                l3 = logit[:, :].rearrange("p (t e) -> p t e", e=E)
                li = l3[:, :, :, None].to_broadcast([P, NT, E, E])
                lj = l3[:, :, None, :].to_broadcast([P, NT, E, E])
                four = lambda a: a[:, :].rearrange("p (t i j) -> p t i j", i=E, j=E)
                three = lambda a: a[:, :].rearrange("p (t e) -> p t e", e=E)
                dve.wait_ge(lg_ready, b + 1)
                step(nc.vector.scalar_tensor_tensor(out=l3, in0=bank[2][:, 0:NT * E].rearrange("p (t e) -> p t e", e=E), scalar=PROJ,
                                                    in1=gate_b[:, None, :].to_broadcast([P, NT, E]), op0=ALU.mult, op1=ALU.add))
                step(nc.vector.reduce_max(top[:, :], l3, AX.X))
                step(nc.vector.tensor_tensor(three(lshift), l3, top[:, :, None].to_broadcast([P, NT, E]), ALU.subtract))
                step(nc.vector.tensor_tensor(four(above), lj, li, ALU.is_gt))
                step(nc.vector.tensor_tensor(four(equal), lj, li, ALU.is_equal))
                step(nc.vector.tensor_tensor(equal[:, :].rearrange("p (t m) -> p t m", t=NT), equal[:, :].rearrange("p (t m) -> p t m", t=NT),
                                             tri[:, None, :].to_broadcast([P, NT, E * E]), ALU.mult))
                step(nc.vector.tensor_tensor(above[:, :], above[:, :], equal[:, :], ALU.add))
                step(nc.vector.reduce_sum(three(rank), four(above), AX.X))
                dve.wait_ge(lexp_done, b + 1)
                step(nc.vector.scalar_tensor_tensor(out=picked[:, :], in0=rank[:, :], scalar=2.0, in1=lexp[:, :], op0=ALU.is_lt, op1=ALU.mult))
                step(nc.vector.reduce_sum(psum_[:, :], three(picked), AX.X))
                nc.vector.reciprocal(top[:, :], psum_[:, :]).then_inc(gate_rcp, 1)
                dve.wait_ge(gate_rcp, b + 1)
                nc.vector.scalar_tensor_tensor(out=three(gates), in0=three(picked), scalar=S_P, in1=top[:, :, None].to_broadcast([P, NT, E]),
                                               op0=ALU.mult, op1=ALU.mult).then_inc(gate_val, 1)
                dve.wait_ge(gate_val, b + 1)
                spread = gates[:, :, None].to_broadcast([P, NT * E, R])
                step(nc.vector.tensor_copy(g_h[:, :].rearrange("p (e r) -> p e r", r=R), spread))
                step(nc.vector.tensor_tensor(g_l[:, :].rearrange("p (e r) -> p e r", r=R), spread,
                                             g_h[:, :].rearrange("p (e r) -> p e r", r=R), ALU.subtract))
                dve.wait_ge(gT_out, b + 1)
                dve.wait_ge(xa_ready, b + 1)
                nc.vector.scalar_tensor_tensor(out=xa[:, :], in0=bank[4][:, :], scalar=PROJ * S_X / S_P, in1=gT[:, :],
                                               op0=ALU.mult, op1=ALU.mult).then_inc(xa_done, 1)
                dve.wait_ge(xa_done, b + 1)
                dve.wait_ge(xa_hi, b + 1)
                nc.vector.tensor_tensor(xa_l[:, :], xa[:, :], xa_h[:, :], ALU.subtract).then_inc(xa_lo, 1)
                for t in range(NT):
                    dve.wait_ge(out_ready, X_MIX + NT * b + t + 1)
                    dve.wait_ge(biased, NT * b + t + 1)
                    xb = cols(x, (b * NT + t) * D, D)
                    nc.vector.scalar_tensor_tensor(out=xb, in0=bank[MIX_BANKS[t]][:, :], scalar=PROJ, in1=xb,
                                                   op0=ALU.mult, op1=ALU.add).then_inc(x_new, 1)

            def ln_whole(n):
                dve.wait_ge(x_loaded[n], 16)
                for t in range(NT):
                    ln_stat_block(n, n, t)
                ln_moments(n)
                ln_lo_part(n, n)
                ln_out(n, n)

            dve.wait_ge(const_in, 16 * 6)
            nc.vector.tensor_scalar(gnw_s[:, :], gnw[:, :], PROJ * S_U, None, ALU.mult).then_inc(gnw_ready, 1)
            dve.wait_ge(gnw_ready, 1)
            ln_whole(0)
            split_lo(0, 0, CH_BIG)
            split_lo(1, CH_BIG, CH_BIG)
            ln_whole(1)
            split_lo(2, 2 * CH_BIG, CH_BIG)
            ln_whole(2)
            split_lo(3, 3 * CH_BIG, CH_BIG)
            ln_whole(3)
            for k in range(4, HGRN_CHUNKS):
                split_lo(k, k * CH_BIG, min(CH_BIG, U_HGRN - k * CH_BIG))
            hgrn_step(0, None)
            with dve.Fori(1, B) as b:
                hgrn_step(b, N_FFN - 1 + b)
            ffn_step(0, N_FFN + B - 1, False)
            with dve.Fori(1, (NQ - 1) * B) as it:
                ffn_step(it, None, False)
            ffn_step((NQ - 1) * B, None, True)
            with dve.Fori(NQ * B - 3, NQ * B) as it:
                ffn_step(it, it - (NQ * B - 3) + N_ATT, True)
            att_step(0, N_ATT + B - 1, None)
            with dve.Fori(1, NKV * B - 3) as it:
                att_step(it, None, None)
            att_step(NKV * B - 3, None, N_MIX)
            with dve.Fori(NKV * B - 2, NKV * B) as it:
                att_step(it, it - (NKV * B - 2) + N_MIX, it - (NKV * B - 2) + N_MIX + 1)
            att_end(N_MIX + 2, N_MIX + 3)
            dve.wait_ge(late_in, 32)
            mix_step(0, N_MIX + 3)
            with dve.Fori(1, B) as b:
                mix_step(b, None)

        @block.gpsimd
        def _(pool):
            def power(n):
                pool.wait_ge(ln_var, n + 1)
                nc.gpsimd.tensor_tensor(rstd[:, :], var[:, :], minus_half[:, :], ALU.pow).then_inc(ln_rstd, 1)

            def hgrn_step(b):
                J = NC * b

                def mix(c):
                    s = slice((c % 2) * L, (c % 2 + 1) * L)
                    pool.wait_ge(sig_if, J + c + 1)
                    nc.gpsimd.tensor_tensor(sig_i[:, s], sig_i[:, s], sig_nf[:, s], ALU.mult).then_inc(inj_mix, 1)

                def add_square(c):
                    pool.wait_ge(gsq_done, J + c + 1)
                    need(pool, gsum, 3 * b + c - 1)
                    nc.gpsimd.tensor_tensor(g_sq[:, 0:L], g_sq[:, 0:L], g_sq[:, c * L:(c + 1) * L], ALU.add).then_inc(gsum, 1)

                mix(0)
                mix(1)
                add_square(1)
                mix(2)
                add_square(2)
                mix(3)
                add_square(3)
                pool.wait_ge(ms_out, b + 1)
                nc.gpsimd.tensor_tensor(rms[:, :], ms[:, :], minus_half[:, :], ALU.pow).then_inc(rms_done, 1)
                power(N_FFN + b)

            def rope_add(it, r):
                s = slice((r % 2) * L, (r % 2 + 1) * L)
                pool.wait_ge(rp_read, 5 * it + r + 1)
                nc.gpsimd.tensor_tensor(r_cos[:, s], r_cos[:, s], r_sin[:, s], ALU.add).then_inc(rp_sum, 1)
                pool.wait_ge(rp_sum, 5 * it + r + 1)
                pool.wait_ge(rp_hi, 5 * it + r + 1)
                hi = k_h[:, :] if r == 0 else q_h[:, (r - 1) * L:r * L]
                lo = k_l[:, :] if r == 0 else q_l[:, (r - 1) * L:r * L]
                nc.gpsimd.tensor_tensor(lo, r_cos[:, s], hi, ALU.subtract).then_inc(rp_lo, 1)

            def att_step(it, norm):
                for r in range(4):
                    rope_add(it, r)
                if norm is not None:
                    power(norm)
                rope_add(it, 4)

            def mix_step(b):
                pool.wait_ge(ln_lo, NT * (N_MIX + b) + NT)
                for t in range(NT):
                    xb = cols(x, (b * NT + t) * D, D)
                    nc.gpsimd.tensor_tensor(xb, xb, bias[:, :], ALU.add).then_inc(biased, 1)

            nc.gpsimd.memset(minus_half[:, :], -0.5).then_inc(memset_done, 1)
            nc.gpsimd.memset(ones[:, :], 1.0).then_inc(memset_done, 1)
            pool.wait_ge(memset_done, 2)
            power(0)
            with pool.Fori(1, B) as n:
                power(n)
            hgrn_step(0)
            with pool.Fori(1, B) as b:
                hgrn_step(b)
            with pool.Fori(N_ATT, N_ATT + B) as n:
                power(n)
            att_step(0, None)
            with pool.Fori(1, NKV * B - 3) as it:
                att_step(it, None)
            with pool.Fori(NKV * B - 3, NKV * B) as it:
                att_step(it, it - (NKV * B - 3) + N_MIX)
            power(N_MIX + 3)
            pool.wait_ge(late_in, 32)
            with pool.Fori(0, B) as b:
                mix_step(b)


SCORE = HD ** -0.5 / (S_Q * S_Q)


def _rows(w_t):
    k, n = w_t.shape
    return w_t.reshape(k // P, P, n).transpose(1, 0, 2).reshape(P, -1)


def _chunks(unit, n, count):
    out = np.zeros((count, P, CH_BIG), np.float32)
    for i in range(count):
        part = unit[:, i * n:(i + 1) * n]
        out[i, :, :part.shape[1]] = part
    return out


def kernel(**inputs):
    import concourse.bacc as bacc
    from concourse.bass_utils import run_bass_kernel_spmd
    a = {k: np.asarray(v) for k, v in inputs.items()}

    packed = [_chunks(np.concatenate([_rows(a[f"L0_attn_{n}"].T) for n in ("Wi", "Wf", "Wg", "Wo")], axis=1), CH_BIG, HGRN_CHUNKS)]
    for q in range(NQ):
        s = slice(q * D, (q + 1) * D)
        unit = np.concatenate([_rows(a["L0_ffn_w_gate"][s].T), _rows(a["L0_ffn_w_up"][s].T), _rows(a["L0_ffn_w_down"][:, s].T)], axis=1)
        packed.append(_chunks(unit, CH_BIG, 4))
    wqkv = a["L1_attn_Wqkv"]
    for g in range(NKV):
        q = wqkv[:, g * GH * HD:(g + 1) * GH * HD]
        k = wqkv[:, (NH + g) * HD:(NH + g + 1) * HD]
        v = wqkv[:, (NH + NKV + g) * HD:(NH + NKV + g + 1) * HD]
        wo = a["L1_attn_Wo"][g * GH * HD:(g + 1) * GH * HD]
        packed.append(_chunks(np.concatenate([_rows(q), _rows(np.concatenate([k, v], axis=1)), _rows(wo)], axis=1), CH_ATT, 4))
    unit = np.concatenate([_rows(a["L1_ffn_W"].T), _rows(a["L1_ffn_lora_A"].reshape(E * R, D).T),
                           _rows(a["L1_ffn_lora_B"].transpose(0, 2, 1).reshape(E * R, D)), _rows(a["L1_ffn_gate_w"].T)], axis=1)
    packed.append(_chunks(unit, CH_ATT, 4))

    freqs = (np.float32(1.0) / np.float32(THETA) ** (np.arange(0, HD, 2, dtype=np.float32) / np.float32(HD))).astype(np.float32)
    ang = (freqs[:, None] * np.arange(L, dtype=np.float32)[None, :]).astype(np.float32)
    scale = np.float32(S_Q * PROJ)
    cos, sin = np.cos(ang).astype(np.float32) * scale, np.sin(ang).astype(np.float32) * scale
    rope = np.stack([np.concatenate([cos, cos]), np.concatenate([-sin, sin])])
    lower = np.tril(np.ones((E, E), np.float32), -1).reshape(1, E * E)
    import ml_dtypes
    mask = np.triu(np.full((P, P), MASK_NEG, np.float32), 1).astype(ml_dtypes.bfloat16)
    arrays = {
        "x_in": np.ascontiguousarray(a["L0_attn_hidden_states"]),
        "w_in": np.concatenate(packed),
        "gnw_in": np.ascontiguousarray(a["L0_attn_g_norm_weight"].reshape(NC, P).T),
        "bias_in": np.ascontiguousarray(np.broadcast_to(a["L1_ffn_b"], (P, D))),
        "gate_b_in": np.ascontiguousarray(np.broadcast_to(a["L1_ffn_gate_b"], (P, E))),
        "rope_in": rope,
        "tri_in": np.ascontiguousarray(np.broadcast_to(lower, (P, E * E))),
        "ident_in": np.eye(P, dtype=np.float16),
        "mask_in": mask,
    }
    nc = bacc.Bacc("TRN2", target_bir_lowering=False, num_devices=1)
    args = [nc.dram_tensor(n, v.shape, mybir.dt.from_np(v.dtype), kind="ExternalInput").ap() for n, v in arrays.items()]
    out = nc.dram_tensor("out", [B, L, D], f32, kind="ExternalOutput").ap()
    build(nc, *args, out)
    r = run_bass_kernel_spmd(nc, [arrays], core_ids=[0])
    return r.results[0]["out"]
```

```python
import numpy as np
import concourse.bass as bass
from concourse import mybir
from contextlib import ExitStack

B, L, D = 4, 512, 512
P = 128
NT, NC = L // P, D // P
HID = 2048
NQ = HID // D
NH, NKV, HD = 16, 4, 128
GH = NH // NKV
E, R = 8, 16
EPS = 1e-5
MASK_NEG = -2.3819763e38
THETA = 10000.0

S_Y = 2.0 ** 8
S_W = 2.0 ** 8
S_U = 2.0 ** 8
S_G = 2.0 ** 6
S_Q = 2.0 ** 6
S_P = 2.0 ** 8
S_A = 2.0 ** 6
S_X = 2.0 ** 8
PROJ = 1.0 / (S_Y * S_W)

CH_BIG, CH_ATT = 1536, 1280
U_HGRN = 4 * NC * D
U_FFN = 3 * NC * D
U_ATT = NC * D + NC * 2 * HD + GH * D
HGRN_CHUNKS = -(-U_HGRN // CH_BIG)
SLOT1 = U_HGRN
W_COLS = SLOT1 + U_FFN
N_CHUNKS = HGRN_CHUNKS + 4 * (NQ + NKV + 1)
FIRST_ATT_CHUNK = HGRN_CHUNKS + 4 * NQ
W_I, W_F, W_G, W_O = 0, NC * D, 2 * NC * D, 3 * NC * D
W_GATE, W_UP, W_DOWN = 0, NC * D, 2 * NC * D
W_Q, W_KV, W_AO = 0, NC * D, NC * D + NC * 2 * HD
W_BASE, W_LA, W_LB, W_RT = 0, NC * D, NC * D + NC * P, NC * D + NC * P + D

ALU = mybir.AluOpType
ACT = mybir.ActivationFunctionType
AX = mybir.AxisListType
f32, f16, bf16 = mybir.dt.float32, mybir.dt.float16, mybir.dt.bfloat16


def slot(unit):
    return (unit % 2) * SLOT1


def cols(t, start, n):
    return t[:, start:start + n] if isinstance(start, int) else t[:, bass.ds(start, n)]


def need(eng, sem, count):
    if not (isinstance(count, int) and count <= 0):
        eng.wait_ge(sem, count)


def ao_at(it, h):
    return h * L if h else (it % 2) * GH * L


def build(nc, x_in, w_in, gnw_in, bias_in, gate_b_in, rope_in, tri_in, ident_in, mask_in, out):
    ctx = ExitStack()
    with ctx:
        def sb(name, n, dt=f32, parts=P):
            return ctx.enter_context(nc.sbuf_tensor(name, [parts, n], dt))

        def sem(name):
            return ctx.enter_context(nc.semaphore(name))

        x = sb("x", B * NT * D)
        yT_h, yT_l = sb("yT_h", B * NC * L, f16), sb("yT_l", B * NC * L, f16)
        w_h, w_l = sb("w_h", W_COLS, f16), sb("w_l", W_COLS, f16)
        stage = sb("stage", 2 * CH_BIG)
        y_h, y_l = sb("y_h", NT * D, f16), sb("y_l", NT * D, f16)
        y_full = sb("y_full", 2 * D)
        stats, moments = sb("stats", NT * 6), sb("moments", NT * 2)
        var, rstd, shift = sb("var", NT), sb("rstd", NT), sb("shift", NT)
        minus_half = sb("minus_half", NT)
        ones, pause = sb("ones", 1), sb("pause", 2)
        gnw, gnw_s = sb("gnw", NC), sb("gnw_s", NC)
        gate_b = sb("gate_b", E)
        ident, causal = sb("ident", P, f16), sb("causal", P, bf16)
        rope_c, rope_s = sb("rope_c", L), sb("rope_s", L)

        stage_ctx = ExitStack()

        def tmp(name, n, dt=f32):
            return stage_ctx.enter_context(nc.sbuf_tensor(name, [P, n], dt))

        with stage_ctx:
            sig_i, sig_nf = tmp("sig_i", 2 * L), tmp("sig_nf", 2 * L)
            fgate = tmp("fgate", NC * L)
            inject, state = tmp("inject", 2 * L), tmp("state", 2 * L)
            sig_o, u = tmp("sig_o", 2 * L), tmp("u", 2 * L)
            g_sq = tmp("g_sq", NC * L)
            u_h, u_l = tmp("u_h", NC * L, f16), tmp("u_l", NC * L, f16)
            ms, rms = tmp("ms", NT), tmp("rms", NT)
        stage_ctx = ExitStack()
        with stage_ctx:
            silu_g, gated = tmp("silu_g", 2 * L), tmp("gated", NC * L)
            gated_h, gated_l = tmp("gated_h", NC * L, f16), tmp("gated_l", NC * L, f16)
        stage_ctx = ExitStack()
        with stage_ctx:
            r_cos, r_sin = tmp("r_cos", 2 * L), tmp("r_sin", 2 * L)
            k_h, k_l = tmp("k_h", L, f16), tmp("k_l", L, f16)
            v_h, v_l = tmp("v_h", 2 * L, f16), tmp("v_l", 2 * L, f16)
            q_h, q_l = tmp("q_h", GH * L, f16), tmp("q_l", GH * L, f16)
            NP = NT * (NT + 1) // 2 * P
            p_e = tmp("p_e", 2 * NP)
            p_h, p_l = tmp("p_h", 2 * NP, f16), tmp("p_l", 2 * NP, f16)
            pT = tmp("pT", 2 * NP, f16)
            ao_h, ao_l = tmp("ao_h", (GH + 1) * L, f16), tmp("ao_l", (GH + 1) * L, f16)
            sneg, ssum, sinv = tmp("sneg", 8), tmp("ssum", 8), tmp("sinv", 8)
        stage_ctx = ExitStack()
        with stage_ctx:
            logit, top, lshift, lexp = tmp("logit", NT * E), tmp("top", NT), tmp("lshift", NT * E), tmp("lexp", NT * E)
            above, equal, rank = tmp("above", NT * E * E), tmp("equal", NT * E * E), tmp("rank", NT * E)
            picked, psum_, gates = tmp("picked", NT * E), tmp("picked_sum", NT), tmp("gates", NT * E)
            g_h, g_l = tmp("g_h", NT * E * R, f16), tmp("g_l", NT * E * R, f16)
            gT, xa = tmp("gT", L), tmp("xa", L)
            xa_h, xa_l = tmp("xa_h", L, f16), tmp("xa_l", L, f16)
            tri = tmp("tri", E * E)
            bias = tmp("bias", D)

        bank = [ctx.enter_context(nc.psum_tensor(f"bank{i}", [P, L], f32)) for i in range(8)]
        bank16 = [bk[:, :].bitcast(f16) for bk in bank]

        const_in, table_in = sem("const_in"), sem("table_in")
        late_in = sem("late_in")
        x_loaded = [sem(f"x_loaded{b}") for b in range(B)]
        w_first = [sem(f"w_first{k}") for k in range(HGRN_CHUNKS)]
        w_loaded, w_hi, w_lo = sem("w_loaded"), sem("w_hi"), sem("w_lo")
        memset_done, gnw_ready = sem("memset_done"), sem("gnw_ready")
        ln_stat, ln_var, ln_rstd, ln_shift = sem("ln_stat"), sem("ln_var"), sem("ln_rstd"), sem("ln_shift")
        ln_hi, ln_full, ln_lo = sem("ln_hi"), sem("ln_full"), sem("ln_lo")
        ln_T, ln_outh, ln_outl = sem("ln_T"), sem("ln_outh"), sem("ln_outl")
        out_ready, x_new = sem("out_ready"), sem("x_new")
        i_ready, f_ready, g_ready = sem("i_ready"), sem("f_ready"), sem("g_ready")
        sig_if, fgate_done, inj_mix, injected = sem("sig_if"), sem("fgate_done"), sem("inj_mix"), sem("injected")
        scanned, sigo_done, silu_o, u_done = sem("scanned"), sem("sigo_done"), sem("silu_o"), sem("u_done")
        u_hi, u_lo, gsq_done, gsum = sem("u_hi"), sem("u_lo"), sem("gsq_done"), sem("gsum")
        ms_ready, ms_out, rms_done = sem("ms_ready"), sem("ms_out"), sem("rms_done")
        gate_ready, up_ready, silu_done = sem("gate_ready"), sem("up_ready"), sem("silu_done")
        gated_done, gated_hi, gated_lo = sem("gated_done"), sem("gated_hi"), sem("gated_lo")
        rp_ready, rp_read, rp_sum, rp_hi, rp_lo = (sem(n) for n in ("rp_ready", "rp_read", "rp_sum", "rp_hi", "rp_lo"))
        v_ready, v_hi, v_lo = sem("v_ready"), sem("v_hi"), sem("v_lo")
        s_ready, s_neg, s_exp, s_scaled, s_inv = (sem(n) for n in ("s_ready", "s_neg", "s_exp", "s_scaled", "s_inv"))
        p_hi, p_lo, pT_ready, pT_vec, pT_act = (sem(n) for n in ("p_hi", "p_lo", "pT_ready", "pT_vec", "pT_act"))
        pv_ready, ao_hi, ao_lo = sem("pv_ready"), sem("ao_hi"), sem("ao_lo")
        lg_ready, xa_ready, gT_ready = sem("lg_ready"), sem("xa_ready"), sem("gT_ready")
        gate_step, lexp_done, gT_out, xa_done, xa_hi, xa_lo = (sem(n) for n in ("gate_step", "lexp_done", "gT_out", "xa_done", "xa_hi", "xa_lo"))
        gate_rcp, gate_val = sem("gate_rcp"), sem("gate_val")
        biased, stored = sem("biased"), sem("stored")

        block = ctx.enter_context(nc.Block())

        X_FFN, X_ATT, X_MIX = 4 * B, 4 * B + 4 * NQ * B, 4 * B + 4 * NQ * B + 4 * NKV * B
        N_FFN, N_ATT, N_MIX = B, 2 * B, 3 * B
        HGRN_BANKS, FFN_BANKS, ATT_BANKS, MIX_BANKS = (0, 1, 2, 3), (4, 5, 0, 1), (1, 0, 1, 1), (0, 1, 5, 3)
        Q_OFF = [sum(range(t + 1)) * P for t in range(NT)]
        S_TILES = ((2, ((3, 0),)), (3, ((2, 0), (0, 3 * P))), (4, ((1, 0),)))
        PT_TILES = ((5, (2, 3)), (7, (1,)), (6, (0,)))
        PT_OFF, at = {}, 0
        for _, kbs in PT_TILES:
            for kb in kbs:
                PT_OFF[kb] = at
                at += 2 * (NT - kb) * P

        @block.sync
        def _(eng):
            def first_chunk(k):
                n = min(CH_BIG, U_HGRN - k * CH_BIG)
                if k >= 2:
                    eng.wait_ge(w_lo, k - 1)
                eng.dma_start(stage[:, (k % 2) * CH_BIG:(k % 2) * CH_BIG + n], w_in[k, :, 0:n]).then_inc(w_first[k], 16)

            def load_x(b):
                eng.dma_start(x[:, b * NT * D:(b + 1) * NT * D].rearrange("p (t d) -> p t d", t=NT),
                              x_in[b].rearrange("(t p) d -> p t d", p=P)).then_inc(x_loaded[b], 16)

            load_x(0)
            eng.dma_start(ident[:, :], ident_in).then_inc(const_in, 16)
            eng.dma_start(gnw[:, :], gnw_in).then_inc(const_in, 16)
            first_chunk(0)
            first_chunk(1)
            for b in range(1, B):
                load_x(b)
            eng.dma_start(rope_c[:, :], rope_in[0]).then_inc(table_in, 16)
            eng.dma_start(rope_s[:, :], rope_in[1]).then_inc(table_in, 16)
            eng.dma_start(causal[:, :], mask_in).then_inc(table_in, 16)
            eng.dma_start(gate_b[:, :], gate_b_in).then_inc(table_in, 16)
            for k in range(2, HGRN_CHUNKS):
                first_chunk(k)

            def later_chunk(k, n):
                eng.wait_ge(w_lo, k)
                eng.dma_start(cols(stage, (k % 2) * CH_BIG, n), w_in[k, :, 0:n] if isinstance(k, int)
                              else w_in[bass.ds(k, 1), :, 0:n].rearrange("a p n -> (a p) n")).then_inc(w_loaded, 16)
            later_chunk(HGRN_CHUNKS, CH_BIG)
            with eng.Fori(HGRN_CHUNKS + 1, FIRST_ATT_CHUNK) as k:
                later_chunk(k, CH_BIG)
            with eng.Fori(FIRST_ATT_CHUNK, N_CHUNKS) as k:
                later_chunk(k, CH_ATT)
            eng.wait_ge(x_new, X_MIX)
            eng.dma_start(tri[:, :], tri_in).then_inc(late_in, 16)
            eng.dma_start(bias[:, :], bias_in).then_inc(late_in, 16)
            with eng.Fori(0, B) as b:
                eng.wait_ge(x_new, X_MIX + NT * b + NT)
                eng.dma_start(out[bass.ds(b, 1)].rearrange("a (t p) d -> p (a t) d", p=P),
                              cols(x, b * NT * D, NT * D).rearrange("p (t d) -> p t d", t=NT)).then_inc(stored, 16)
            eng.wait_ge(stored, 16 * B)

        @block.tensor
        def _(pe):
            def mm3(dst, ah, al, bh, bl, first, last):
                nc.tensor.matmul(dst, ah, bh, start=first, stop=False)
                nc.tensor.matmul(dst, ah, bl, start=False, stop=False)
                return nc.tensor.matmul(dst, al, bh, start=False, stop=last)

            def project(bk, w_off, stride, b):
                for k in range(NC):
                    wo, yo = w_off + k * stride, b * (NC * L) + k * L
                    i = mm3(bank[bk][:, :], cols(w_h, wo, P), cols(w_l, wo, P), cols(yT_h, yo, L), cols(yT_l, yo, L),
                            k == 0, k == NC - 1)
                return i

            def back(bk, t, ah, al, w_off, chunks, first, last, first_at=0):
                for c in chunks:
                    o = (first_at if c == 0 else c * L) + t * P
                    i = mm3(bank[bk][:, :], cols(ah, o, P), cols(al, o, P),
                            cols(w_h, w_off + c * D, D), cols(w_l, w_off + c * D, D),
                            first and c == chunks[0], last and c == chunks[-1])
                return i

            def transpose_ln(n):
                for r in range(2):
                    need(pe, ln_hi, NT * n + 2 * r + 2)
                    need(pe, ln_lo, NT * n + 2 * r + 2)
                    for bk, src, emptied in ((6, y_h, ln_outh), (7, y_l, ln_outl)):
                        need(pe, emptied, 2 * n + r)
                        for t in range(2):
                            for c in range(NC):
                                i = nc.tensor.transpose(bank16[bk][:, (2 * c + t) * P:(2 * c + t + 1) * P],
                                                        src[:, (2 * r + t) * D + c * P:(2 * r + t) * D + (c + 1) * P], ident[:, :])
                        i.then_inc(ln_T, 1)

            def yT_there(n):
                need(pe, ln_outh, 2 * n + 2)
                need(pe, ln_outl, 2 * n + 2)

            def hgrn_step(b, ln):
                J = NC * b
                yT_there(b)
                for c in range(NC):
                    need(pe, x_new, NT * (b - 1) + 3 + c if c < 2 else 0)
                    need(pe, injected, J + c - 1)
                    if isinstance(b, int) and b == 0:
                        need(pe, w_lo, -(-(W_I + NC * D) // CH_BIG))
                    project(2 + c % 2, W_I + c * P, D, b).then_inc(i_ready, 1)
                    need(pe, fgate_done, J + c - 1)
                    if isinstance(b, int) and b == 0:
                        need(pe, w_lo, -(-(W_F + NC * D) // CH_BIG))
                    project(c % 2, W_F + c * P, D, b).then_inc(f_ready, 1)
                    need(pe, u_done, J + c - 1)
                    if c == 0:
                        need(pe, ms_out, b)
                    if isinstance(b, int) and b == 0:
                        need(pe, w_lo, -(-(W_G + NC * D) // CH_BIG))
                    project(4 + c % 2, W_G + c * P, D, b).then_inc(g_ready, 1)
                    if isinstance(b, int) and b == 0 and c + 1 < B:
                        transpose_ln(c + 1)
                need(pe, w_lo, HGRN_CHUNKS)
                pe.wait_ge(u_lo, J + 2)
                for t in range(NT):
                    if t == 0:
                        pe.wait_ge(fgate_done, J + 4)
                    if t == 2:
                        pe.wait_ge(injected, J + 4)
                    back(HGRN_BANKS[t], t, u_h, u_l, W_O, (0, 1), True, False)
                pe.wait_ge(u_lo, J + 3)
                for t in range(NT):
                    back(HGRN_BANKS[t], t, u_h, u_l, W_O, (2,), False, False)
                pe.wait_ge(gsum, 3 * b + 3)
                pe.wait_ge(u_done, J + 3)
                for t in range(NT):
                    i = nc.tensor.matmul(bank[4][:, t:t + 1], g_sq[:, t * P:(t + 1) * P], ones[:, :], start=True, stop=True)
                i.then_inc(ms_ready, 1)
                if ln is not None:
                    transpose_ln(ln)
                pe.wait_ge(u_lo, J + 4)
                for t in range(NT):
                    back(HGRN_BANKS[t], t, u_h, u_l, W_O, (3,), False, True).then_inc(out_ready, 1)

            def ffn_step(it, ln):
                b, J = it % B, NC * it
                W = slot(it // B + 1)
                if isinstance(it, int) and it == 0:
                    pe.wait_ge(x_new, X_FFN)
                yT_there(N_FFN + b)
                pe.wait_ge(w_lo, HGRN_CHUNKS + 4 * (it // B) + 4)
                for j in range(NC):
                    if j < 2:
                        need(pe, x_new, X_FFN + NT * (it - 1) + 3 + j)
                    else:
                        need(pe, silu_done, J + j - 1)
                    project(j % 2, W + W_GATE + j * P, D, b).then_inc(gate_ready, 1)
                    need(pe, gated_done, J + j - 1)
                    project(2 + j % 2, W + W_UP + j * P, D, b).then_inc(up_ready, 1)
                pe.wait_ge(gated_lo, J + 2)
                for t in range(NT):
                    if t == 2:
                        pe.wait_ge(silu_done, J + 4)
                    back(FFN_BANKS[t], t, gated_h, gated_l, W + W_DOWN, (0, 1), True, False)
                if ln is not None:
                    transpose_ln(ln)
                pe.wait_ge(gated_lo, J + 4)
                for t in range(NT):
                    back(FFN_BANKS[t], t, gated_h, gated_l, W + W_DOWN, (2, 3), False, True).then_inc(out_ready, 1)

            def rope_tile(it, bk, w_off, stride):
                project(bk, w_off, stride, it % B).then_inc(rp_ready, 1)

            def scores(it, h):
                G = GH * it + h
                pe.wait_ge(rp_lo, 5 * it + h + 2)
                for i, (bk, parts) in enumerate(S_TILES):
                    need(pe, s_exp, 4 * G - (3, 1, 0)[i])
                    for qb, at in parts:
                        n = (qb + 1) * P
                        qs = slice(h * L + qb * P, h * L + (qb + 1) * P)
                        mm3(bank[bk][:, at:at + n], q_h[:, qs], q_l[:, qs], k_h[:, 0:n], k_l[:, 0:n], True, False)
                        i_ = nc.tensor.matmul(bank[bk][:, at + qb * P:at + n], ident[:, :], causal[:, :], start=False, stop=True)
                    i_.then_inc(s_ready, 1)

            def transpose_p(G, h):
                pb = (h % 2) * NP
                for i, (bk, kbs) in enumerate(PT_TILES):
                    pe.wait_ge(p_lo, 4 * G + NT - min(kbs))
                    need(pe, {5: ao_lo, 6: pT_vec, 7: pT_act}[bk], 2 * G if bk == 7 else G)
                    base = PT_OFF[kbs[0]]
                    for kb in kbs:
                        for part, src in enumerate((p_h, p_l)):
                            for qb in range(kb, NT):
                                dst = PT_OFF[kb] - base + (part * (NT - kb) + qb - kb) * P
                                s = pb + Q_OFF[qb] + kb * P
                                t = nc.tensor.transpose(bank16[bk][:, dst:dst + P], src[:, s:s + P], ident[:, :])
                    t.then_inc(pT_ready, 1)

            def weigh_v(G, it):
                v0 = (it % 2) * L
                pe.wait_ge(pT_act, 2 * G + 2)
                pe.wait_ge(pT_vec, G + 1)
                for kb in range(NT):
                    n = (NT - kb) * P
                    o = PT_OFF[kb]
                    i = mm3(bank[5][:, kb * P:L], cols(v_h, v0 + kb * P, P), cols(v_l, v0 + kb * P, P),
                            pT[:, o:o + n], pT[:, o + n:o + 2 * n], kb == 0, kb == NT - 1)
                i.then_inc(pv_ready, 1)

            def att_back(it, t):
                if t == 0:
                    pe.wait_ge(ao_lo, GH * (it + 1))
                if t >= 2:
                    pe.wait_ge(x_new, X_ATT + NT * it + (0, 0, 1, 3)[t])
                back(ATT_BANKS[t], t, ao_h, ao_l, slot(it // B + NQ + 1) + W_AO, (0, 1, 2, 3), True, True,
                     ao_at(it, 0)).then_inc(out_ready, 1)

            def values(it):
                b, W = it % B, slot(it // B + NQ + 1)
                for t in range(NT):
                    for k in range(NC):
                        yo, wo = b * (NC * L) + k * L + t * P, W + W_KV + k * 2 * HD + HD
                        i = mm3(bank[1][:, t * P:(t + 1) * P], cols(yT_h, yo, P), cols(yT_l, yo, P),
                                cols(w_h, wo, HD), cols(w_l, wo, HD), k == 0, k == NC - 1)
                i.then_inc(v_ready, 1)

            def query(it, h, bk):
                rope_tile(it, bk, slot(it // B + NQ + 1) + W_Q + h * HD, D)

            def key(it):
                rope_tile(it, 0, slot(it // B + NQ + 1) + W_KV, 2 * HD)

            def att_step(it, ln, prev=True, following=True):
                G, T = GH * it, 5 * it + 3
                scores(it, 0)
                pe.wait_ge(rp_read, T - 1)
                query(it, 2, 0)
                if prev:
                    transpose_p(G - 1, 3)
                pe.wait_ge(rp_read, T)
                values(it)
                if ln is not None:
                    need(pe, pT_act, 2 * G)
                    need(pe, pT_vec, G)
                    transpose_ln(ln)
                if prev:
                    weigh_v(G - 1, it - 1)
                scores(it, 1)
                pe.wait_ge(rp_read, T + 1)
                query(it, 3, 0)
                if ln is not None:
                    yT_there(ln)
                transpose_p(G, 0)
                pe.wait_ge(v_lo, it + 1)
                if prev:
                    att_back(it - 1, 0)
                weigh_v(G, it)
                pe.wait_ge(rp_read, T + 2)
                if prev:
                    att_back(it - 1, 1)
                scores(it, 2)
                if prev:
                    att_back(it - 1, 2)
                transpose_p(G + 1, 1)
                if following:
                    if prev:
                        pe.wait_ge(x_new, X_ATT + NT * (it - 1) + 2)
                    yT_there(N_ATT + (it + 1) % B)
                    pe.wait_ge(w_lo, FIRST_ATT_CHUNK + 4 * ((it + 1) // B) + 4)
                    query(it + 1, 0, 0)
                weigh_v(G + 1, it)
                if prev:
                    att_back(it - 1, 3)
                scores(it, 3)
                if following:
                    pe.wait_ge(rp_read, T + 3)
                    key(it + 1)
                transpose_p(G + 2, 2)
                if following:
                    if prev:
                        pe.wait_ge(x_new, X_ATT + NT * it)
                    query(it + 1, 1, 1)
                weigh_v(G + 2, it)

            def att_begin():
                pe.wait_ge(x_new, X_ATT)
                yT_there(N_ATT)
                pe.wait_ge(w_lo, FIRST_ATT_CHUNK + 4)
                query(0, 0, 0)
                pe.wait_ge(rp_read, 1)
                key(0)
                query(0, 1, 1)

            def att_end(ln):
                G = GH * NKV * B
                transpose_p(G - 1, 3)
                pe.wait_ge(pT_act, 2 * G)
                pe.wait_ge(pT_vec, G)
                transpose_ln(ln)
                weigh_v(G - 1, NKV * B - 1)
                pe.wait_ge(x_new, X_MIX - NT)
                for t in range(NT):
                    att_back(NKV * B - 1, t)

            W_MIX = slot(NQ + NKV + 1)

            def mix_route(b):
                yT_there(N_MIX + b)
                need(pe, gate_step, 12 * b)
                for t in range(NT):
                    for k in range(NC):
                        yo, wo = b * (NC * L) + k * L + t * P, W_MIX + W_RT + k * E
                        i = mm3(bank[2][:, t * E:(t + 1) * E], cols(yT_h, yo, P), cols(yT_l, yo, P),
                                w_h[:, wo:wo + E], w_l[:, wo:wo + E], k == 0, k == NC - 1)
                i.then_inc(lg_ready, 1)
                need(pe, xa_done, b)
                project(4, W_MIX + W_LA, E * R, b).then_inc(xa_ready, 1)

            def mix_begin():
                pe.wait_ge(w_lo, N_CHUNKS)
                mix_route(0)

            def mix_step(b, ln):
                pe.wait_ge(gate_step, 12 * b + 12)
                need(pe, gT_out, b)
                yT_there(N_MIX + (2 if isinstance(b, int) and b == 0 else 3))
                for t in range(NT):
                    nc.tensor.matmul(bank[6][:, t * P:(t + 1) * P], g_h[:, t * P:(t + 1) * P], ident[:, :], start=True, stop=False)
                    i = nc.tensor.matmul(bank[6][:, t * P:(t + 1) * P], g_l[:, t * P:(t + 1) * P], ident[:, :], start=False, stop=True)
                i.then_inc(gT_ready, 1)
                if not (isinstance(b, int) and b == B - 1):
                    mix_route(b + 1)
                for t in range(NT):
                    need(pe, x_new, X_MIX + NT * (b - 1) + t + 1)
                    for k in range(NC):
                        yo, wo = b * (NC * L) + k * L + t * P, W_MIX + W_BASE + k * D
                        mm3(bank[MIX_BANKS[t]][:, :], cols(yT_h, yo, P), cols(yT_l, yo, P),
                            w_h[:, wo:wo + D], w_l[:, wo:wo + D], k == 0, False)
                if ln is not None:
                    pe.wait_ge(gT_out, b + 1)
                    transpose_ln(ln)
                pe.wait_ge(xa_lo, b + 1)
                for t in range(NT):
                    ts = slice(t * P, (t + 1) * P)
                    mm3(bank[MIX_BANKS[t]][:, :], xa_h[:, ts], xa_l[:, ts],
                        w_h[:, W_MIX + W_LB:W_MIX + W_LB + D], w_l[:, W_MIX + W_LB:W_MIX + W_LB + D], False, True).then_inc(out_ready, 1)

            pe.wait_ge(const_in, 16 * 2)
            pe.wait_ge(memset_done, 2)
            transpose_ln(0)
            hgrn_step(0, None)
            with pe.Fori(1, B) as b:
                hgrn_step(b, N_FFN - 1 + b)
            ffn_step(0, N_FFN + B - 1)
            with pe.Fori(1, NQ * B - 3) as it:
                ffn_step(it, None)
            with pe.Fori(NQ * B - 3, NQ * B) as it:
                ffn_step(it, it - (NQ * B - 3) + N_ATT)
            pe.wait_ge(table_in, 16 * 4)
            att_begin()
            att_step(0, N_ATT + B - 1, prev=False)
            with pe.Fori(1, NKV * B - 2) as it:
                att_step(it, None)
            att_step(NKV * B - 2, N_MIX)
            att_step(NKV * B - 1, N_MIX + 1, following=False)
            att_end(N_MIX + 2)
            mix_begin()
            mix_step(0, N_MIX + 3)
            with pe.Fori(1, B - 1) as b:
                mix_step(b, None)
            mix_step(B - 1, None)

        @block.scalar
        def _(act):
            def split_hi(k, dst, n):
                if isinstance(k, int) and k < HGRN_CHUNKS:
                    act.wait_ge(w_first[k], 16)
                else:
                    act.wait_ge(w_loaded, 16 * (k - HGRN_CHUNKS + 1))
                nc.scalar.activation(cols(w_h, dst, n), cols(stage, (k % 2) * CH_BIG, n), ACT.Copy, scale=S_W).then_inc(w_hi, 1)

            def ln_hi_part(n, b):
                act.wait_ge(ln_shift, n + 1)
                for t in range(NT):
                    nc.scalar.activation(y_h[:, t * D:(t + 1) * D], cols(x, (b * NT + t) * D, D), ACT.Identity,
                                         scale=rstd[:, t:t + 1], bias=shift[:, t:t + 1]).then_inc(ln_hi, 1)

            def ln_out(n, b):
                for r in range(2):
                    act.wait_ge(ln_T, 4 * n + 2 * r + 2)
                    nc.scalar.activation(cols(yT_l, b * (NC * L), NC * L).rearrange("p (c n) -> p c n", c=NC)[:, :, 2 * r * P:2 * (r + 1) * P],
                                         bank16[7].rearrange("p (c n) -> p c n", c=NC), ACT.Copy).then_inc(ln_outl, 1)

            def ln_whole(n):
                ln_hi_part(n, n)
                ln_out(n, n)

            def hgrn_step(b, ln):
                J = NC * b

                def gates(c):
                    s = slice((c % 2) * L, (c % 2 + 1) * L)
                    act.wait_ge(i_ready, J + c + 1)
                    nc.scalar.activation(sig_i[:, s], bank[2 + c % 2][:, :], ACT.Sigmoid, scale=PROJ)
                    act.wait_ge(f_ready, J + c + 1)
                    nc.scalar.activation(sig_nf[:, s], bank[c % 2][:, :], ACT.Sigmoid, scale=-PROJ).then_inc(sig_if, 1)
                    nc.scalar.activation(fgate[:, c * L:(c + 1) * L], bank[c % 2][:, :], ACT.Sigmoid, scale=PROJ).then_inc(fgate_done, 1)

                def sig_state(c):
                    s = slice((c % 2) * L, (c % 2 + 1) * L)
                    act.wait_ge(scanned, J + c + 1)
                    nc.scalar.activation(sig_o[:, s], state[:, s], ACT.Sigmoid).then_inc(sigo_done, 1)

                def square_g(c):
                    act.wait_ge(g_ready, J + c + 1)
                    nc.scalar.activation(g_sq[:, c * L:(c + 1) * L], bank[4 + c % 2][:, :], ACT.Square, scale=PROJ).then_inc(gsq_done, 1)

                def hi_u(c):
                    s = slice((c % 2) * L, (c % 2 + 1) * L)
                    act.wait_ge(u_done, J + c + 1)
                    nc.scalar.activation(u_h[:, c * L:(c + 1) * L], u[:, s], ACT.Copy).then_inc(u_hi, 1)

                for c in range(NC):
                    gates(c)
                    if c:
                        sig_state(c - 1)
                    square_g(c)
                    if c:
                        hi_u(c - 1)
                    if isinstance(b, int) and b == 0:
                        if c == 0:
                            for k in range(4, HGRN_CHUNKS):
                                split_hi(k, k * CH_BIG, min(CH_BIG, U_HGRN - k * CH_BIG))
                        if c + 1 < B:
                            ln_whole(c + 1)
                sig_state(3)
                hi_u(3)
                split_hi(b + HGRN_CHUNKS, SLOT1 + b * CH_BIG, CH_BIG)
                if ln is not None:
                    ln_out(ln, b - 1)
                ln_hi_part(N_FFN + b, b)

            def ffn_step(it, ln, norm):
                b, J = it % B, NC * it

                def silu(j):
                    act.wait_ge(gate_ready, J + j + 1)
                    nc.scalar.activation(silu_g[:, (j % 2) * L:(j % 2 + 1) * L], bank[j % 2][:, :], ACT.Silu, scale=PROJ).then_inc(silu_done, 1)

                def hi(j):
                    act.wait_ge(gated_done, J + j + 1)
                    nc.scalar.activation(gated_h[:, j * L:(j + 1) * L], gated[:, j * L:(j + 1) * L], ACT.Copy).then_inc(gated_hi, 1)

                silu(0)
                n = CH_ATT if norm else CH_BIG
                split_hi(it + HGRN_CHUNKS + 4, slot(it // B) + b * n, n)
                for j in range(1, NC):
                    silu(j)
                    hi(j - 1)
                hi(3)
                if ln is not None:
                    ln_out(ln, (b + 3) % B)
                if norm:
                    ln_hi_part(it - (NQ - 1) * B + N_ATT, b)

            def rope_hi(T, half, dst):
                act.wait_ge(rp_sum, T + 1)
                nc.scalar.activation(dst, r_cos[:, half * L:(half + 1) * L], ACT.Copy).then_inc(rp_hi, 1)

            def exps(G, h):
                e = (h % 2) * NP
                o = (h % 2) * NT
                n_done = 0
                for bk, parts in S_TILES:
                    n_done += len(parts)
                    for qb, at in parts:
                        n = (qb + 1) * P
                        act.wait_ge(s_neg, 4 * G + n_done)
                        nc.scalar.activation(p_e[:, e + Q_OFF[qb]:e + Q_OFF[qb] + n], bank[bk][:, at:at + n], ACT.Exp,
                                             scale=-1.0, bias=sneg[:, o + qb:o + qb + 1],
                                             accum_out=ssum[:, o + qb:o + qb + 1]).then_inc(s_exp, 1)

            def probs_hi(G, h):
                act.wait_ge(s_inv, G + 1)
                e = (h % 2) * NP
                for qb in reversed(range(NT)):
                    s = slice(e + Q_OFF[qb], e + Q_OFF[qb] + (qb + 1) * P)
                    nc.scalar.activation(p_h[:, s], p_e[:, s], ACT.Copy, scale=sinv[:, (h % 2) * NT + qb:(h % 2) * NT + qb + 1]).then_inc(p_hi, 1)

            def pT_copy(G):
                for i in (0, 1):
                    bk, kbs = PT_TILES[i]
                    o, n = PT_OFF[kbs[0]], sum(2 * (NT - kb) * P for kb in kbs)
                    act.wait_ge(pT_ready, 3 * G + i + 1)
                    nc.scalar.activation(pT[:, o:o + n], bank16[bk][:, 0:n], ACT.Copy).then_inc(pT_act, 1)

            def ao_part(G, h, it):
                act.wait_ge(pv_ready, G + 1)
                if h == 1:
                    act.wait_ge(out_ready, X_ATT + NT * it)
                nc.scalar.activation(cols(ao_h, ao_at(it, h), L), bank[5][:, :], ACT.Copy, scale=S_A / (S_P * S_Q)).then_inc(ao_hi, 1)

            def att_step(it, ln, norm, prev=True, following=True):
                b, G, T = it % B, GH * it, 5 * it + 3
                exps(G, 0)
                if prev:
                    pT_copy(G - 1)
                rope_hi(T, 0, q_h[:, 2 * L:3 * L])
                probs_hi(G, 0)
                act.wait_ge(v_ready, it + 1)
                nc.scalar.activation(cols(v_h, (it % 2) * L, L), bank[1][:, :], ACT.Copy, scale=S_Q * PROJ).then_inc(v_hi, 1)
                if ln is not None:
                    ln_out(ln, (b + 3) % B if norm is None else (b + 2) % B)
                if prev:
                    ao_part(G - 1, 3, it - 1)
                exps(G + 1, 1)
                pT_copy(G)
                rope_hi(T + 1, 1, q_h[:, 3 * L:4 * L])
                probs_hi(G + 1, 1)
                ao_part(G, 0, it)
                split_hi(it + FIRST_ATT_CHUNK + 4, slot(it // B) + b * CH_ATT, CH_ATT)
                exps(G + 2, 2)
                pT_copy(G + 1)
                probs_hi(G + 2, 2)
                if following:
                    rope_hi(T + 2, 0, q_h[:, 0:L])
                ao_part(G + 1, 1, it)
                exps(G + 3, 3)
                pT_copy(G + 2)
                if following:
                    rope_hi(T + 3, 1, k_h[:, :])
                probs_hi(G + 3, 3)
                ao_part(G + 2, 2, it)
                if following:
                    rope_hi(T + 4, 0, q_h[:, L:2 * L])
                if norm is not None:
                    ln_hi_part(norm, (b + 3) % B)

            def att_begin():
                rope_hi(0, 0, q_h[:, 0:L])
                rope_hi(1, 1, k_h[:, :])
                rope_hi(2, 0, q_h[:, L:2 * L])

            def att_end(ln, norm):
                it = NKV * B
                G = GH * it
                pT_copy(G - 1)
                ln_out(ln, 2)
                ao_part(G - 1, 3, it - 1)
                ln_hi_part(norm, 3)

            def mix_gates(b):
                act.wait_ge(gate_step, 12 * b + 3)
                nc.scalar.activation(lexp[:, :], lshift[:, :], ACT.Exp).then_inc(lexp_done, 1)

            def mix_step(b, ln):
                act.wait_ge(gT_ready, b + 1)
                nc.scalar.activation(gT[:, :], bank[6][:, :], ACT.Copy).then_inc(gT_out, 1)
                act.wait_ge(xa_done, b + 1)
                nc.scalar.activation(xa_h[:, :], xa[:, :], ACT.Copy).then_inc(xa_hi, 1)
                if not (isinstance(b, int) and b == B - 1):
                    mix_gates(b + 1)
                if ln is not None:
                    ln_out(ln, 3)

            ln_whole(0)
            for k in range(4):
                split_hi(k, k * CH_BIG, CH_BIG)
            hgrn_step(0, None)
            with act.Fori(1, B) as b:
                hgrn_step(b, N_FFN - 1 + b)
            ffn_step(0, N_FFN + B - 1, False)
            with act.Fori(1, (NQ - 1) * B) as it:
                ffn_step(it, None, False)
            ffn_step((NQ - 1) * B, None, True)
            with act.Fori(NQ * B - 3, NQ * B) as it:
                ffn_step(it, it - (NQ * B - 3) + N_ATT, True)
            att_begin()
            att_step(0, N_ATT + B - 1, None, prev=False)
            with act.Fori(1, NKV * B - 3) as it:
                att_step(it, None, None)
            att_step(NKV * B - 3, None, N_MIX)
            att_step(NKV * B - 2, N_MIX, N_MIX + 1)
            att_step(NKV * B - 1, N_MIX + 1, N_MIX + 2, following=False)
            att_end(N_MIX + 2, N_MIX + 3)
            mix_gates(0)
            mix_step(0, N_MIX + 3)
            with act.Fori(1, B - 1) as b:
                mix_step(b, None)
            mix_step(B - 1, None)

        @block.vector
        def _(dve):
            def split_lo(k, dst, n):
                dve.wait_ge(w_hi, k + 1)
                nc.vector.scalar_tensor_tensor(out=cols(w_l, dst, n), in0=cols(stage, (k % 2) * CH_BIG, n), scalar=S_W,
                                               in1=cols(w_h, dst, n), op0=ALU.mult, op1=ALU.subtract).then_inc(w_lo, 1)

            def wait_alone(sem, count, column):
                dve.wait_ge(sem, count)
                nc.vector.memset(pause[:, column:column + 1], 0.0)

            def ln_stat_block(n, b, t):
                nc.vector.bn_stats(stats[:, 6 * t:6 * t + 6], cols(x, (b * NT + t) * D, D)).then_inc(ln_stat, 1)

            def ln_moments(n):
                wait_alone(ln_stat, 8 * n + NT, 1)
                for t in range(NT):
                    nc.vector.bn_aggr(moments[:, 2 * t:2 * t + 2], stats[:, 6 * t:6 * t + 6]).then_inc(ln_stat, 1)
                dve.wait_ge(ln_stat, 8 * n + 2 * NT)
                nc.vector.tensor_scalar(var[:, :], moments[:, :].rearrange("p (t s) -> p t s", s=2)[:, :, 1], EPS, S_Y ** -2,
                                        ALU.add, ALU.mult).then_inc(ln_var, 1)

            def ln_lo_part(n, b):
                dve.wait_ge(ln_rstd, n + 1)
                nc.vector.scalar_tensor_tensor(out=shift[:, :], in0=moments[:, :].rearrange("p (t s) -> p t s", s=2)[:, :, 0],
                                               scalar=-1.0, in1=rstd[:, :], op0=ALU.mult, op1=ALU.mult).then_inc(ln_shift, 1)

                def full(t):
                    nc.vector.tensor_scalar(y_full[:, (t % 2) * D:(t % 2 + 1) * D], cols(x, (b * NT + t) * D, D),
                                            moments[:, 2 * t:2 * t + 1], rstd[:, t:t + 1], ALU.subtract, ALU.mult).then_inc(ln_full, 1)

                def lo(t):
                    dve.wait_ge(ln_full, NT * n + t + 1)
                    dve.wait_ge(ln_hi, NT * n + t + 1)
                    nc.vector.tensor_tensor(y_l[:, t * D:(t + 1) * D], y_full[:, (t % 2) * D:(t % 2 + 1) * D],
                                            y_h[:, t * D:(t + 1) * D], ALU.subtract).then_inc(ln_lo, 1)

                full(0)
                full(1)
                for t in range(NT):
                    lo(t)
                    if t + 2 < NT:
                        dve.wait_ge(ln_lo, NT * n + t + 1)
                        full(t + 2)

            def ln_out(n, b):
                for r in range(2):
                    dve.wait_ge(ln_T, 4 * n + 2 * r + 1)
                    nc.vector.tensor_copy(cols(yT_h, b * (NC * L), NC * L).rearrange("p (c n) -> p c n", c=NC)[:, :, 2 * r * P:2 * (r + 1) * P],
                                          bank16[6].rearrange("p (c n) -> p c n", c=NC)).then_inc(ln_outh, 1)

            def ln_whole(n):
                dve.wait_ge(x_loaded[n], 16)
                for t in range(NT):
                    ln_stat_block(n, n, t)
                ln_moments(n)
                ln_lo_part(n, n)
                ln_out(n, n)

            def update_block(X, b, t, banks, scale, n=None):
                dve.wait_ge(out_ready, X + t + 1)
                if n is not None and t:
                    dve.wait_ge(x_new, X + t)
                xb = cols(x, (b * NT + t) * D, D)
                nc.vector.scalar_tensor_tensor(out=xb, in0=bank[banks[t]][:, :], scalar=scale, in1=xb,
                                               op0=ALU.mult, op1=ALU.add).then_inc(x_new, 1)
                if n is not None and t:
                    ln_stat_block(n, b, t - 1)

            def update_end(X, b, n):
                wait_alone(x_new, X + NT, 0)
                ln_stat_block(n, b, NT - 1)
                ln_moments(n)

            def update_x(X, b, banks, scale, n=None):
                for t in range(NT):
                    update_block(X, b, t, banks, scale(t), n)
                if n is not None:
                    update_end(X, b, n)

            def hgrn_step(b, ln):
                J = NC * b

                def scan(c):
                    s = slice((c % 2) * L, (c % 2 + 1) * L)
                    dve.wait_ge(inj_mix, J + c + 1)
                    nc.vector.scalar_tensor_tensor(out=inject[:, s], in0=bank[2 + c % 2][:, :], scalar=PROJ, in1=sig_i[:, s],
                                                   op0=ALU.mult, op1=ALU.mult).then_inc(injected, 1)
                    dve.wait_ge(injected, J + c + 1)
                    dve.wait_ge(fgate_done, J + c + 1)
                    nc.vector.tensor_tensor_scan(state[:, s], fgate[:, c * L:(c + 1) * L], inject[:, s], 0.0,
                                                 ALU.mult, ALU.add).then_inc(scanned, 1)

                def make_u(c):
                    s = slice((c % 2) * L, (c % 2 + 1) * L)
                    dve.wait_ge(sigo_done, J + c + 1)
                    nc.vector.tensor_tensor(sig_o[:, s], sig_o[:, s], state[:, s], ALU.mult).then_inc(silu_o, 1)
                    dve.wait_ge(silu_o, J + c + 1)
                    dve.wait_ge(gsq_done, J + c + 1)
                    nc.vector.scalar_tensor_tensor(out=u[:, s], in0=bank[4 + c % 2][:, :], scalar=gnw_s[:, c:c + 1], in1=sig_o[:, s],
                                                   op0=ALU.mult, op1=ALU.mult).then_inc(u_done, 1)

                def lo_u(c):
                    s = slice((c % 2) * L, (c % 2 + 1) * L)
                    dve.wait_ge(u_hi, J + c + 1)
                    nc.vector.tensor_tensor(u_l[:, c * L:(c + 1) * L], u[:, s], u_h[:, c * L:(c + 1) * L], ALU.subtract).then_inc(u_lo, 1)

                for c in range(NC):
                    scan(c)
                    if c > 1:
                        lo_u(c - 2)
                    if c:
                        make_u(c - 1)
                    if isinstance(b, int) and b == 0:
                        if c == 0:
                            for k in range(4, HGRN_CHUNKS):
                                split_lo(k, k * CH_BIG, min(CH_BIG, U_HGRN - k * CH_BIG))
                        if c + 1 < B:
                            ln_whole(c + 1)
                lo_u(2)
                make_u(3)
                lo_u(3)
                split_lo(b + HGRN_CHUNKS, SLOT1 + b * CH_BIG, CH_BIG)
                dve.wait_ge(ms_ready, b + 1)
                back_scale = (S_U * S_W) ** 2
                nc.vector.tensor_scalar(ms[:, :], bank[4][:, 0:NT], back_scale / D, EPS * back_scale, ALU.mult, ALU.add).then_inc(ms_out, 1)
                if ln is not None:
                    ln_out(ln, b - 1)
                dve.wait_ge(rms_done, b + 1)
                update_x(NT * b, b, HGRN_BANKS, lambda t: rms[:, t:t + 1], N_FFN + b)
                ln_lo_part(N_FFN + b, b)

            def ffn_step(it, ln, norm):
                b, J = it % B, NC * it

                def gate(j):
                    s = slice((j % 2) * L, (j % 2 + 1) * L)
                    dve.wait_ge(silu_done, J + j + 1)
                    dve.wait_ge(up_ready, J + j + 1)
                    nc.vector.scalar_tensor_tensor(out=gated[:, j * L:(j + 1) * L], in0=bank[2 + j % 2][:, :], scalar=PROJ * S_G, in1=silu_g[:, s],
                                                   op0=ALU.mult, op1=ALU.mult).then_inc(gated_done, 1)

                def lo(j):
                    dve.wait_ge(gated_hi, J + j + 1)
                    nc.vector.tensor_tensor(gated_l[:, j * L:(j + 1) * L], gated[:, j * L:(j + 1) * L],
                                            gated_h[:, j * L:(j + 1) * L], ALU.subtract).then_inc(gated_lo, 1)

                gate(0)
                n = CH_ATT if norm else CH_BIG
                split_lo(it + HGRN_CHUNKS + 4, slot(it // B) + b * n, n)
                for j in range(1, NC):
                    gate(j)
                    lo(j - 1)
                lo(3)
                if ln is not None:
                    ln_out(ln, (b + 3) % B)
                n = it - (NQ - 1) * B + N_ATT if norm else None
                update_x(X_FFN + NT * it, b, FFN_BANKS, lambda t: 1.0 / (S_G * S_W), n)
                if norm:
                    ln_lo_part(n, b)

            def rotate(T, half, bk):
                s = slice(half * L, (half + 1) * L)
                h = HD // 2
                dve.wait_ge(rp_ready, T + 1)
                need(dve, rp_lo, T - 1)
                nc.vector.tensor_tensor(r_cos[:, s], bank[bk][:, :], rope_c[:, :], ALU.mult)
                nc.vector.tensor_tensor(r_sin[0:h, s], bank[bk][h:HD, :], rope_s[0:h, :], ALU.mult)
                nc.vector.tensor_tensor(r_sin[h:HD, s], bank[bk][0:h, :], rope_s[h:HD, :], ALU.mult).then_inc(rp_read, 1)

            def maxima(G, h):
                o = (h % 2) * NT
                for i, (bk, parts) in enumerate(S_TILES):
                    dve.wait_ge(s_ready, 3 * G + i + 1)
                    for qb, at in parts:
                        s = bank[bk][:, at:at + (qb + 1) * P]
                        nc.vector.tensor_scalar(s, s, -SCORE, None, ALU.mult, ALU.min, accum_out=sneg[:, o + qb:o + qb + 1]).then_inc(s_neg, 1)

            def recip(G, h):
                o = (h % 2) * NT
                dve.wait_ge(s_exp, 4 * G + 4)
                nc.vector.tensor_scalar(ssum[:, o:o + NT], ssum[:, o:o + NT], 1.0 / S_P, None, ALU.mult).then_inc(s_scaled, 1)
                dve.wait_ge(s_scaled, G + 1)
                nc.vector.reciprocal(sinv[:, o:o + NT], ssum[:, o:o + NT]).then_inc(s_inv, 1)

            def probs_lo(G, h):
                e = (h % 2) * NP
                dve.wait_ge(s_inv, G + 1)
                for qb in reversed(range(NT)):
                    s = slice(e + Q_OFF[qb], e + Q_OFF[qb] + (qb + 1) * P)
                    dve.wait_ge(p_hi, 4 * G + NT - qb)
                    nc.vector.scalar_tensor_tensor(out=p_l[:, s], in0=p_e[:, s], scalar=sinv[:, (h % 2) * NT + qb:(h % 2) * NT + qb + 1],
                                                   in1=p_h[:, s], op0=ALU.mult, op1=ALU.subtract).then_inc(p_lo, 1)

            def pT_copy(G):
                bk, kbs = PT_TILES[2]
                o, n = PT_OFF[kbs[0]], sum(2 * (NT - kb) * P for kb in kbs)
                dve.wait_ge(pT_ready, 3 * G + 3)
                nc.vector.tensor_copy(pT[:, o:o + n], bank16[bk][:, 0:n]).then_inc(pT_vec, 1)

            def ao_part(G, h, it):
                o = ao_at(it, h)
                dve.wait_ge(ao_hi, G + 1)
                nc.vector.scalar_tensor_tensor(out=cols(ao_l, o, L), in0=bank[5][:, :], scalar=S_A / (S_P * S_Q), in1=cols(ao_h, o, L),
                                               op0=ALU.mult, op1=ALU.subtract).then_inc(ao_lo, 1)

            ATT_BACK = 1.0 / (S_A * S_W)

            def att_step(it, ln, norm, prev=True, following=True):
                b, G, T = it % B, GH * it, 5 * it + 3
                X = X_ATT + NT * (it - 1)
                last_b = (b + 3) % B
                maxima(G, 0)
                need(dve, rp_lo, T)
                rotate(T, 0, 0)
                if prev:
                    pT_copy(G - 1)
                recip(G, 0)
                probs_lo(G, 0)
                dve.wait_ge(v_hi, it + 1)
                nc.vector.scalar_tensor_tensor(out=cols(v_l, (it % 2) * L, L), in0=bank[1][:, :], scalar=S_Q * PROJ,
                                               in1=cols(v_h, (it % 2) * L, L), op0=ALU.mult, op1=ALU.subtract).then_inc(v_lo, 1)
                if ln is not None:
                    ln_out(ln, (b + 3) % B if norm is None else (b + 2) % B)
                if prev:
                    ao_part(G - 1, 3, it - 1)
                maxima(G + 1, 1)
                rotate(T + 1, 1, 0)
                pT_copy(G)
                recip(G + 1, 1)
                probs_lo(G + 1, 1)
                if prev:
                    update_block(X, last_b, 0, ATT_BANKS, ATT_BACK, norm)
                ao_part(G, 0, it)
                split_lo(it + FIRST_ATT_CHUNK + 4, slot(it // B) + b * CH_ATT, CH_ATT)
                if prev:
                    update_block(X, last_b, 1, ATT_BANKS, ATT_BACK, norm)
                maxima(G + 2, 2)
                if prev:
                    update_block(X, last_b, 2, ATT_BANKS, ATT_BACK, norm)
                pT_copy(G + 1)
                recip(G + 2, 2)
                probs_lo(G + 2, 2)
                if following:
                    rotate(T + 2, 0, 0)
                ao_part(G + 1, 1, it)
                if prev:
                    update_block(X, last_b, 3, ATT_BANKS, ATT_BACK, norm)
                maxima(G + 3, 3)
                if following:
                    rotate(T + 3, 1, 0)
                pT_copy(G + 2)
                recip(G + 3, 3)
                if norm is not None:
                    update_end(X, last_b, norm)
                probs_lo(G + 3, 3)
                ao_part(G + 2, 2, it)
                if following:
                    rotate(T + 4, 0, 1)
                if norm is not None:
                    ln_lo_part(norm, last_b)

            def att_begin():
                rotate(0, 0, 0)
                rotate(1, 1, 0)
                rotate(2, 0, 1)

            def att_end(ln, norm):
                it = NKV * B
                G = GH * it
                pT_copy(G - 1)
                ln_out(ln, 2)
                ao_part(G - 1, 3, it - 1)
                update_x(X_MIX - NT, 3, ATT_BANKS, lambda t: ATT_BACK, norm)
                ln_lo_part(norm, 3)

            def mix_gates(b):
                g0 = 12 * b
                count = [0]

                def step(ins):
                    ins.then_inc(gate_step, 1)
                    count[0] += 1
                    dve.wait_ge(gate_step, g0 + count[0])

                l3 = logit[:, :].rearrange("p (t e) -> p t e", e=E)
                li = l3[:, :, :, None].to_broadcast([P, NT, E, E])
                lj = l3[:, :, None, :].to_broadcast([P, NT, E, E])
                four = lambda a: a[:, :].rearrange("p (t i j) -> p t i j", i=E, j=E)
                three = lambda a: a[:, :].rearrange("p (t e) -> p t e", e=E)
                dve.wait_ge(lg_ready, b + 1)
                step(nc.vector.scalar_tensor_tensor(out=l3, in0=bank[2][:, 0:NT * E].rearrange("p (t e) -> p t e", e=E), scalar=PROJ,
                                                    in1=gate_b[:, None, :].to_broadcast([P, NT, E]), op0=ALU.mult, op1=ALU.add))
                step(nc.vector.reduce_max(top[:, :], l3, AX.X))
                step(nc.vector.tensor_tensor(three(lshift), l3, top[:, :, None].to_broadcast([P, NT, E]), ALU.subtract))
                step(nc.vector.tensor_tensor(four(above), lj, li, ALU.is_gt))
                step(nc.vector.tensor_tensor(four(equal), lj, li, ALU.is_equal))
                step(nc.vector.tensor_tensor(equal[:, :].rearrange("p (t m) -> p t m", t=NT), equal[:, :].rearrange("p (t m) -> p t m", t=NT),
                                             tri[:, None, :].to_broadcast([P, NT, E * E]), ALU.mult))
                step(nc.vector.tensor_tensor(above[:, :], above[:, :], equal[:, :], ALU.add))
                step(nc.vector.reduce_sum(three(rank), four(above), AX.X))
                dve.wait_ge(lexp_done, b + 1)
                step(nc.vector.scalar_tensor_tensor(out=picked[:, :], in0=rank[:, :], scalar=2.0, in1=lexp[:, :], op0=ALU.is_lt, op1=ALU.mult))
                step(nc.vector.reduce_sum(psum_[:, :], three(picked), AX.X))
                nc.vector.reciprocal(top[:, :], psum_[:, :]).then_inc(gate_rcp, 1)
                dve.wait_ge(gate_rcp, b + 1)
                nc.vector.scalar_tensor_tensor(out=three(gates), in0=three(picked), scalar=S_P, in1=top[:, :, None].to_broadcast([P, NT, E]),
                                               op0=ALU.mult, op1=ALU.mult).then_inc(gate_val, 1)
                dve.wait_ge(gate_val, b + 1)
                spread = gates[:, :, None].to_broadcast([P, NT * E, R])
                step(nc.vector.tensor_copy(g_h[:, :].rearrange("p (e r) -> p e r", r=R), spread))
                step(nc.vector.tensor_tensor(g_l[:, :].rearrange("p (e r) -> p e r", r=R), spread,
                                             g_h[:, :].rearrange("p (e r) -> p e r", r=R), ALU.subtract))

            def mix_step(b, ln):
                dve.wait_ge(gT_out, b + 1)
                dve.wait_ge(xa_ready, b + 1)
                nc.vector.scalar_tensor_tensor(out=xa[:, :], in0=bank[4][:, :], scalar=PROJ * S_X / S_P, in1=gT[:, :],
                                               op0=ALU.mult, op1=ALU.mult).then_inc(xa_done, 1)
                dve.wait_ge(xa_done, b + 1)
                dve.wait_ge(xa_hi, b + 1)
                nc.vector.tensor_tensor(xa_l[:, :], xa[:, :], xa_h[:, :], ALU.subtract).then_inc(xa_lo, 1)
                if not (isinstance(b, int) and b == B - 1):
                    mix_gates(b + 1)
                if ln is not None:
                    ln_out(ln, 3)
                for t in range(NT):
                    dve.wait_ge(out_ready, X_MIX + NT * b + t + 1)
                    dve.wait_ge(biased, NT * b + t + 1)
                    xb = cols(x, (b * NT + t) * D, D)
                    nc.vector.scalar_tensor_tensor(out=xb, in0=bank[MIX_BANKS[t]][:, :], scalar=PROJ, in1=xb,
                                                   op0=ALU.mult, op1=ALU.add).then_inc(x_new, 1)

            dve.wait_ge(const_in, 16 * 2)
            nc.vector.tensor_scalar(gnw_s[:, :], gnw[:, :], PROJ * S_U, None, ALU.mult).then_inc(gnw_ready, 1)
            dve.wait_ge(gnw_ready, 1)
            ln_whole(0)
            for k in range(4):
                split_lo(k, k * CH_BIG, CH_BIG)
            hgrn_step(0, None)
            with dve.Fori(1, B) as b:
                hgrn_step(b, N_FFN - 1 + b)
            ffn_step(0, N_FFN + B - 1, False)
            with dve.Fori(1, (NQ - 1) * B) as it:
                ffn_step(it, None, False)
            ffn_step((NQ - 1) * B, None, True)
            with dve.Fori(NQ * B - 3, NQ * B) as it:
                ffn_step(it, it - (NQ * B - 3) + N_ATT, True)
            att_begin()
            att_step(0, N_ATT + B - 1, None, prev=False)
            with dve.Fori(1, NKV * B - 3) as it:
                att_step(it, None, None)
            att_step(NKV * B - 3, None, N_MIX)
            att_step(NKV * B - 2, N_MIX, N_MIX + 1)
            att_step(NKV * B - 1, N_MIX + 1, N_MIX + 2, following=False)
            att_end(N_MIX + 2, N_MIX + 3)
            dve.wait_ge(late_in, 32)
            mix_gates(0)
            mix_step(0, N_MIX + 3)
            with dve.Fori(1, B - 1) as b:
                mix_step(b, None)
            mix_step(B - 1, None)

        @block.gpsimd
        def _(pool):
            def power(n):
                pool.wait_ge(ln_var, n + 1)
                nc.gpsimd.tensor_tensor(rstd[:, :], var[:, :], minus_half[:, :], ALU.pow).then_inc(ln_rstd, 1)

            def hgrn_step(b):
                J = NC * b

                def mix(c):
                    s = slice((c % 2) * L, (c % 2 + 1) * L)
                    pool.wait_ge(sig_if, J + c + 1)
                    nc.gpsimd.tensor_tensor(sig_i[:, s], sig_i[:, s], sig_nf[:, s], ALU.mult).then_inc(inj_mix, 1)

                def add_square(c):
                    pool.wait_ge(gsq_done, J + c + 1)
                    need(pool, gsum, 3 * b + c - 1)
                    nc.gpsimd.tensor_tensor(g_sq[:, 0:L], g_sq[:, 0:L], g_sq[:, c * L:(c + 1) * L], ALU.add).then_inc(gsum, 1)

                for c in range(NC):
                    mix(c)
                    if c:
                        add_square(c)
                    if isinstance(b, int) and b == 0 and c + 1 < B:
                        power(c + 1)
                pool.wait_ge(ms_out, b + 1)
                nc.gpsimd.tensor_tensor(rms[:, :], ms[:, :], minus_half[:, :], ALU.pow).then_inc(rms_done, 1)
                power(N_FFN + b)

            def rope_add(T, half, hi, lo):
                s = slice(half * L, (half + 1) * L)
                pool.wait_ge(rp_read, T + 1)
                nc.gpsimd.tensor_tensor(r_cos[:, s], r_cos[:, s], r_sin[:, s], ALU.add).then_inc(rp_sum, 1)
                pool.wait_ge(rp_sum, T + 1)
                pool.wait_ge(rp_hi, T + 1)
                nc.gpsimd.tensor_tensor(lo, r_cos[:, s], hi, ALU.subtract).then_inc(rp_lo, 1)

            def query(T, half, h):
                rope_add(T, half, q_h[:, h * L:(h + 1) * L], q_l[:, h * L:(h + 1) * L])

            def att_step(it, norm, following=True):
                T = 5 * it + 3
                query(T, 0, 2)
                query(T + 1, 1, 3)
                if following:
                    query(T + 2, 0, 0)
                if norm is not None:
                    power(norm)
                if following:
                    rope_add(T + 3, 1, k_h[:, :], k_l[:, :])
                    query(T + 4, 0, 1)

            def mix_step(b):
                pool.wait_ge(ln_lo, NT * (N_MIX + b) + NT)
                for t in range(NT):
                    xb = cols(x, (b * NT + t) * D, D)
                    nc.gpsimd.tensor_tensor(xb, xb, bias[:, :], ALU.add).then_inc(biased, 1)

            nc.gpsimd.memset(minus_half[:, :], -0.5).then_inc(memset_done, 1)
            nc.gpsimd.memset(ones[:, :], 1.0).then_inc(memset_done, 1)
            pool.wait_ge(memset_done, 2)
            power(0)
            hgrn_step(0)
            with pool.Fori(1, B) as b:
                hgrn_step(b)
            with pool.Fori(N_ATT, N_ATT + B) as n:
                power(n)
            query(0, 0, 0)
            rope_add(1, 1, k_h[:, :], k_l[:, :])
            query(2, 0, 1)
            with pool.Fori(0, NKV * B - 3) as it:
                att_step(it, None)
            with pool.Fori(NKV * B - 3, NKV * B - 1) as it:
                att_step(it, it - (NKV * B - 3) + N_MIX)
            att_step(NKV * B - 1, N_MIX + 2, following=False)
            power(N_MIX + 3)
            pool.wait_ge(late_in, 32)
            with pool.Fori(0, B) as b:
                mix_step(b)


SCORE = HD ** -0.5 / (S_Q * S_Q)


def _rows(w_t):
    k, n = w_t.shape
    return w_t.reshape(k // P, P, n).transpose(1, 0, 2).reshape(P, -1)


def _chunks(unit, n, count):
    out = np.zeros((count, P, CH_BIG), np.float32)
    for i in range(count):
        part = unit[:, i * n:(i + 1) * n]
        out[i, :, :part.shape[1]] = part
    return out


def kernel(**inputs):
    import concourse.bacc as bacc
    from concourse.bass_utils import run_bass_kernel_spmd
    a = {k: np.asarray(v) for k, v in inputs.items()}

    packed = [_chunks(np.concatenate([_rows(a[f"L0_attn_{n}"].T) for n in ("Wi", "Wf", "Wg", "Wo")], axis=1), CH_BIG, HGRN_CHUNKS)]
    for q in range(NQ):
        s = slice(q * D, (q + 1) * D)
        unit = np.concatenate([_rows(a["L0_ffn_w_gate"][s].T), _rows(a["L0_ffn_w_up"][s].T), _rows(a["L0_ffn_w_down"][:, s].T)], axis=1)
        packed.append(_chunks(unit, CH_BIG, 4))
    wqkv = a["L1_attn_Wqkv"]
    for g in range(NKV):
        q = wqkv[:, g * GH * HD:(g + 1) * GH * HD]
        k = wqkv[:, (NH + g) * HD:(NH + g + 1) * HD]
        v = wqkv[:, (NH + NKV + g) * HD:(NH + NKV + g + 1) * HD]
        wo = a["L1_attn_Wo"][g * GH * HD:(g + 1) * GH * HD]
        packed.append(_chunks(np.concatenate([_rows(q), _rows(np.concatenate([k, v], axis=1)), _rows(wo)], axis=1), CH_ATT, 4))
    unit = np.concatenate([_rows(a["L1_ffn_W"].T), _rows(a["L1_ffn_lora_A"].reshape(E * R, D).T),
                           _rows(a["L1_ffn_lora_B"].transpose(0, 2, 1).reshape(E * R, D)), _rows(a["L1_ffn_gate_w"].T)], axis=1)
    packed.append(_chunks(unit, CH_ATT, 4))

    freqs = (np.float32(1.0) / np.float32(THETA) ** (np.arange(0, HD, 2, dtype=np.float32) / np.float32(HD))).astype(np.float32)
    ang = (freqs[:, None] * np.arange(L, dtype=np.float32)[None, :]).astype(np.float32)
    scale = np.float32(S_Q * PROJ)
    cos, sin = np.cos(ang).astype(np.float32) * scale, np.sin(ang).astype(np.float32) * scale
    rope = np.stack([np.concatenate([cos, cos]), np.concatenate([-sin, sin])])
    lower = np.tril(np.ones((E, E), np.float32), -1).reshape(1, E * E)
    import ml_dtypes
    mask = np.triu(np.full((P, P), MASK_NEG, np.float32), 1).astype(ml_dtypes.bfloat16)
    arrays = {
        "x_in": np.ascontiguousarray(a["L0_attn_hidden_states"]),
        "w_in": np.concatenate(packed),
        "gnw_in": np.ascontiguousarray(a["L0_attn_g_norm_weight"].reshape(NC, P).T),
        "bias_in": np.ascontiguousarray(np.broadcast_to(a["L1_ffn_b"], (P, D))),
        "gate_b_in": np.ascontiguousarray(np.broadcast_to(a["L1_ffn_gate_b"], (P, E))),
        "rope_in": rope,
        "tri_in": np.ascontiguousarray(np.broadcast_to(lower, (P, E * E))),
        "ident_in": np.eye(P, dtype=np.float16),
        "mask_in": mask,
    }
    nc = bacc.Bacc("TRN2", target_bir_lowering=False, num_devices=1)
    args = [nc.dram_tensor(n, v.shape, mybir.dt.from_np(v.dtype), kind="ExternalInput").ap() for n, v in arrays.items()]
    out = nc.dram_tensor("out", [B, L, D], f32, kind="ExternalOutput").ap()
    build(nc, *args, out)
    r = run_bass_kernel_spmd(nc, [arrays], core_ids=[0])
    return r.results[0]["out"]
```

```python
import numpy as np
import concourse.bass as bass
from concourse import mybir
from contextlib import ExitStack

B, L, D = 4, 512, 512
P = 128
NT, NC = L // P, D // P
HID = 2048
NQ = HID // D
NH, NKV, HD = 16, 4, 128
GH = NH // NKV
E, R = 8, 16
EPS = 1e-5
MASK_NEG = -2.3819763e38
THETA = 10000.0

S_Y = 2.0 ** 8
S_W = 2.0 ** 8
S_U = 2.0 ** 8
S_G = 2.0 ** 6
S_Q = 2.0 ** 6
S_P = 2.0 ** 8
S_A = 2.0 ** 6
S_X = 2.0 ** 8
PROJ = 1.0 / (S_Y * S_W)

U_HGRN = 4 * NC * D
U_FFN = 3 * NC * D
U_ATT = NC * D + NC * 2 * HD + GH * D
CH_BIG, CH_ATT = U_FFN // 4, U_ATT // 4
HGRN_CHUNKS = -(-U_HGRN // CH_BIG)
SLOT1 = U_HGRN
W_COLS = SLOT1 + U_FFN
N_CHUNKS = HGRN_CHUNKS + 4 * (NQ + NKV + 1)
FIRST_ATT_CHUNK = HGRN_CHUNKS + 4 * NQ
W_I, W_F, W_G, W_O = 0, NC * P, 2 * NC * P, 3 * NC * D
W_GATE, W_UP, W_DOWN = 0, NC * D, 2 * NC * D
W_Q, W_KV, W_AO = 0, NC * D, NC * D + NC * 2 * HD
W_BASE, W_LA, W_LB, W_RT = 0, NC * D, NC * D + NC * P, NC * D + NC * P + D

ALU = mybir.AluOpType
ACT = mybir.ActivationFunctionType
AX = mybir.AxisListType
f32, f16, bf16 = mybir.dt.float32, mybir.dt.float16, mybir.dt.bfloat16


def slot(unit):
    return (unit % 2) * SLOT1


def cols(t, start, n):
    return t[:, start:start + n] if isinstance(start, int) else t[:, bass.ds(start, n)]


def need(eng, sem, count):
    if not (isinstance(count, int) and count <= 0):
        eng.wait_ge(sem, count)


def first_ln(b):
    return 0 if isinstance(b, int) and b == 0 else 2 * b - 1


def second_ln(b):
    return 2 * B - 1 if isinstance(b, int) and b == B - 1 else 2 * b + 2


def ao_at(it, h):
    return h * L if h else (it % 2) * GH * L


def build(nc, x_in, w_in, gnw_in, bias_in, gate_b_in, rope_in, tri_in, ident_in, mask_in, out):
    ctx = ExitStack()
    with ctx:
        def sb(name, n, dt=f32, parts=P):
            return ctx.enter_context(nc.sbuf_tensor(name, [parts, n], dt))

        def sem(name):
            return ctx.enter_context(nc.semaphore(name))

        x = sb("x", B * NT * D)
        yT_h, yT_l = sb("yT_h", B * NC * L, f16), sb("yT_l", B * NC * L, f16)
        w_h, w_l = sb("w_h", W_COLS, f16), sb("w_l", W_COLS, f16)
        stage = sb("stage", 2 * CH_BIG)
        y_h, y_l = sb("y_h", NT * D, f16), sb("y_l", NT * D, f16)
        y_full = sb("y_full", 2 * D)
        stats, moments = sb("stats", NT * 6), sb("moments", NT * 2)
        var, rstd, shift = sb("var", NT), sb("rstd", NT), sb("shift", NT)
        minus_half = sb("minus_half", NT)
        ones, pause = sb("ones", 1), sb("pause", 2)
        gnw, gnw_s = sb("gnw", NC), sb("gnw_s", NC)
        gate_b, tri = sb("gate_b", E), sb("tri", E * E)
        ident, causal = sb("ident", P, f16), sb("causal", P, bf16)
        rope_c, rope_s = sb("rope_c", L), sb("rope_s", L)

        stage_ctx = ExitStack()

        def tmp(name, n, dt=f32):
            return stage_ctx.enter_context(nc.sbuf_tensor(name, [P, n], dt))

        with stage_ctx:
            sig_i, sig_nf = tmp("sig_i", 2 * L), tmp("sig_nf", 2 * L)
            fgate = tmp("fgate", NC * L)
            inject, state = tmp("inject", 2 * L), tmp("state", 2 * L)
            sig_o, u = tmp("sig_o", 2 * L), tmp("u", 2 * L)
            g_sq = tmp("g_sq", NC * L)
            u_h, u_l = tmp("u_h", NC * L, f16), tmp("u_l", NC * L, f16)
            ms, rms = tmp("ms", NT), tmp("rms", NT)
        stage_ctx = ExitStack()
        with stage_ctx:
            silu_g, gated = tmp("silu_g", 2 * L), tmp("gated", NC * L)
            gated_h, gated_l = tmp("gated_h", NC * L, f16), tmp("gated_l", NC * L, f16)
        stage_ctx = ExitStack()
        with stage_ctx:
            r_cos, r_sin = tmp("r_cos", 2 * L), tmp("r_sin", 2 * L)
            k_h, k_l = tmp("k_h", L, f16), tmp("k_l", L, f16)
            v_h, v_l = tmp("v_h", 2 * L, f16), tmp("v_l", 2 * L, f16)
            q_h, q_l = tmp("q_h", GH * L, f16), tmp("q_l", GH * L, f16)
            NP = NT * (NT + 1) // 2 * P
            p_e = tmp("p_e", 2 * NP)
            p_h, p_l = tmp("p_h", 2 * NP, f16), tmp("p_l", 2 * NP, f16)
            pT = tmp("pT", 2 * NP, f16)
            ao_h, ao_l = tmp("ao_h", (GH + 1) * L, f16), tmp("ao_l", (GH + 1) * L, f16)
            sneg, ssum, sinv = tmp("sneg", 8), tmp("ssum", 8), tmp("sinv", 8)
        stage_ctx = ExitStack()
        with stage_ctx:
            logit, top, lshift, lexp = tmp("logit", NT * E), tmp("top", NT), tmp("lshift", NT * E), tmp("lexp", NT * E)
            above, equal, rank = tmp("above", NT * E * E), tmp("equal", NT * E * E), tmp("rank", NT * E)
            picked, psum_, gates = tmp("picked", NT * E), tmp("picked_sum", NT), tmp("gates", NT * E)
            g_h, g_l = tmp("g_h", NT * E * R, f16), tmp("g_l", NT * E * R, f16)
            gT, xa = tmp("gT", L), tmp("xa", L)
            xa_h, xa_l = tmp("xa_h", L, f16), tmp("xa_l", L, f16)
            bias = tmp("bias", D)

        bank = [ctx.enter_context(nc.psum_tensor(f"bank{i}", [P, L], f32)) for i in range(8)]
        bank16 = [bk[:, :].bitcast(f16) for bk in bank]

        const_in, table_in = sem("const_in"), sem("table_in")
        late_in = sem("late_in")
        x_first = [sem(f"x_first{t}") for t in range(NT)]
        x_loaded = [None] + [sem(f"x_loaded{b}") for b in range(1, B)]
        w_first = [sem(f"w_first{k}") for k in range(HGRN_CHUNKS)]
        w_loaded, w_hi, w_lo = sem("w_loaded"), sem("w_hi"), sem("w_lo")
        memset_done, gnw_ready = sem("memset_done"), sem("gnw_ready")
        ln_stat, ln_var, ln_rstd, ln_shift = sem("ln_stat"), sem("ln_var"), sem("ln_rstd"), sem("ln_shift")
        ln_hi, ln_full, ln_lo = sem("ln_hi"), sem("ln_full"), sem("ln_lo")
        ln_T, ln_outh, ln_outl = sem("ln_T"), sem("ln_outh"), sem("ln_outl")
        out_ready, x_new = sem("out_ready"), sem("x_new")
        i_ready, f_ready, g_ready = sem("i_ready"), sem("f_ready"), sem("g_ready")
        sig_if, fgate_done, inj_mix, injected = sem("sig_if"), sem("fgate_done"), sem("inj_mix"), sem("injected")
        scanned, sigo_done, silu_o, u_done = sem("scanned"), sem("sigo_done"), sem("silu_o"), sem("u_done")
        u_hi, u_lo, gsq_done, gsum = sem("u_hi"), sem("u_lo"), sem("gsq_done"), sem("gsum")
        ms_ready, ms_out, rms_done = sem("ms_ready"), sem("ms_out"), sem("rms_done")
        gate_ready, up_ready, silu_done = sem("gate_ready"), sem("up_ready"), sem("silu_done")
        gated_done, gated_hi, gated_lo = sem("gated_done"), sem("gated_hi"), sem("gated_lo")
        rp_ready, rp_read, rp_sum, rp_hi, rp_lo = (sem(n) for n in ("rp_ready", "rp_read", "rp_sum", "rp_hi", "rp_lo"))
        v_ready, v_hi, v_lo = sem("v_ready"), sem("v_hi"), sem("v_lo")
        s_ready, s_neg, s_exp, s_scaled, s_inv = (sem(n) for n in ("s_ready", "s_neg", "s_exp", "s_scaled", "s_inv"))
        p_hi, p_lo, pT_ready, pT_vec, pT_act = (sem(n) for n in ("p_hi", "p_lo", "pT_ready", "pT_vec", "pT_act"))
        pv_ready, ao_hi, ao_lo = sem("pv_ready"), sem("ao_hi"), sem("ao_lo")
        lg_ready, xa_ready, gT_ready = sem("lg_ready"), sem("xa_ready"), sem("gT_ready")
        gate_step, lexp_done, gT_out, xa_done, xa_hi, xa_lo = (sem(n) for n in ("gate_step", "lexp_done", "gT_out", "xa_done", "xa_hi", "xa_lo"))
        gate_rcp, gate_val = sem("gate_rcp"), sem("gate_val")
        biased, stored = sem("biased"), sem("stored")

        block = ctx.enter_context(nc.Block())

        X_FFN, X_ATT, X_MIX = 4 * B, 4 * B + 4 * NQ * B, 4 * B + 4 * NQ * B + 4 * NKV * B
        N_ATT, N_MIX = 2 * B, 3 * B
        HGRN_BANKS, FFN_BANKS, ATT_BANKS, MIX_BANKS = (0, 1, 2, 3), (4, 5, 0, 1), (1, 0, 1, 1), (0, 1, 5, 3)
        END_BANKS = (3, 5, 3, 5)
        Q_OFF = [sum(range(t + 1)) * P for t in range(NT)]
        S_TILES = ((2, ((3, 0),)), (3, ((2, 0), (0, 3 * P))), (4, ((1, 0),)))
        PT_TILES = ((5, (2, 3)), (7, (1,)), (6, (0,)))
        PT_OFF, at = {}, 0
        for _, kbs in PT_TILES:
            for kb in kbs:
                PT_OFF[kb] = at
                at += 2 * (NT - kb) * P

        @block.sync
        def _(eng):
            def first_chunk(k):
                n = min(CH_BIG, U_HGRN - k * CH_BIG)
                if k >= 2:
                    eng.wait_ge(w_lo, k - 1)
                eng.dma_start(stage[:, (k % 2) * CH_BIG:(k % 2) * CH_BIG + n], w_in[k, :, 0:n]).then_inc(w_first[k], 16)

            def load_x(b):
                eng.dma_start(x[:, b * NT * D:(b + 1) * NT * D].rearrange("p (t d) -> p t d", t=NT),
                              x_in[b].rearrange("(t p) d -> p t d", p=P)).then_inc(x_loaded[b], 16)

            for t in range(NT):
                eng.dma_start(x[:, t * D:(t + 1) * D], x_in[0, t * P:(t + 1) * P]).then_inc(x_first[t], 16)
            first_chunk(0)
            eng.dma_start(ident[:, :], ident_in).then_inc(const_in, 16)
            eng.dma_start(gnw[:, :], gnw_in).then_inc(const_in, 16)
            first_chunk(1)
            load_x(1)
            first_chunk(2)
            first_chunk(3)
            for b in range(2, B):
                load_x(b)
            eng.dma_start(rope_c[:, :], rope_in[0]).then_inc(table_in, 16)
            eng.dma_start(rope_s[:, :], rope_in[1]).then_inc(table_in, 16)
            eng.dma_start(causal[:, :], mask_in).then_inc(table_in, 16)
            eng.dma_start(gate_b[:, :], gate_b_in).then_inc(table_in, 16)
            eng.dma_start(tri[:, :], tri_in).then_inc(table_in, 16)
            for k in range(4, HGRN_CHUNKS):
                first_chunk(k)

            def later_chunk(k, n):
                eng.wait_ge(w_lo, k)
                eng.dma_start(cols(stage, (k % 2) * CH_BIG, n), w_in[k, :, 0:n] if isinstance(k, int)
                              else w_in[bass.ds(k, 1), :, 0:n].rearrange("a p n -> (a p) n")).then_inc(w_loaded, 16)
            later_chunk(HGRN_CHUNKS, CH_BIG)
            with eng.Fori(HGRN_CHUNKS + 1, FIRST_ATT_CHUNK) as k:
                later_chunk(k, CH_BIG)
            with eng.Fori(FIRST_ATT_CHUNK, N_CHUNKS) as k:
                later_chunk(k, CH_ATT)
            eng.wait_ge(x_new, X_MIX)
            eng.dma_start(bias[:, :], bias_in).then_inc(late_in, 16)
            with eng.Fori(0, B) as b:
                eng.wait_ge(x_new, X_MIX + NT * b + NT)
                eng.dma_start(out[bass.ds(b, 1)].rearrange("a (t p) d -> p (a t) d", p=P),
                              cols(x, b * NT * D, NT * D).rearrange("p (t d) -> p t d", t=NT)).then_inc(stored, 16)
            eng.wait_ge(stored, 16 * B)

        @block.tensor
        def _(pe):
            def mm3(dst, ah, al, bh, bl, first, last):
                nc.tensor.matmul(dst, ah, bh, start=first, stop=False)
                nc.tensor.matmul(dst, ah, bl, start=False, stop=False)
                return nc.tensor.matmul(dst, al, bh, start=False, stop=last)

            def project(bk, w_off, stride, b):
                for k in range(NC):
                    wo, yo = w_off + k * stride, b * (NC * L) + k * L
                    i = mm3(bank[bk][:, :], cols(w_h, wo, P), cols(w_l, wo, P), cols(yT_h, yo, L), cols(yT_l, yo, L),
                            k == 0, k == NC - 1)
                return i

            def back(bk, t, ah, al, w_off, chunks, first, last, first_at=0):
                for c in chunks:
                    o = (first_at if c == 0 else c * L) + t * P
                    i = mm3(bank[bk][:, :], cols(ah, o, P), cols(al, o, P),
                            cols(w_h, w_off + c * D, D), cols(w_l, w_off + c * D, D),
                            first and c == chunks[0], last and c == chunks[-1])
                return i

            def transpose_ln(n, rounds=(0, 1)):
                for r in rounds:
                    need(pe, ln_hi, NT * n + 2 * r + 2)
                    need(pe, ln_lo, NT * n + 2 * r + 2)
                    for bk, src, emptied in ((6, y_h, ln_outh), (7, y_l, ln_outl)):
                        need(pe, emptied, 2 * n + r)
                        for t in range(2):
                            for c in range(NC):
                                i = nc.tensor.transpose(bank16[bk][:, (2 * c + t) * P:(2 * c + t + 1) * P],
                                                        src[:, (2 * r + t) * D + c * P:(2 * r + t) * D + (c + 1) * P], ident[:, :])
                        i.then_inc(ln_T, 1)

            def yT_there(n):
                need(pe, ln_outh, 2 * n + 2)
                need(pe, ln_outl, 2 * n + 2)

            def hgrn_step(b):
                J = NC * b
                first, last = (isinstance(b, int) and b == n for n in (0, B - 1))
                yT_there(first_ln(b))
                for c in range(NC):
                    ln = None if (c != 1 or first) and (c != 3 or last) else second_ln(b - 1) if c == 1 else first_ln(b + 1)
                    need(pe, x_new, NT * (b - 1) + 1 + c if c < 2 else 0)
                    need(pe, fgate_done, J + c - 1)
                    if first:
                        pe.wait_ge(w_lo, c + 1)
                    project(c % 2, W_F + c * CH_BIG, P, b).then_inc(f_ready, 1)
                    need(pe, x_new, NT * (b - 1) + 3 + c if c < 2 else 0)
                    need(pe, injected, J + c - 1)
                    project(2 + c % 2, W_I + c * CH_BIG, P, b).then_inc(i_ready, 1)
                    if ln is not None:
                        transpose_ln(ln, (0,))
                    need(pe, u_done, J + c - 1)
                    if c == 0:
                        need(pe, ms_out, b)
                    project(4 + c % 2, W_G + c * CH_BIG, P, b).then_inc(g_ready, 1)
                    if ln is not None:
                        transpose_ln(ln, (1,))
                if first:
                    pe.wait_ge(w_lo, HGRN_CHUNKS)
                pe.wait_ge(u_lo, J + 2)
                for t in range(NT):
                    if t == 0:
                        pe.wait_ge(fgate_done, J + 4)
                    if t == 2:
                        pe.wait_ge(injected, J + 4)
                    back(HGRN_BANKS[t], t, u_h, u_l, W_O, (0, 1), True, False)
                pe.wait_ge(gsum, 3 * b + 3)
                pe.wait_ge(u_done, J + 3)
                for t in range(NT):
                    i = nc.tensor.matmul(bank[4][:, t:t + 1], g_sq[:, t * P:(t + 1) * P], ones[:, :], start=True, stop=True)
                i.then_inc(ms_ready, 1)
                for chunk in (2, 3):
                    pe.wait_ge(u_lo, J + chunk + 1)
                    for t in range(NT):
                        i = back(HGRN_BANKS[t], t, u_h, u_l, W_O, (chunk,), False, chunk == 3)
                        if chunk == 3:
                            i.then_inc(out_ready, 1)

            def ffn_step(it, ln):
                b, J = it % B, NC * it
                W = slot(it // B + 1)
                first = isinstance(it, int) and it == 0
                yT_there(second_ln(0 if isinstance(it, int) and it == 0 else B - 1))
                pe.wait_ge(w_lo, HGRN_CHUNKS + 4 * (it // B) + 4)
                for j in range(NC):
                    if j < 2 and first:
                        pe.wait_ge(x_new, X_FFN - 3 + j)
                    elif j < 2:
                        need(pe, x_new, X_FFN + NT * (it - 1) + 3 + j)
                    else:
                        need(pe, silu_done, J + j - 1)
                    project(j % 2, W + W_GATE + j * P, D, b).then_inc(gate_ready, 1)
                    if j < 2 and first:
                        pe.wait_ge(x_new, X_FFN - 1 + j)
                    need(pe, gated_done, J + j - 1)
                    project(2 + j % 2, W + W_UP + j * P, D, b).then_inc(up_ready, 1)
                if ln is not None:
                    transpose_ln(ln, (0,))
                pe.wait_ge(gated_lo, J + 2)
                for t in range(NT):
                    if t == 2:
                        pe.wait_ge(silu_done, J + 4)
                    back(FFN_BANKS[t], t, gated_h, gated_l, W + W_DOWN, (0, 1), True, False)
                if ln is not None:
                    transpose_ln(ln, (1,))
                pe.wait_ge(gated_lo, J + 4)
                for t in range(NT):
                    back(FFN_BANKS[t], t, gated_h, gated_l, W + W_DOWN, (2, 3), False, True).then_inc(out_ready, 1)

            W_MIX = slot(NQ + NKV + 1)

            def rope_tile(it, bk, w_off, stride):
                project(bk, w_off, stride, it % B).then_inc(rp_ready, 1)

            def scores(it, h):
                G = GH * it + h
                pe.wait_ge(rp_lo, 5 * it + h + 2)
                for i, (bk, parts) in enumerate(S_TILES):
                    need(pe, s_exp, 4 * G - (3, 1, 0)[i])
                    for qb, at in parts:
                        n = (qb + 1) * P
                        qs = slice(h * L + qb * P, h * L + (qb + 1) * P)
                        mm3(bank[bk][:, at:at + n], q_h[:, qs], q_l[:, qs], k_h[:, 0:n], k_l[:, 0:n], True, False)
                        i_ = nc.tensor.matmul(bank[bk][:, at + qb * P:at + n], ident[:, :], causal[:, :], start=False, stop=True)
                    i_.then_inc(s_ready, 1)

            def transpose_p(G, h):
                pb = (h % 2) * NP
                for i, (bk, kbs) in enumerate(PT_TILES):
                    pe.wait_ge(p_lo, 4 * G + NT - min(kbs))
                    need(pe, {5: ao_lo, 6: pT_vec, 7: pT_act}[bk], 2 * G if bk == 7 else G)
                    base = PT_OFF[kbs[0]]
                    for kb in kbs:
                        for part, src in enumerate((p_h, p_l)):
                            for qb in range(kb, NT):
                                dst = PT_OFF[kb] - base + (part * (NT - kb) + qb - kb) * P
                                s = pb + Q_OFF[qb] + kb * P
                                t = nc.tensor.transpose(bank16[bk][:, dst:dst + P], src[:, s:s + P], ident[:, :])
                    t.then_inc(pT_ready, 1)

            def weigh_v(G, it):
                v0 = (it % 2) * L
                pe.wait_ge(pT_act, 2 * G + 2)
                pe.wait_ge(pT_vec, G + 1)
                for kb in range(NT):
                    n = (NT - kb) * P
                    o = PT_OFF[kb]
                    i = mm3(bank[5][:, kb * P:L], cols(v_h, v0 + kb * P, P), cols(v_l, v0 + kb * P, P),
                            pT[:, o:o + n], pT[:, o + n:o + 2 * n], kb == 0, kb == NT - 1)
                i.then_inc(pv_ready, 1)

            def att_back(it, t, end=False):
                if t == 0:
                    pe.wait_ge(ao_lo, GH * (it + 1))
                if t >= 2:
                    pe.wait_ge(x_new, X_ATT + NT * it + ((0, 0, 1, 2) if end else (0, 0, 1, 3))[t])
                back((END_BANKS if end else ATT_BANKS)[t], t, ao_h, ao_l, slot(it // B + NQ + 1) + W_AO, (0, 1, 2, 3), True, True,
                     ao_at(it, 0)).then_inc(out_ready, 1)

            def values(it):
                b, W = it % B, slot(it // B + NQ + 1)
                for t in range(NT):
                    for k in range(NC):
                        yo, wo = b * (NC * L) + k * L + t * P, W + W_KV + k * 2 * HD + HD
                        i = mm3(bank[1][:, t * P:(t + 1) * P], cols(yT_h, yo, P), cols(yT_l, yo, P),
                                cols(w_h, wo, HD), cols(w_l, wo, HD), k == 0, k == NC - 1)
                i.then_inc(v_ready, 1)

            def query(it, h, bk):
                rope_tile(it, bk, slot(it // B + NQ + 1) + W_Q + h * HD, D)

            def key(it, bk=0):
                rope_tile(it, bk, slot(it // B + NQ + 1) + W_KV, 2 * HD)

            def mix_base(b, t):
                for k in range(NC):
                    yo, wo = b * (NC * L) + k * L + t * P, W_MIX + W_BASE + k * D
                    mm3(bank[MIX_BANKS[t]][:, :], cols(yT_h, yo, P), cols(yT_l, yo, P),
                        w_h[:, wo:wo + D], w_l[:, wo:wo + D], k == 0, False)

            def att_step(it, ln, prev=True, following=True):
                G, T = GH * it, 5 * it + 3
                scores(it, 0)
                pe.wait_ge(rp_read, T - 1)
                query(it, 2, 0)
                if prev:
                    yT_there(N_ATT + B - 1 if ln is None else ln - 1)
                    transpose_p(G - 1, 3)
                pe.wait_ge(rp_read, T)
                values(it)
                if prev:
                    weigh_v(G - 1, it - 1)
                scores(it, 1)
                pe.wait_ge(rp_read, T + 1)
                query(it, 3, 0)
                transpose_p(G, 0)
                pe.wait_ge(v_lo, it + 1)
                if prev:
                    att_back(it - 1, 0)
                weigh_v(G, it)
                pe.wait_ge(rp_read, T + 2)
                if prev:
                    att_back(it - 1, 1)
                scores(it, 2)
                if prev:
                    att_back(it - 1, 2)
                transpose_p(G + 1, 1)
                if following:
                    if prev:
                        pe.wait_ge(x_new, X_ATT + NT * (it - 1) + 2)
                    yT_there(N_ATT + (it + 1) % B)
                    pe.wait_ge(w_lo, FIRST_ATT_CHUNK + 4 * ((it + 1) // B) + 4)
                    query(it + 1, 0, 0)
                else:
                    pe.wait_ge(x_new, X_ATT + NT * (it - 1) + 2)
                    yT_there(N_MIX)
                    pe.wait_ge(w_lo, N_CHUNKS)
                    mix_base(0, 0)
                weigh_v(G + 1, it)
                if ln is not None:
                    transpose_ln(ln, (0,))
                if prev:
                    att_back(it - 1, 3)
                scores(it, 3)
                if following:
                    pe.wait_ge(rp_read, T + 3)
                    key(it + 1)
                if ln is not None:
                    pe.wait_ge(ln_outh, 2 * ln + 1)
                    pe.wait_ge(ln_outl, 2 * ln + 1)
                transpose_p(G + 2, 2)
                if following:
                    if prev:
                        pe.wait_ge(x_new, X_ATT + NT * it)
                    query(it + 1, 1, 1)
                else:
                    pe.wait_ge(x_new, X_ATT + NT * it)
                    mix_base(0, 1)
                weigh_v(G + 2, it)
                if ln is not None:
                    transpose_ln(ln, (1,))

            def att_begin():
                yT_there(N_ATT)
                pe.wait_ge(w_lo, FIRST_ATT_CHUNK + 4)
                query(0, 0, 2)
                key(0, 3)
                pe.wait_ge(x_new, X_ATT)
                query(0, 1, 1)

            def att_end(ln):
                G = GH * NKV * B
                yT_there(ln - 1)
                transpose_p(G - 1, 3)
                pe.wait_ge(pT_act, 2 * G)
                pe.wait_ge(pT_vec, G)
                mix_begin()
                weigh_v(G - 1, NKV * B - 1)
                transpose_ln(ln, (0,))
                for t in range(NT):
                    att_back(NKV * B - 1, t, end=True)
                    if t == 0:
                        transpose_ln(ln, (1,))

            def mix_route(b):
                yT_there(N_MIX + b)
                need(pe, gate_step, 12 * b)
                for t in range(NT):
                    for k in range(NC):
                        yo, wo = b * (NC * L) + k * L + t * P, W_MIX + W_RT + k * E
                        i = mm3(bank[2][:, t * E:(t + 1) * E], cols(yT_h, yo, P), cols(yT_l, yo, P),
                                w_h[:, wo:wo + E], w_l[:, wo:wo + E], k == 0, k == NC - 1)
                i.then_inc(lg_ready, 1)
                need(pe, xa_done, b)
                project(4, W_MIX + W_LA, E * R, b).then_inc(xa_ready, 1)

            def mix_begin():
                pe.wait_ge(w_lo, N_CHUNKS)
                pe.wait_ge(s_exp, 4 * GH * NKV * B)
                mix_route(0)

            def mix_step(b, ln):
                pe.wait_ge(gate_step, 12 * b + 12)
                need(pe, gT_out, b)
                yT_there(N_MIX + (2 if isinstance(b, int) and b == 0 else 3))
                for t in range(NT):
                    nc.tensor.matmul(bank[6][:, t * P:(t + 1) * P], g_h[:, t * P:(t + 1) * P], ident[:, :], start=True, stop=False)
                    i = nc.tensor.matmul(bank[6][:, t * P:(t + 1) * P], g_l[:, t * P:(t + 1) * P], ident[:, :], start=False, stop=True)
                i.then_inc(gT_ready, 1)
                for t in range(NT):
                    if t == 2 and not (isinstance(b, int) and b == B - 1):
                        mix_route(b + 1)
                    if isinstance(b, int) and b == 0:
                        if t >= 2:
                            pe.wait_ge(x_new, X_MIX)
                            mix_base(b, t)
                    else:
                        pe.wait_ge(x_new, X_MIX + NT * (b - 1) + t + 1)
                        mix_base(b, t)
                    if ln is not None and t >= 2:
                        pe.wait_ge(gT_out, b + 1)
                        transpose_ln(ln, (t - 2,))
                pe.wait_ge(xa_lo, b + 1)
                for t in range(NT):
                    ts = slice(t * P, (t + 1) * P)
                    mm3(bank[MIX_BANKS[t]][:, :], xa_h[:, ts], xa_l[:, ts],
                        w_h[:, W_MIX + W_LB:W_MIX + W_LB + D], w_l[:, W_MIX + W_LB:W_MIX + W_LB + D], False, True).then_inc(out_ready, 1)

            pe.wait_ge(const_in, 16 * 2)
            pe.wait_ge(memset_done, 2)
            transpose_ln(0)
            hgrn_step(0)
            with pe.Fori(1, B - 1) as b:
                hgrn_step(b)
            hgrn_step(B - 1)
            ffn_step(0, second_ln(B - 1))
            with pe.Fori(1, NQ * B - 3) as it:
                ffn_step(it, None)
            with pe.Fori(NQ * B - 3, NQ * B) as it:
                ffn_step(it, it - (NQ * B - 3) + N_ATT)
            pe.wait_ge(table_in, 16 * 5)
            att_begin()
            att_step(0, None, prev=False)
            att_step(1, N_ATT + B - 1)
            with pe.Fori(2, NKV * B - 2) as it:
                att_step(it, None)
            att_step(NKV * B - 2, N_MIX)
            att_step(NKV * B - 1, N_MIX + 1, following=False)
            att_end(N_MIX + 2)
            mix_step(0, N_MIX + 3)
            with pe.Fori(1, B - 1) as b:
                mix_step(b, None)
            mix_step(B - 1, None)

        @block.scalar
        def _(act):
            def split_hi(k, dst, n):
                if isinstance(k, int) and k < HGRN_CHUNKS:
                    act.wait_ge(w_first[k], 16)
                else:
                    act.wait_ge(w_loaded, 16 * (k - HGRN_CHUNKS + 1))
                nc.scalar.activation(cols(w_h, dst, n), cols(stage, (k % 2) * CH_BIG, n), ACT.Copy, scale=S_W).then_inc(w_hi, 1)

            def ln_hi_part(n, b, blocks=range(NT)):
                act.wait_ge(ln_shift, n + 1)
                for t in blocks:
                    nc.scalar.activation(y_h[:, t * D:(t + 1) * D], cols(x, (b * NT + t) * D, D), ACT.Identity,
                                         scale=rstd[:, t:t + 1], bias=shift[:, t:t + 1]).then_inc(ln_hi, 1)

            def ln_out(n, b, rounds=(0, 1)):
                for r in rounds:
                    act.wait_ge(ln_T, 4 * n + 2 * r + 2)
                    nc.scalar.activation(cols(yT_l, b * (NC * L), NC * L).rearrange("p (c n) -> p c n", c=NC)[:, :, 2 * r * P:2 * (r + 1) * P],
                                         bank16[7].rearrange("p (c n) -> p c n", c=NC), ACT.Copy).then_inc(ln_outl, 1)

            def hgrn_step(b):
                J = NC * b
                first, last = (isinstance(b, int) and b == n for n in (0, B - 1))

                def gates(c):
                    s = slice((c % 2) * L, (c % 2 + 1) * L)
                    act.wait_ge(f_ready, J + c + 1)
                    nc.scalar.activation(sig_nf[:, s], bank[c % 2][:, :], ACT.Sigmoid, scale=-PROJ)
                    nc.scalar.activation(fgate[:, c * L:(c + 1) * L], bank[c % 2][:, :], ACT.Sigmoid, scale=PROJ).then_inc(fgate_done, 1)
                    act.wait_ge(i_ready, J + c + 1)
                    nc.scalar.activation(sig_i[:, s], bank[2 + c % 2][:, :], ACT.Sigmoid, scale=PROJ).then_inc(sig_if, 1)

                def sig_state(c):
                    s = slice((c % 2) * L, (c % 2 + 1) * L)
                    act.wait_ge(scanned, J + c + 1)
                    nc.scalar.activation(sig_o[:, s], state[:, s], ACT.Sigmoid).then_inc(sigo_done, 1)

                def square_g(c):
                    act.wait_ge(g_ready, J + c + 1)
                    nc.scalar.activation(g_sq[:, c * L:(c + 1) * L], bank[4 + c % 2][:, :], ACT.Square, scale=PROJ).then_inc(gsq_done, 1)

                def hi_u(c):
                    s = slice((c % 2) * L, (c % 2 + 1) * L)
                    act.wait_ge(u_done, J + c + 1)
                    nc.scalar.activation(u_h[:, c * L:(c + 1) * L], u[:, s], ACT.Copy).then_inc(u_hi, 1)

                for c in range(NC):
                    ln, ln_b = None, None
                    if c == 1 and not first:
                        ln, ln_b = second_ln(b - 1), b - 1
                    if c == 3 and not last:
                        ln, ln_b = first_ln(b + 1), b + 1
                    gates(c)
                    if ln is not None:
                        ln_out(ln, ln_b, (0,))
                    if c:
                        sig_state(c - 1)
                    square_g(c)
                    if c:
                        hi_u(c - 1)
                    if first and c < 3:
                        for k in ((2, 3), (4,), (5,))[c]:
                            split_hi(k, k * CH_BIG, min(CH_BIG, U_HGRN - k * CH_BIG))
                    if ln is not None:
                        ln_out(ln, ln_b, (1,))
                    if c == 1 and not last:
                        ln_hi_part(first_ln(b + 1), b + 1)
                sig_state(3)
                hi_u(3)
                split_hi(b + HGRN_CHUNKS, SLOT1 + b * CH_BIG, CH_BIG)
                ln_hi_part(second_ln(b), b)

            def ffn_step(it, ln, norm, finish=True):
                b, J = it % B, NC * it

                def silu(j):
                    act.wait_ge(gate_ready, J + j + 1)
                    nc.scalar.activation(silu_g[:, (j % 2) * L:(j % 2 + 1) * L], bank[j % 2][:, :], ACT.Silu, scale=PROJ).then_inc(silu_done, 1)

                def hi(j):
                    act.wait_ge(gated_done, J + j + 1)
                    nc.scalar.activation(gated_h[:, j * L:(j + 1) * L], gated[:, j * L:(j + 1) * L], ACT.Copy).then_inc(gated_hi, 1)

                silu(0)
                n = CH_ATT if norm else CH_BIG
                split_hi(it + HGRN_CHUNKS + 4, slot(it // B) + b * n, n)
                for j in range(1, NC):
                    silu(j)
                    hi(j - 1)
                if ln is not None:
                    ln_out(ln, (b + 3) % B, (0,))
                hi(3)
                if ln is not None:
                    ln_out(ln, (b + 3) % B, (1,))
                if norm and finish:
                    ln_hi_part(it - (NQ - 1) * B + N_ATT, b)

            def rope_hi(T, half, dst):
                act.wait_ge(rp_sum, T + 1)
                nc.scalar.activation(dst, r_cos[:, half * L:(half + 1) * L], ACT.Copy).then_inc(rp_hi, 1)

            def exps(G, h):
                e = (h % 2) * NP
                o = (h % 2) * NT
                n_done = 0
                for bk, parts in S_TILES:
                    n_done += len(parts)
                    for qb, at in parts:
                        n = (qb + 1) * P
                        act.wait_ge(s_neg, 4 * G + n_done)
                        nc.scalar.activation(p_e[:, e + Q_OFF[qb]:e + Q_OFF[qb] + n], bank[bk][:, at:at + n], ACT.Exp,
                                             scale=-1.0, bias=sneg[:, o + qb:o + qb + 1],
                                             accum_out=ssum[:, o + qb:o + qb + 1]).then_inc(s_exp, 1)

            def probs_hi(G, h):
                act.wait_ge(s_inv, G + 1)
                e = (h % 2) * NP
                for qb in reversed(range(NT)):
                    s = slice(e + Q_OFF[qb], e + Q_OFF[qb] + (qb + 1) * P)
                    nc.scalar.activation(p_h[:, s], p_e[:, s], ACT.Copy, scale=sinv[:, (h % 2) * NT + qb:(h % 2) * NT + qb + 1]).then_inc(p_hi, 1)

            def pT_copy(G):
                for i in (0, 1):
                    bk, kbs = PT_TILES[i]
                    o, n = PT_OFF[kbs[0]], sum(2 * (NT - kb) * P for kb in kbs)
                    act.wait_ge(pT_ready, 3 * G + i + 1)
                    nc.scalar.activation(pT[:, o:o + n], bank16[bk][:, 0:n], ACT.Copy).then_inc(pT_act, 1)

            def ao_part(G, h, it):
                act.wait_ge(pv_ready, G + 1)
                if h == 1:
                    act.wait_ge(out_ready, X_ATT + NT * it)
                nc.scalar.activation(cols(ao_h, ao_at(it, h), L), bank[5][:, :], ACT.Copy, scale=S_A / (S_P * S_Q)).then_inc(ao_hi, 1)

            def att_step(it, ln, ln_b, norm, prev=True, following=True):
                b, G, T = it % B, GH * it, 5 * it + 3
                exps(G, 0)
                if prev:
                    pT_copy(G - 1)
                rope_hi(T, 0, q_h[:, 2 * L:3 * L])
                probs_hi(G, 0)
                act.wait_ge(v_ready, it + 1)
                nc.scalar.activation(cols(v_h, (it % 2) * L, L), bank[1][:, :], ACT.Copy, scale=S_Q * PROJ).then_inc(v_hi, 1)
                if prev:
                    ao_part(G - 1, 3, it - 1)
                exps(G + 1, 1)
                pT_copy(G)
                rope_hi(T + 1, 1, q_h[:, 3 * L:4 * L])
                probs_hi(G + 1, 1)
                ao_part(G, 0, it)
                split_hi(it + FIRST_ATT_CHUNK + 4, slot(it // B) + b * CH_ATT, CH_ATT)
                if ln is not None:
                    ln_hi_part(ln, ln_b, (0, 1))
                exps(G + 2, 2)
                pT_copy(G + 1)
                probs_hi(G + 2, 2)
                if following:
                    rope_hi(T + 2, 0, q_h[:, 0:L])
                ao_part(G + 1, 1, it)
                if ln is not None:
                    ln_out(ln, ln_b, (0,))
                    ln_hi_part(ln, ln_b, (2, 3))
                exps(G + 3, 3)
                pT_copy(G + 2)
                if following:
                    rope_hi(T + 3, 1, k_h[:, :])
                probs_hi(G + 3, 3)
                ao_part(G + 2, 2, it)
                if ln is not None:
                    ln_out(ln, ln_b, (1,))
                if following:
                    rope_hi(T + 4, 0, q_h[:, L:2 * L])

            def att_begin():
                rope_hi(0, 0, q_h[:, 0:L])
                rope_hi(1, 1, k_h[:, :])
                rope_hi(2, 0, q_h[:, L:2 * L])

            def att_end(ln, norm):
                it = NKV * B
                G = GH * it
                pT_copy(G - 1)
                ln_hi_part(ln, 2)
                ao_part(G - 1, 3, it - 1)
                ln_out(ln, 2, (0,))
                mix_gates(0)
                ln_out(ln, 2, (1,))

            def mix_gates(b):
                act.wait_ge(gate_step, 12 * b + 3)
                nc.scalar.activation(lexp[:, :], lshift[:, :], ACT.Exp).then_inc(lexp_done, 1)

            def mix_step(b, ln):
                act.wait_ge(gT_ready, b + 1)
                nc.scalar.activation(gT[:, :], bank[6][:, :], ACT.Copy).then_inc(gT_out, 1)
                act.wait_ge(xa_done, b + 1)
                nc.scalar.activation(xa_h[:, :], xa[:, :], ACT.Copy).then_inc(xa_hi, 1)
                if ln is not None:
                    ln_hi_part(ln, 3)
                if not (isinstance(b, int) and b == B - 1):
                    mix_gates(b + 1)
                if ln is not None:
                    ln_out(ln, 3)

            split_hi(0, 0, CH_BIG)
            ln_hi_part(0, 0)
            ln_out(0, 0)
            split_hi(1, CH_BIG, CH_BIG)
            hgrn_step(0)
            with act.Fori(1, B - 1) as b:
                hgrn_step(b)
            hgrn_step(B - 1)
            ffn_step(0, second_ln(B - 1), False)
            with act.Fori(1, (NQ - 1) * B) as it:
                ffn_step(it, None, False)
            ffn_step((NQ - 1) * B, None, True)
            with act.Fori(NQ * B - 3, NQ * B - 1) as it:
                ffn_step(it, it - (NQ * B - 3) + N_ATT, True)
            ffn_step(NQ * B - 1, N_ATT + 2, True, finish=False)
            att_begin()
            att_step(0, None, None, None, prev=False)
            att_step(1, N_ATT + B - 1, B - 1, None)
            with act.Fori(2, NKV * B - 3) as it:
                att_step(it, None, None, None)
            att_step(NKV * B - 3, None, None, N_MIX)
            att_step(NKV * B - 2, N_MIX, 0, N_MIX + 1)
            att_step(NKV * B - 1, N_MIX + 1, 1, N_MIX + 2, following=False)
            att_end(N_MIX + 2, N_MIX + 3)
            mix_step(0, N_MIX + 3)
            with act.Fori(1, B - 1) as b:
                mix_step(b, None)
            mix_step(B - 1, None)

        @block.vector
        def _(dve):
            def split_lo(k, dst, n):
                dve.wait_ge(w_hi, k + 1)
                nc.vector.scalar_tensor_tensor(out=cols(w_l, dst, n), in0=cols(stage, (k % 2) * CH_BIG, n), scalar=S_W,
                                               in1=cols(w_h, dst, n), op0=ALU.mult, op1=ALU.subtract).then_inc(w_lo, 1)

            def wait_alone(sem, count, column):
                dve.wait_ge(sem, count)
                nc.vector.memset(pause[:, column:column + 1], 0.0)

            def ln_stat_block(n, b, t):
                nc.vector.bn_stats(stats[:, 6 * t:6 * t + 6], cols(x, (b * NT + t) * D, D)).then_inc(ln_stat, 1)

            def ln_moments(n):
                wait_alone(ln_stat, 8 * n + NT, 1)
                for t in range(NT):
                    nc.vector.bn_aggr(moments[:, 2 * t:2 * t + 2], stats[:, 6 * t:6 * t + 6]).then_inc(ln_stat, 1)
                dve.wait_ge(ln_stat, 8 * n + 2 * NT)
                nc.vector.tensor_scalar(var[:, :], moments[:, :].rearrange("p (t s) -> p t s", s=2)[:, :, 1], EPS, S_Y ** -2,
                                        ALU.add, ALU.mult).then_inc(ln_var, 1)

            def ln_lo_part(n, b, blocks=range(NT)):
                if 0 in blocks:
                    dve.wait_ge(ln_rstd, n + 1)
                    nc.vector.scalar_tensor_tensor(out=shift[:, :], in0=moments[:, :].rearrange("p (t s) -> p t s", s=2)[:, :, 0],
                                                   scalar=-1.0, in1=rstd[:, :], op0=ALU.mult, op1=ALU.mult).then_inc(ln_shift, 1)
                else:
                    dve.wait_ge(ln_lo, NT * n + 2)

                def full(t):
                    nc.vector.tensor_scalar(y_full[:, (t % 2) * D:(t % 2 + 1) * D], cols(x, (b * NT + t) * D, D),
                                            moments[:, 2 * t:2 * t + 1], rstd[:, t:t + 1], ALU.subtract, ALU.mult).then_inc(ln_full, 1)

                def lo(t):
                    dve.wait_ge(ln_full, NT * n + t + 1)
                    dve.wait_ge(ln_hi, NT * n + t + 1)
                    nc.vector.tensor_tensor(y_l[:, t * D:(t + 1) * D], y_full[:, (t % 2) * D:(t % 2 + 1) * D],
                                            y_h[:, t * D:(t + 1) * D], ALU.subtract).then_inc(ln_lo, 1)

                full(blocks[0])
                full(blocks[1])
                for t in blocks:
                    lo(t)
                    if t + 2 in blocks:
                        dve.wait_ge(ln_lo, NT * n + t + 1)
                        full(t + 2)

            def ln_out(n, b, rounds=(0, 1)):
                for r in rounds:
                    dve.wait_ge(ln_T, 4 * n + 2 * r + 1)
                    nc.vector.tensor_copy(cols(yT_h, b * (NC * L), NC * L).rearrange("p (c n) -> p c n", c=NC)[:, :, 2 * r * P:2 * (r + 1) * P],
                                          bank16[6].rearrange("p (c n) -> p c n", c=NC)).then_inc(ln_outh, 1)

            def ln_stats(n, b):
                for t in range(NT):
                    ln_stat_block(n, b, t)
                ln_moments(n)

            def update_block(X, b, t, banks, scale, n=None):
                dve.wait_ge(out_ready, X + t + 1)
                if n is not None and t:
                    dve.wait_ge(x_new, X + t)
                xb = cols(x, (b * NT + t) * D, D)
                nc.vector.scalar_tensor_tensor(out=xb, in0=bank[banks[t]][:, :], scalar=scale, in1=xb,
                                               op0=ALU.mult, op1=ALU.add).then_inc(x_new, 1)
                if n is not None and t:
                    ln_stat_block(n, b, t - 1)

            def update_end(X, b, n):
                wait_alone(x_new, X + NT, 0)
                ln_stat_block(n, b, NT - 1)
                ln_moments(n)

            def update_x(X, b, banks, scale, n=None, finish=True):
                for t in range(NT):
                    update_block(X, b, t, banks, scale(t), n)
                if n is not None and finish:
                    update_end(X, b, n)

            def hgrn_step(b):
                J = NC * b
                first, last = (isinstance(b, int) and b == n for n in (0, B - 1))

                def scan(c):
                    s = slice((c % 2) * L, (c % 2 + 1) * L)
                    dve.wait_ge(inj_mix, J + c + 1)
                    nc.vector.scalar_tensor_tensor(out=inject[:, s], in0=bank[2 + c % 2][:, :], scalar=PROJ, in1=sig_i[:, s],
                                                   op0=ALU.mult, op1=ALU.mult).then_inc(injected, 1)
                    dve.wait_ge(injected, J + c + 1)
                    dve.wait_ge(fgate_done, J + c + 1)
                    nc.vector.tensor_tensor_scan(state[:, s], fgate[:, c * L:(c + 1) * L], inject[:, s], 0.0,
                                                 ALU.mult, ALU.add).then_inc(scanned, 1)

                def make_u(c):
                    s = slice((c % 2) * L, (c % 2 + 1) * L)
                    dve.wait_ge(sigo_done, J + c + 1)
                    nc.vector.tensor_tensor(sig_o[:, s], sig_o[:, s], state[:, s], ALU.mult).then_inc(silu_o, 1)
                    dve.wait_ge(silu_o, J + c + 1)
                    dve.wait_ge(gsq_done, J + c + 1)
                    nc.vector.scalar_tensor_tensor(out=u[:, s], in0=bank[4 + c % 2][:, :], scalar=gnw_s[:, c:c + 1], in1=sig_o[:, s],
                                                   op0=ALU.mult, op1=ALU.mult).then_inc(u_done, 1)

                def lo_u(c):
                    s = slice((c % 2) * L, (c % 2 + 1) * L)
                    dve.wait_ge(u_hi, J + c + 1)
                    nc.vector.tensor_tensor(u_l[:, c * L:(c + 1) * L], u[:, s], u_h[:, c * L:(c + 1) * L], ALU.subtract).then_inc(u_lo, 1)

                for c in range(NC):
                    ln, ln_b = None, None
                    if c == 1 and not first:
                        ln, ln_b = second_ln(b - 1), b - 1
                    if c == 3 and not last:
                        ln, ln_b = first_ln(b + 1), b + 1
                    if ln is not None:
                        ln_out(ln, ln_b, (0,))
                    if c == 1 and not last:
                        if first:
                            dve.wait_ge(x_loaded[1], 16)
                        ln_stats(first_ln(b + 1), b + 1)
                    scan(c)
                    if c:
                        make_u(c - 1)
                    if first and c < 3:
                        for k in ((2, 3), (4,), (5,))[c]:
                            split_lo(k, k * CH_BIG, min(CH_BIG, U_HGRN - k * CH_BIG))
                    if c:
                        lo_u(c - 1)
                    if ln is not None:
                        ln_out(ln, ln_b, (1,))
                    if c == 1 and not last:
                        ln_lo_part(first_ln(b + 1), b + 1)
                make_u(3)
                lo_u(3)
                dve.wait_ge(ms_ready, b + 1)
                back_scale = (S_U * S_W) ** 2
                nc.vector.tensor_scalar(ms[:, :], bank[4][:, 0:NT], back_scale / D, EPS * back_scale, ALU.mult, ALU.add).then_inc(ms_out, 1)
                split_lo(b + HGRN_CHUNKS, SLOT1 + b * CH_BIG, CH_BIG)
                dve.wait_ge(rms_done, b + 1)
                update_x(NT * b, b, HGRN_BANKS, lambda t: rms[:, t:t + 1], second_ln(b))
                ln_lo_part(second_ln(b), b)

            def ffn_step(it, ln, norm, finish=True):
                b, J = it % B, NC * it

                def gate(j):
                    s = slice((j % 2) * L, (j % 2 + 1) * L)
                    dve.wait_ge(silu_done, J + j + 1)
                    dve.wait_ge(up_ready, J + j + 1)
                    nc.vector.scalar_tensor_tensor(out=gated[:, j * L:(j + 1) * L], in0=bank[2 + j % 2][:, :], scalar=PROJ * S_G, in1=silu_g[:, s],
                                                   op0=ALU.mult, op1=ALU.mult).then_inc(gated_done, 1)

                def lo(j):
                    dve.wait_ge(gated_hi, J + j + 1)
                    nc.vector.tensor_tensor(gated_l[:, j * L:(j + 1) * L], gated[:, j * L:(j + 1) * L],
                                            gated_h[:, j * L:(j + 1) * L], ALU.subtract).then_inc(gated_lo, 1)

                gate(0)
                n = CH_ATT if norm else CH_BIG
                split_lo(it + HGRN_CHUNKS + 4, slot(it // B) + b * n, n)
                for j in range(1, NC):
                    gate(j)
                    lo(j - 1)
                if ln is not None:
                    ln_out(ln, (b + 3) % B, (0,))
                lo(3)
                if ln is not None:
                    ln_out(ln, (b + 3) % B, (1,))
                n = it - (NQ - 1) * B + N_ATT if norm else None
                update_x(X_FFN + NT * it, b, FFN_BANKS, lambda t: 1.0 / (S_G * S_W), n, finish)
                if norm and finish:
                    ln_lo_part(n, b)

            def rotate(T, half, bk):
                s = slice(half * L, (half + 1) * L)
                h = HD // 2
                dve.wait_ge(rp_ready, T + 1)
                need(dve, rp_lo, T - 1)
                nc.vector.tensor_tensor(r_cos[:, s], bank[bk][:, :], rope_c[:, :], ALU.mult)
                nc.vector.tensor_tensor(r_sin[0:h, s], bank[bk][h:HD, :], rope_s[0:h, :], ALU.mult)
                nc.vector.tensor_tensor(r_sin[h:HD, s], bank[bk][0:h, :], rope_s[h:HD, :], ALU.mult).then_inc(rp_read, 1)

            def maxima(G, h):
                o = (h % 2) * NT
                for i, (bk, parts) in enumerate(S_TILES):
                    dve.wait_ge(s_ready, 3 * G + i + 1)
                    for qb, at in parts:
                        s = bank[bk][:, at:at + (qb + 1) * P]
                        nc.vector.tensor_scalar(s, s, -SCORE, None, ALU.mult, ALU.min, accum_out=sneg[:, o + qb:o + qb + 1]).then_inc(s_neg, 1)

            def recip(G, h):
                o = (h % 2) * NT
                dve.wait_ge(s_exp, 4 * G + 4)
                nc.vector.tensor_scalar(ssum[:, o:o + NT], ssum[:, o:o + NT], 1.0 / S_P, None, ALU.mult).then_inc(s_scaled, 1)
                dve.wait_ge(s_scaled, G + 1)
                nc.vector.reciprocal(sinv[:, o:o + NT], ssum[:, o:o + NT]).then_inc(s_inv, 1)

            def probs_lo(G, h):
                e = (h % 2) * NP
                dve.wait_ge(s_inv, G + 1)
                for qb in reversed(range(NT)):
                    s = slice(e + Q_OFF[qb], e + Q_OFF[qb] + (qb + 1) * P)
                    dve.wait_ge(p_hi, 4 * G + NT - qb)
                    nc.vector.scalar_tensor_tensor(out=p_l[:, s], in0=p_e[:, s], scalar=sinv[:, (h % 2) * NT + qb:(h % 2) * NT + qb + 1],
                                                   in1=p_h[:, s], op0=ALU.mult, op1=ALU.subtract).then_inc(p_lo, 1)

            def pT_copy(G):
                bk, kbs = PT_TILES[2]
                o, n = PT_OFF[kbs[0]], sum(2 * (NT - kb) * P for kb in kbs)
                dve.wait_ge(pT_ready, 3 * G + 3)
                nc.vector.tensor_copy(pT[:, o:o + n], bank16[bk][:, 0:n]).then_inc(pT_vec, 1)

            def ao_part(G, h, it):
                o = ao_at(it, h)
                dve.wait_ge(ao_hi, G + 1)
                nc.vector.scalar_tensor_tensor(out=cols(ao_l, o, L), in0=bank[5][:, :], scalar=S_A / (S_P * S_Q), in1=cols(ao_h, o, L),
                                               op0=ALU.mult, op1=ALU.subtract).then_inc(ao_lo, 1)

            ATT_BACK = 1.0 / (S_A * S_W)

            def att_step(it, ln, ln_b, norm, prev=True, following=True):
                b, G, T = it % B, GH * it, 5 * it + 3
                X = X_ATT + NT * (it - 1)
                last_b = (b + 3) % B
                maxima(G, 0)
                if prev:
                    pT_copy(G - 1)
                need(dve, rp_lo, T)
                rotate(T, 0, 0)
                recip(G, 0)
                probs_lo(G, 0)
                dve.wait_ge(v_hi, it + 1)
                nc.vector.scalar_tensor_tensor(out=cols(v_l, (it % 2) * L, L), in0=bank[1][:, :], scalar=S_Q * PROJ,
                                               in1=cols(v_h, (it % 2) * L, L), op0=ALU.mult, op1=ALU.subtract).then_inc(v_lo, 1)
                if prev:
                    ao_part(G - 1, 3, it - 1)
                maxima(G + 1, 1)
                rotate(T + 1, 1, 0)
                pT_copy(G)
                recip(G + 1, 1)
                probs_lo(G + 1, 1)
                if prev:
                    update_block(X, last_b, 0, ATT_BANKS, ATT_BACK, norm)
                ao_part(G, 0, it)
                split_lo(it + FIRST_ATT_CHUNK + 4, slot(it // B) + b * CH_ATT, CH_ATT)
                if prev:
                    update_block(X, last_b, 1, ATT_BANKS, ATT_BACK, norm)
                if ln is not None:
                    ln_lo_part(ln, ln_b, (0, 1))
                maxima(G + 2, 2)
                if prev:
                    update_block(X, last_b, 2, ATT_BANKS, ATT_BACK, norm)
                pT_copy(G + 1)
                recip(G + 2, 2)
                probs_lo(G + 2, 2)
                if following:
                    rotate(T + 2, 0, 0)
                ao_part(G + 1, 1, it)
                if ln is not None:
                    ln_out(ln, ln_b, (0,))
                    ln_lo_part(ln, ln_b, (2, 3))
                if prev:
                    update_block(X, last_b, 3, ATT_BANKS, ATT_BACK, norm)
                maxima(G + 3, 3)
                if following:
                    rotate(T + 3, 1, 0)
                pT_copy(G + 2)
                recip(G + 3, 3)
                if norm is not None:
                    update_end(X, last_b, norm)
                probs_lo(G + 3, 3)
                ao_part(G + 2, 2, it)
                if ln is not None:
                    ln_out(ln, ln_b, (1,))
                if following:
                    rotate(T + 4, 0, 1)

            def att_begin():
                rotate(0, 0, 2)
                rotate(1, 1, 3)
                update_end(X_ATT - NT, B - 1, N_ATT + B - 1)
                rotate(2, 0, 1)

            def att_end(ln, norm):
                it = NKV * B
                G = GH * it
                pT_copy(G - 1)
                ln_lo_part(ln, 2)
                ao_part(G - 1, 3, it - 1)
                ln_out(ln, 2, (0,))
                dve.wait_ge(rp_lo, 5 * it)
                mix_gates(0)
                ln_out(ln, 2, (1,))
                update_x(X_MIX - NT, 3, END_BANKS, lambda t: ATT_BACK, norm)

            def mix_gates(b):
                g0 = 12 * b
                count = [0]

                def step(ins):
                    ins.then_inc(gate_step, 1)
                    count[0] += 1
                    dve.wait_ge(gate_step, g0 + count[0])

                l3 = logit[:, :].rearrange("p (t e) -> p t e", e=E)
                li = l3[:, :, :, None].to_broadcast([P, NT, E, E])
                lj = l3[:, :, None, :].to_broadcast([P, NT, E, E])
                four = lambda a: a[:, :].rearrange("p (t i j) -> p t i j", i=E, j=E)
                three = lambda a: a[:, :].rearrange("p (t e) -> p t e", e=E)
                dve.wait_ge(lg_ready, b + 1)
                step(nc.vector.scalar_tensor_tensor(out=l3, in0=bank[2][:, 0:NT * E].rearrange("p (t e) -> p t e", e=E), scalar=PROJ,
                                                    in1=gate_b[:, None, :].to_broadcast([P, NT, E]), op0=ALU.mult, op1=ALU.add))
                step(nc.vector.reduce_max(top[:, :], l3, AX.X))
                step(nc.vector.tensor_tensor(three(lshift), l3, top[:, :, None].to_broadcast([P, NT, E]), ALU.subtract))
                step(nc.vector.tensor_tensor(four(above), lj, li, ALU.is_gt))
                step(nc.vector.tensor_tensor(four(equal), lj, li, ALU.is_equal))
                step(nc.vector.tensor_tensor(equal[:, :].rearrange("p (t m) -> p t m", t=NT), equal[:, :].rearrange("p (t m) -> p t m", t=NT),
                                             tri[:, None, :].to_broadcast([P, NT, E * E]), ALU.mult))
                step(nc.vector.tensor_tensor(above[:, :], above[:, :], equal[:, :], ALU.add))
                step(nc.vector.reduce_sum(three(rank), four(above), AX.X))
                dve.wait_ge(lexp_done, b + 1)
                step(nc.vector.scalar_tensor_tensor(out=picked[:, :], in0=rank[:, :], scalar=2.0, in1=lexp[:, :], op0=ALU.is_lt, op1=ALU.mult))
                step(nc.vector.reduce_sum(psum_[:, :], three(picked), AX.X))
                nc.vector.reciprocal(top[:, :], psum_[:, :]).then_inc(gate_rcp, 1)
                dve.wait_ge(gate_rcp, b + 1)
                nc.vector.scalar_tensor_tensor(out=three(gates), in0=three(picked), scalar=S_P, in1=top[:, :, None].to_broadcast([P, NT, E]),
                                               op0=ALU.mult, op1=ALU.mult).then_inc(gate_val, 1)
                dve.wait_ge(gate_val, b + 1)
                spread = gates[:, :, None].to_broadcast([P, NT * E, R])
                step(nc.vector.tensor_copy(g_h[:, :].rearrange("p (e r) -> p e r", r=R), spread))
                step(nc.vector.tensor_tensor(g_l[:, :].rearrange("p (e r) -> p e r", r=R), spread,
                                             g_h[:, :].rearrange("p (e r) -> p e r", r=R), ALU.subtract))

            def mix_step(b, ln):
                dve.wait_ge(gT_out, b + 1)
                dve.wait_ge(xa_ready, b + 1)
                nc.vector.scalar_tensor_tensor(out=xa[:, :], in0=bank[4][:, :], scalar=PROJ * S_X / S_P, in1=gT[:, :],
                                               op0=ALU.mult, op1=ALU.mult).then_inc(xa_done, 1)
                dve.wait_ge(xa_done, b + 1)
                dve.wait_ge(xa_hi, b + 1)
                nc.vector.tensor_tensor(xa_l[:, :], xa[:, :], xa_h[:, :], ALU.subtract).then_inc(xa_lo, 1)
                if ln is not None:
                    ln_lo_part(ln, 3)
                if not (isinstance(b, int) and b == B - 1):
                    mix_gates(b + 1)
                if ln is not None:
                    ln_out(ln, 3)
                for t in range(NT):
                    dve.wait_ge(out_ready, X_MIX + NT * b + t + 1)
                    dve.wait_ge(biased, NT * b + t + 1)
                    xb = cols(x, (b * NT + t) * D, D)
                    nc.vector.scalar_tensor_tensor(out=xb, in0=bank[MIX_BANKS[t]][:, :], scalar=PROJ, in1=xb,
                                                   op0=ALU.mult, op1=ALU.add).then_inc(x_new, 1)

            for t in range(NT):
                dve.wait_ge(x_first[t], 16)
                ln_stat_block(0, 0, t)
            ln_moments(0)
            ln_lo_part(0, 0)
            ln_out(0, 0, (0,))
            split_lo(0, 0, CH_BIG)
            ln_out(0, 0, (1,))
            split_lo(1, CH_BIG, CH_BIG)
            dve.wait_ge(const_in, 16 * 2)
            nc.vector.tensor_scalar(gnw_s[:, :], gnw[:, :], PROJ * S_U, None, ALU.mult).then_inc(gnw_ready, 1)
            dve.wait_ge(gnw_ready, 1)
            hgrn_step(0)
            dve.wait_ge(x_loaded[2], 16)
            dve.wait_ge(x_loaded[3], 16)
            with dve.Fori(1, B - 1) as b:
                hgrn_step(b)
            hgrn_step(B - 1)
            ffn_step(0, second_ln(B - 1), False)
            with dve.Fori(1, (NQ - 1) * B) as it:
                ffn_step(it, None, False)
            ffn_step((NQ - 1) * B, None, True)
            with dve.Fori(NQ * B - 3, NQ * B - 1) as it:
                ffn_step(it, it - (NQ * B - 3) + N_ATT, True)
            ffn_step(NQ * B - 1, N_ATT + 2, True, finish=False)
            dve.wait_ge(table_in, 16 * 5)
            att_begin()
            att_step(0, None, None, None, prev=False)
            att_step(1, N_ATT + B - 1, B - 1, None)
            with dve.Fori(2, NKV * B - 3) as it:
                att_step(it, None, None, None)
            att_step(NKV * B - 3, None, None, N_MIX)
            att_step(NKV * B - 2, N_MIX, 0, N_MIX + 1)
            att_step(NKV * B - 1, N_MIX + 1, 1, N_MIX + 2, following=False)
            att_end(N_MIX + 2, N_MIX + 3)
            mix_step(0, N_MIX + 3)
            with dve.Fori(1, B - 1) as b:
                mix_step(b, None)
            mix_step(B - 1, None)

        @block.gpsimd
        def _(pool):
            def power(n):
                pool.wait_ge(ln_var, n + 1)
                nc.gpsimd.tensor_tensor(rstd[:, :], var[:, :], minus_half[:, :], ALU.pow).then_inc(ln_rstd, 1)

            def hgrn_step(b):
                J = NC * b

                def mix(c):
                    s = slice((c % 2) * L, (c % 2 + 1) * L)
                    pool.wait_ge(sig_if, J + c + 1)
                    nc.gpsimd.tensor_tensor(sig_i[:, s], sig_i[:, s], sig_nf[:, s], ALU.mult).then_inc(inj_mix, 1)

                def add_square(c):
                    pool.wait_ge(gsq_done, J + c + 1)
                    need(pool, gsum, 3 * b + c - 1)
                    nc.gpsimd.tensor_tensor(g_sq[:, 0:L], g_sq[:, 0:L], g_sq[:, c * L:(c + 1) * L], ALU.add).then_inc(gsum, 1)

                for c in range(NC):
                    mix(c)
                    if c:
                        add_square(c)
                    if c == 1 and not (isinstance(b, int) and b == B - 1):
                        power(first_ln(b + 1))
                pool.wait_ge(ms_out, b + 1)
                nc.gpsimd.tensor_tensor(rms[:, :], ms[:, :], minus_half[:, :], ALU.pow).then_inc(rms_done, 1)
                power(second_ln(b))

            def rope_add(T, half, hi, lo):
                s = slice(half * L, (half + 1) * L)
                pool.wait_ge(rp_read, T + 1)
                nc.gpsimd.tensor_tensor(r_cos[:, s], r_cos[:, s], r_sin[:, s], ALU.add).then_inc(rp_sum, 1)
                pool.wait_ge(rp_sum, T + 1)
                pool.wait_ge(rp_hi, T + 1)
                nc.gpsimd.tensor_tensor(lo, r_cos[:, s], hi, ALU.subtract).then_inc(rp_lo, 1)

            def query(T, half, h):
                rope_add(T, half, q_h[:, h * L:(h + 1) * L], q_l[:, h * L:(h + 1) * L])

            def att_step(it, norm, following=True):
                T = 5 * it + 3
                query(T, 0, 2)
                query(T + 1, 1, 3)
                if following:
                    query(T + 2, 0, 0)
                if following:
                    rope_add(T + 3, 1, k_h[:, :], k_l[:, :])
                if norm is not None:
                    power(norm)
                if following:
                    query(T + 4, 0, 1)

            def mix_step(b):
                pool.wait_ge(ln_lo, NT * (N_MIX + b) + NT)
                for t in range(NT):
                    xb = cols(x, (b * NT + t) * D, D)
                    nc.gpsimd.tensor_tensor(xb, xb, bias[:, :], ALU.add).then_inc(biased, 1)

            nc.gpsimd.memset(minus_half[:, :], -0.5).then_inc(memset_done, 1)
            nc.gpsimd.memset(ones[:, :], 1.0).then_inc(memset_done, 1)
            pool.wait_ge(memset_done, 2)
            power(0)
            hgrn_step(0)
            with pool.Fori(1, B - 1) as b:
                hgrn_step(b)
            hgrn_step(B - 1)
            with pool.Fori(N_ATT, N_ATT + B - 1) as n:
                power(n)
            query(0, 0, 0)
            rope_add(1, 1, k_h[:, :], k_l[:, :])
            power(N_ATT + B - 1)
            query(2, 0, 1)
            with pool.Fori(0, NKV * B - 3) as it:
                att_step(it, None)
            with pool.Fori(NKV * B - 3, NKV * B - 1) as it:
                att_step(it, it - (NKV * B - 3) + N_MIX)
            att_step(NKV * B - 1, N_MIX + 2, following=False)
            power(N_MIX + 3)
            pool.wait_ge(late_in, 16)
            with pool.Fori(0, B) as b:
                mix_step(b)


SCORE = HD ** -0.5 / (S_Q * S_Q)


def _rows(w_t):
    k, n = w_t.shape
    return w_t.reshape(k // P, P, n).transpose(1, 0, 2).reshape(P, -1)


def _chunks(unit, n, count):
    out = np.zeros((count, P, CH_BIG), np.float32)
    for i in range(count):
        part = unit[:, i * n:(i + 1) * n]
        out[i, :, :part.shape[1]] = part
    return out


def kernel(**inputs):
    import concourse.bacc as bacc
    from concourse.bass_utils import run_bass_kernel_spmd
    a = {k: np.asarray(v) for k, v in inputs.items()}

    unit = [_rows(a[f"L0_attn_{n}"][c * P:(c + 1) * P].T) for c in range(NC) for n in ("Wi", "Wf", "Wg")] + [_rows(a["L0_attn_Wo"].T)]
    packed = [_chunks(np.concatenate(unit, axis=1), CH_BIG, HGRN_CHUNKS)]
    for q in range(NQ):
        s = slice(q * D, (q + 1) * D)
        unit = np.concatenate([_rows(a["L0_ffn_w_gate"][s].T), _rows(a["L0_ffn_w_up"][s].T), _rows(a["L0_ffn_w_down"][:, s].T)], axis=1)
        packed.append(_chunks(unit, CH_BIG, 4))
    wqkv = a["L1_attn_Wqkv"]
    for g in range(NKV):
        q = wqkv[:, g * GH * HD:(g + 1) * GH * HD]
        k = wqkv[:, (NH + g) * HD:(NH + g + 1) * HD]
        v = wqkv[:, (NH + NKV + g) * HD:(NH + NKV + g + 1) * HD]
        wo = a["L1_attn_Wo"][g * GH * HD:(g + 1) * GH * HD]
        packed.append(_chunks(np.concatenate([_rows(q), _rows(np.concatenate([k, v], axis=1)), _rows(wo)], axis=1), CH_ATT, 4))
    unit = np.concatenate([_rows(a["L1_ffn_W"].T), _rows(a["L1_ffn_lora_A"].reshape(E * R, D).T),
                           _rows(a["L1_ffn_lora_B"].transpose(0, 2, 1).reshape(E * R, D)), _rows(a["L1_ffn_gate_w"].T)], axis=1)
    packed.append(_chunks(unit, CH_ATT, 4))

    freqs = (np.float32(1.0) / np.float32(THETA) ** (np.arange(0, HD, 2, dtype=np.float32) / np.float32(HD))).astype(np.float32)
    ang = (freqs[:, None] * np.arange(L, dtype=np.float32)[None, :]).astype(np.float32)
    scale = np.float32(S_Q * PROJ)
    cos, sin = np.cos(ang).astype(np.float32) * scale, np.sin(ang).astype(np.float32) * scale
    rope = np.stack([np.concatenate([cos, cos]), np.concatenate([-sin, sin])])
    lower = np.tril(np.ones((E, E), np.float32), -1).reshape(1, E * E)
    import ml_dtypes
    mask = np.triu(np.full((P, P), MASK_NEG, np.float32), 1).astype(ml_dtypes.bfloat16)
    arrays = {
        "x_in": np.ascontiguousarray(a["L0_attn_hidden_states"]),
        "w_in": np.concatenate(packed),
        "gnw_in": np.ascontiguousarray(a["L0_attn_g_norm_weight"].reshape(NC, P).T),
        "bias_in": np.ascontiguousarray(np.broadcast_to(a["L1_ffn_b"], (P, D))),
        "gate_b_in": np.ascontiguousarray(np.broadcast_to(a["L1_ffn_gate_b"], (P, E))),
        "rope_in": rope,
        "tri_in": np.ascontiguousarray(np.broadcast_to(lower, (P, E * E))),
        "ident_in": np.eye(P, dtype=np.float16),
        "mask_in": mask,
    }
    nc = bacc.Bacc("TRN2", target_bir_lowering=False, num_devices=1)
    args = [nc.dram_tensor(n, v.shape, mybir.dt.from_np(v.dtype), kind="ExternalInput").ap() for n, v in arrays.items()]
    out = nc.dram_tensor("out", [B, L, D], f32, kind="ExternalOutput").ap()
    build(nc, *args, out)
    r = run_bass_kernel_spmd(nc, [arrays], core_ids=[0])
    return r.results[0]["out"]
```
